# Optimizing a Trainium2 kernel written in Bass

```python
import numpy as np
import jax
import jax.numpy as jnp

def _softmax(x, axis=-1):
    return jax.nn.softmax(x, axis=axis)

def _gelu(x):
    return jax.nn.gelu(x, approximate=True)

def _silu(x):
    return jax.nn.silu(x)

def _sigmoid(x):
    return jax.nn.sigmoid(x)

def _layernorm(x, axis=-1, eps=1e-05):
    m = jnp.mean(x, axis=axis, keepdims=True)
    v = jnp.var(x, axis=axis, keepdims=True)
    return (x - m) / jnp.sqrt(v + eps)

def _scatter_add(tgt, idx, src, axis=0):
    return tgt.at[idx].add(src)

def _segment_sum(src, seg, n):
    return jax.ops.segment_sum(src, seg, n)
kernel_name = 'mk_flamingo_gated_d1_seqx_r2_dc914b'

def setup_inputs(seed: int=0):
    np.random.seed(seed)
    _w = jnp.asarray

    def _rec_inputs():
        import jax
        import jax.numpy as jnp
        _rk = jax.random.key(seed)
        x = -0.0002928 + 1 * jax.random.normal(jax.random.fold_in(_rk, 1), (4, 2048, 512), jnp.float32)
        _lenS = 2048 - jax.random.randint(jax.random.fold_in(_rk, 7), (4,), 0, max(1, 2048 // 4) + 1, jnp.int32)
        _lenS2 = 154 - jax.random.randint(jax.random.fold_in(_rk, 8), (4,), 0, max(1, 154 // 4) + 1, jnp.int32)
        _ctx_768P = jax.random.normal(jax.random.fold_in(_rk, 11), (4, 16, 384), jnp.float32)
        _ctx_768c = jax.random.dirichlet(jax.random.fold_in(_rk, 511), 0.3 * jnp.ones((16,), jnp.float32), (4, 154))
        _ctx_768t = jnp.einsum('bsk,bkd->bsd', _ctx_768c, _ctx_768P)
        _ctx_768t = _ctx_768t * jax.lax.rsqrt(jnp.mean(jnp.square(_ctx_768t)) + 1e-12) * 0.953939
        ctx_768 = -0.00055796 + 0.999787 * (_ctx_768t + 0.3 * jax.random.normal(jax.random.fold_in(_rk, 611), (4, 154, 384), jnp.float32))
        _g = jax.random.normal(jax.random.fold_in(_rk, 9001), (2, 1), jnp.float32)
        _g = jnp.sign(_g) * jnp.maximum(jnp.abs(_g), 1.0) + (_g == 0) * 1.0
        g_xattn = _g[0]
        g_ffn = _g[1]
        return (x, ctx_768, g_xattn, g_ffn)
    x, ctx_768, g_xattn, g_ffn = _rec_inputs()

    def _L0_xattn_setup():
        import jax, jax.numpy as jnp
        import numpy as np
        HEADS = 16
        DIM_HEAD = 64
        key = jax.random.key(seed)
        ks = jax.random.split(key, 7)
        b, n, m = (2, 1024, 512)
        query_dim, context_dim = (512, 384)
        inner = HEADS * DIM_HEAD
        s_q = 1.0 / np.sqrt(query_dim)
        s_c = 1.0 / np.sqrt(context_dim)
        s_i = 1.0 / np.sqrt(inner)
        return {'x': jax.random.normal(ks[0], (b, n, query_dim), jnp.float32), 'context': jax.random.normal(ks[1], (b, m, context_dim), jnp.float32), 'Wq': jax.random.normal(ks[2], (query_dim, inner), jnp.float32) * s_q, 'Wk': jax.random.normal(ks[3], (context_dim, inner), jnp.float32) * s_c, 'Wv': jax.random.normal(ks[4], (context_dim, inner), jnp.float32) * s_c, 'Wo': jax.random.normal(ks[5], (inner, query_dim), jnp.float32) * s_i, 'bo': jax.random.normal(ks[6], (query_dim,), jnp.float32) * 0.01}
    _L0_xattn_all = _L0_xattn_setup()
    _L0_xattn_in = {k: v for k, v in _L0_xattn_all.items() if k in ('Wq', 'Wk', 'Wv', 'Wo', 'bo')}
    del _L0_xattn_all

    def _L0_ffn_setup():
        import jax, jax.numpy as jnp
        import numpy as np
        NUM_EXPERTS = 8
        CAPACITY_FACTOR = 1.0
        key = jax.random.key(seed)
        k1, k2, k3, k4 = jax.random.split(key, 4)
        B, S, D, E, F = (8, 1024, 512, NUM_EXPERTS, 2048)
        x = jax.random.normal(k1, (B, S, D), dtype=jnp.float32)
        router_w = jax.random.normal(k2, (D, E), dtype=jnp.float32) * D ** (-0.5)
        w1 = jax.random.normal(k3, (E, D, F), dtype=jnp.float32) * D ** (-0.5)
        w2 = jax.random.normal(k4, (E, F, D), dtype=jnp.float32) * F ** (-0.5)
        return {'x': x, 'router_w': router_w, 'w1': w1, 'w2': w2}
    _L0_ffn_all = _L0_ffn_setup()
    _L0_ffn_in = {k: v for k, v in _L0_ffn_all.items() if k in ('router_w', 'w1', 'w2')}
    del _L0_ffn_all
    return {'x': x, 'ctx_768': ctx_768, 'g_xattn': g_xattn, 'g_ffn': g_ffn, 'L0_xattn_Wq': _L0_xattn_in['Wq'], 'L0_xattn_Wk': _L0_xattn_in['Wk'], 'L0_xattn_Wv': _L0_xattn_in['Wv'], 'L0_xattn_Wo': _L0_xattn_in['Wo'], 'L0_xattn_bo': _L0_xattn_in['bo'], 'L0_ffn_router_w': _L0_ffn_in['router_w'], 'L0_ffn_w1': _L0_ffn_in['w1'], 'L0_ffn_w2': _L0_ffn_in['w2']}

def reference(x, ctx_768, g_xattn, g_ffn, L0_xattn_Wq, L0_xattn_Wk, L0_xattn_Wv, L0_xattn_Wo, L0_xattn_bo, L0_ffn_router_w, L0_ffn_w1, L0_ffn_w2):
    import jax
    import jax.numpy as jnp

    def _L0_xattn_ref(x, context, Wq, Wk, Wv, Wo, bo):
        import jax, jax.numpy as jnp
        import numpy as np
        HEADS = 16
        DIM_HEAD = 64
        b, n, _ = x.shape
        h, d = (HEADS, DIM_HEAD)
        scale = d ** (-0.5)
        q = (x @ Wq).reshape(b, n, h, d).transpose(0, 2, 1, 3)
        k = (context @ Wk).reshape(b, -1, h, d).transpose(0, 2, 1, 3)
        v = (context @ Wv).reshape(b, -1, h, d).transpose(0, 2, 1, 3)
        sim = jnp.einsum('bhid,bhjd->bhij', q, k) * scale
        attn = jax.nn.softmax(sim, axis=-1)
        out = jnp.einsum('bhij,bhjd->bhid', attn, v)
        out = out.transpose(0, 2, 1, 3).reshape(b, n, h * d)
        return out @ Wo + bo

    def _L0_ffn_ref(x, router_w, w1, w2):
        import jax, jax.numpy as jnp
        import numpy as np
        NUM_EXPERTS = 8
        CAPACITY_FACTOR = 1.0
        B, S, D = x.shape
        E = router_w.shape[1]
        T = B * S
        C = int(CAPACITY_FACTOR * T / E)
        x_flat = x.reshape(T, D)
        logits = x_flat @ router_w
        probs = jax.nn.softmax(logits, axis=-1)
        expert_idx = jnp.argmax(probs, axis=-1)
        gate = jnp.take_along_axis(probs, expert_idx[:, None], axis=1)[:, 0]
        onehot = jax.nn.one_hot(expert_idx, E, dtype=jnp.float32)
        pos_all = jnp.cumsum(onehot, axis=0) - 1.0
        pos = jnp.take_along_axis(pos_all, expert_idx[:, None], axis=1)[:, 0]
        pos = pos.astype(jnp.int32)
        keep = (pos < C).astype(x_flat.dtype)
        pos_c = jnp.clip(pos, 0, C - 1)
        expert_in = jnp.zeros((E, C, D), dtype=x_flat.dtype)
        expert_in = expert_in.at[expert_idx, pos_c].add(x_flat * keep[:, None])
        hidden = jax.nn.gelu(jnp.einsum('ecd,edf->ecf', expert_in, w1))
        expert_out = jnp.einsum('ecf,efd->ecd', hidden, w2)
        y = expert_out[expert_idx, pos_c] * (gate * keep)[:, None]
        return y.reshape(B, S, D)
    x = x + jnp.tanh(g_xattn[0]) * _L0_xattn_ref(_layernorm(x, axis=-1), ctx_768, L0_xattn_Wq, L0_xattn_Wk, L0_xattn_Wv, L0_xattn_Wo, L0_xattn_bo)
    x = x + jnp.tanh(g_ffn[0]) * _L0_ffn_ref(_layernorm(x, axis=-1), L0_ffn_router_w, L0_ffn_w1, L0_ffn_w2)
    return x

_drawn_inputs = setup_inputs


def setup_inputs(seed=0):
    import zlib

    import numpy as np

    out = dict(_drawn_inputs(seed))
    spreads = {}
    factors = {'L0_xattn_bo': 2.911}
    for name, (base, spread) in spreads.items():
        noise = np.random.default_rng([zlib.crc32(name.encode()), seed]).standard_normal(out[name].shape)
        drawn = base * np.exp(spread * noise) if base else spread * noise
        out[name] = jnp.asarray(drawn.astype(out[name].dtype))
    for name, factor in factors.items():
        out[name] = (out[name] * factor).astype(out[name].dtype)
    return out
```

```python
from contextlib import ExitStack

import concourse.bass as bass
from concourse import mybir

F32 = mybir.dt.float32
F32R = mybir.dt.float32r
BF16 = mybir.dt.bfloat16
U32 = mybir.dt.uint32
ALU = mybir.AluOpType
ACT = mybir.ActivationFunctionType
AX = mybir.AxisListType

P = 128
HEADS = 16
DH = 64
TILES = 4
GN = TILES * P
QUADS = HEADS // 4
HP = 160
EPS = 1e-5

HI, LO = 0, 1
PASSES = ((LO, HI), (HI, LO), (HI, HI))


def split_matmul(pe, out, stationary, moving, first, last):
    for n, (s, m) in enumerate(PASSES):
        ins = pe.matmul(out, stationary(s), moving(m), start=first and n == 0,
                        stop=last and n == len(PASSES) - 1)
    return ins


def alone(engine, waits_met):
    engine.sem_inc(waits_met, 1)


def flamingo_block(nc, x, ctx_in, g_xattn, g_ffn, Wq, Wk, Wv, Wo, bo, router_w, w1, w2, out):
    B, N, D = x.shape
    _, M, DC = ctx_in.shape
    INNER = Wq.shape[1]
    E, _, F = w1.shape
    T = B * N
    CAP = T // E
    NG = T // GN
    GPB = NG // B
    KC, CC, IC = D // P, DC // P, INNER // P
    REM = M - P
    assert INNER == HEADS * DH and P < M <= P + 32 and CAP % GN == 0 and GPB == 4 and E == 8
    ROWS = B * M
    RT = ROWS // P
    RL = ROWS - RT * P
    PAIR = 2 * M
    KQ = 2 * PAIR
    VP = 3 * DH
    VQ = 2 * VP + 2 * P
    SCALE = float(DH) ** -0.5

    x_rows = x.rearrange("b n d -> (b n) d")
    out_rows = out.rearrange("b n d -> (b n) d")
    x_tiles = x_rows.rearrange("(t p) d -> p t d", p=P)
    out_tiles = out_rows.rearrange("(t p) d -> p t d", p=P)

    keys_dram = nc.dram_tensor("keys_dram", (B, QUADS, P, 2 * KQ), F32, kind="Internal").ap()
    values_dram = nc.dram_tensor("values_dram", (B, QUADS, P, 2 * VQ), F32, kind="Internal").ap()
    x1_dram = nc.dram_tensor("x1_dram", (T + 1, D), F32, kind="Internal").ap()
    slots_dram = nc.dram_tensor("slots_dram", (T, 2), U32, kind="Internal").ap()
    x1_tiles = x1_dram[0:T, :].rearrange("(t p) d -> p t d", p=P)

    outer = ExitStack()
    sb = lambda stack, name, shape, dt: stack.enter_context(nc.sbuf_tensor(name, shape, dt))
    with outer:
        psum = outer.enter_context(nc.psum_tensor("psum", [P, 8, 512], F32))
        ident = sb(outer, "ident", [P, P], F32)
        tanh_g = sb(outer, "tanh_g", [P, 2], F32)
        half_neg = sb(outer, "half_neg", [P, TILES], F32)
        with ExitStack() as attention:
            wq = sb(attention, "wq", [P, 2, KC, INNER], F32R)
            wo = sb(attention, "wo", [P, 2, IC, D], F32R)
            bias = sb(attention, "bias", [P, D], F32)
            wr = sb(attention, "wr", [P, KC, E], F32)
            ones = sb(attention, "ones", [P, P], BF16)
            upto = sb(attention, "upto", [P, P], BF16)
            weight8 = sb(attention, "weight8", [P, E], F32)
            token = sb(attention, "token", [P, TILES], F32)
            with ExitStack() as stack:
                setup_block(nc, stack, sb, locals())
            with ExitStack() as stack:
                attention_block(nc, stack, sb, locals())
        with ExitStack() as stack:
            ffn_block(nc, stack, sb, locals())


def setup_block(nc, stack, sb, env):
    (psum, ident, tanh_g, half_neg, wq, wo, bias, wr, ones, upto, weight8, token) = [env[k] for k in (
        "psum", "ident", "tanh_g", "half_neg", "wq", "wo", "bias", "wr", "ones", "upto", "weight8", "token")]
    (B, M, KC, CC, IC, INNER, D, E, T) = [env[k] for k in ("B", "M", "KC", "CC", "IC", "INNER", "D", "E", "T")]
    (RT, RL, ROWS, REM, PAIR, KQ, VP, VQ) = [env[k] for k in ("RT", "RL", "ROWS", "REM", "PAIR", "KQ", "VP", "VQ")]
    ctx_in, keys_dram, values_dram, x1_dram, slots_dram = [env[k] for k in (
        "ctx_in", "keys_dram", "values_dram", "x1_dram", "slots_dram")]

    raw = [sb(stack, f"raw{i}", [P, 4096], F32) for i in range(2)]
    wk = sb(stack, "wk", [P, 2, CC, INNER], F32R)
    wv = sb(stack, "wv", [P, 2, CC, INNER], F32R)
    ctx_sb = sb(stack, "ctx_sb", [P, RT + 1, CC * P], F32)
    ctxT = sb(stack, "ctxT", [P, 2, CC, ROWS], F32R)
    ctx_last = sb(stack, "ctx_last", [P, 2, CC, B, 4, 32], F32R)
    stage = sb(stack, "stage", [P, QUADS * 2 * VQ], F32R)
    empty_slots = sb(stack, "empty_slots", [P, T // P, 2], U32)
    zero_row = sb(stack, "zero_row", [1, D], F32)
    gains = sb(stack, "gains", [P, 2], F32)
    keys_stage = stage[:, 0:B * 2 * KQ].rearrange("p (b s n) -> p b s n", b=B, s=2)
    stages = [t.rearrange("p (q s n) -> p q s n", q=QUADS, s=2) for t in (
        wk[:, :, :, :].rearrange("p s c n -> p (s c n)")[:, 0:QUADS * 2 * VQ], stage[:, :])]
    wk_flat = wk[:, :, :, :].rearrange("p s c n -> p (s c n)").bitcast(F32)

    sem = lambda name: stack.enter_context(nc.semaphore(name))
    ctx_loaded, small_loaded = sem("ctx_loaded"), sem("small_loaded")
    raw_loaded = [sem("raw_loaded0"), sem("raw_loaded1")]
    raw_split = sem("raw_split")
    raw_hi = sem("raw_hi")
    consts_set, consts_shaped = sem("consts_set"), sem("consts_shaped")
    gains_ready, bias_ready = sem("gains_ready"), sem("bias_ready")
    ctxT_ready, ctxT_hi, ctxT_lo = sem("ctxT_ready"), sem("ctxT_hi"), sem("ctxT_lo")
    last_zeroed, last_ready = sem("last_zeroed"), sem("last_ready")
    bank_ready, bank_hi, bank_lo = sem("bank_ready"), sem("bank_hi"), sem("bank_lo")
    stage_zeroed, keys_zeroed = sem("stage_zeroed"), sem("keys_zeroed")
    keys_stored = sem("keys_stored")
    values_stored = [sem("values_stored0"), sem("values_stored1")]
    misc_stored = sem("misc_stored")
    KEY_USES = QUADS * 2 * 2
    weights = ((wk, env["Wk"], CC), (wv, env["Wv"], CC), (wq, env["Wq"], KC), (wo, env["Wo"], IC))

    block = stack.enter_context(nc.Block())

    @block.sync
    def _(sp):
        rows = ctx_in.rearrange("b m d -> (b m) d")
        sp.dma_start(ctx_sb[:, 0:RT, :], rows[0:RT * P, :].rearrange("(t p) d -> p t d", p=P)).then_inc(ctx_loaded, 16)
        sp.dma_start(ctx_sb[0:RL, RT, :], rows[RT * P:ROWS, :]).then_inc(ctx_loaded, 16)
        for n, (_, w, chunks) in enumerate(weights):
            if n >= 2:
                sp.wait_ge(raw_split, n - 1)
            size = w.shape[0] * w.shape[1] // P
            sp.dma_start(raw[n % 2][:, 0:size].rearrange("p (c n) -> p c n", c=chunks),
                         w.rearrange("(c p) n -> p c n", p=P)).then_inc(raw_loaded[n % 2], 16)
            if n == 0:
                sp.dma_start(gains[:, 0:1], env["g_xattn"].rearrange("(a n) -> a n", a=1).to_broadcast([P, 1])).then_inc(small_loaded, 16)
                sp.dma_start(gains[:, 1:2], env["g_ffn"].rearrange("(a n) -> a n", a=1).to_broadcast([P, 1])).then_inc(small_loaded, 16)
                sp.dma_start(bias[:, :], env["bo"].rearrange("(a n) -> a n", a=1).to_broadcast([P, D])).then_inc(small_loaded, 16)
                sp.dma_start(wr[:, :, :], env["router_w"].rearrange("(c p) e -> p c e", p=P)).then_inc(small_loaded, 16)
        sp.wait_ge(consts_set, 9)
        sp.dma_start(slots_dram.rearrange("(p n) c -> p n c", p=P), empty_slots[:, :, :]).then_inc(misc_stored, 16)
        sp.dma_start(x1_dram[T:T + 1, :], zero_row[:, :]).then_inc(misc_stored, 16)
        for q in range(QUADS):
            sp.wait_ge(bank_lo, 4 * (q + 1))
            sp.dma_start(keys_dram[:, q].rearrange("b p n -> p b n"),
                         stage[:, 0:B * 2 * KQ].bitcast(F32).rearrange("p (b n) -> p b n", b=B)).then_inc(keys_stored, 16)
        for b in range(B):
            sp.wait_ge(bank_lo, KEY_USES + 4 * (b + 1))
            sp.dma_start(values_dram[b].rearrange("q p n -> p q n"),
                         stages[b % 2].rearrange("p q s n -> p q (s n)").bitcast(F32)).then_inc(values_stored[b % 2], 16)
        sp.wait_ge(misc_stored, 32)
        sp.wait_ge(keys_stored, 16 * QUADS)
        for s in values_stored:
            sp.wait_ge(s, 16 * (B // 2))

    @block.gpsimd
    def _(pool):
        pool.memset(ident[:, :], 0.0).then_inc(consts_set, 1)
        pool.memset(upto[:, :], 1.0).then_inc(consts_set, 1)
        pool.memset(ones[:, :], 1.0).then_inc(consts_set, 1)
        pool.memset(half_neg[:, :], -0.5).then_inc(consts_set, 1)
        pool.memset(zero_row[:, :], 0.0).then_inc(consts_set, 1)
        pool.memset(empty_slots[:, :, 0:1], T).then_inc(consts_set, 1)
        pool.memset(empty_slots[:, :, 1:2], 0).then_inc(consts_set, 1)
        pool.iota(weight8[:, :], [[-1, E]], base=E, channel_multiplier=0,
                  allow_small_or_imprecise_dtypes=True).then_inc(consts_set, 1)
        pool.iota(token[:, :], [[P, TILES]], base=0, channel_multiplier=1,
                  allow_small_or_imprecise_dtypes=True).then_inc(consts_set, 1)
        pool.wait_ge(consts_set, 9)
        pool.affine_select(out=ident[:, :], in_=ident[:, :], compare_op=ALU.not_equal, fill=1.0, base=0,
                           pattern=[[-1, P]], channel_multiplier=1).then_inc(consts_shaped, 1)
        pool.affine_select(out=upto[:, :], in_=upto[:, :], compare_op=ALU.is_ge, fill=0.0, base=0,
                           pattern=[[1, P]], channel_multiplier=-1).then_inc(consts_shaped, 1)
        pool.memset(ctx_last[:, :, :, :, :, :].rearrange("p s c b j n -> p (s c b j n)").bitcast(F32), 0.0).then_inc(last_zeroed, 1)
        pool.memset(stage[:, :].bitcast(F32), 0.0).then_inc(keys_zeroed, 1)
        pool.wait_ge(bank_ready, KEY_USES)
        pool.memset(wk_flat, 0.0).then_inc(stage_zeroed, 1)
        pool.wait_ge(keys_stored, 16 * QUADS)
        pool.memset(stage[:, :].bitcast(F32), 0.0).then_inc(stage_zeroed, 1)

    def key_rows(which, n, src_of):
        q, i, hb = n // 4, n // 2 % 2, n % 2
        for r in range(2):
            rows = slice(DH * r, DH * (r + 1))
            dst = keys_stage[rows, 2 * hb:2 * hb + 2, which, PAIR * i + M * r:PAIR * i + M * (r + 1)]
            yield rows, dst

    def value_ops(n):
        b, half, last = n // 4, n // 2 % 2, n % 2
        to = stages[b % 2]
        bank = psum[:, 4 + n % 4, :]
        ops = []
        if not last:
            for q in range(2):
                for i in range(2):
                    ops.append((
                        lambda s, q=q, i=i: to[:, 2 * half + q, s, VP * i:VP * (i + 1)].rearrange(
                            "p (c d) -> p c d", d=DH)[:, 0:3:2, :],
                        bank[:, 256 * q + 128 * i:256 * q + 128 * (i + 1)].rearrange("p (c d) -> p c d", d=DH)))
        else:
            for j in range(4):
                rows = slice(32 * j, 32 * j + 32)
                col = 2 * VP + P * (j // 2) + DH * (j % 2)
                ops.append((
                    lambda s, rows=rows, col=col: to[rows, 2 * half:2 * half + 2, s, col:col + DH],
                    bank[rows, :].rearrange("p (q n) -> p q n", q=2)[:, :, DH * j:DH * (j + 1)]))
        return ops

    def context_hi(act):
        for c in range(CC + 1):
            act.wait_ge(ctxT_ready, c + 1)
            src = psum[:, c, 0:RT * P] if c < CC else psum[:, c, 0:CC * RL].rearrange("p (c n) -> p c n", c=CC)
            dst = ctxT[:, HI, c, 0:RT * P] if c < CC else ctxT[:, HI, :, RT * P:ROWS]
            act.activation(dst, src, ACT.Copy).then_inc(ctxT_hi, 1)

    def keys_hi(act):
        act.wait_ge(keys_zeroed, 1)
        for n in range(KEY_USES):
            act.wait_ge(bank_ready, n + 1)
            if n % 4 == 0 and n:
                act.wait_ge(keys_stored, 16 * (n // 4))
            for rows, dst in key_rows(HI, n, None):
                ins = act.activation(dst, psum[rows, 4 + n % 4, 0:PAIR].rearrange("p (b m) -> p b m", b=2), ACT.Copy)
            ins.then_inc(bank_hi, 1)
        for n in range(4 * B):
            b = n // 4
            act.wait_ge(bank_ready, KEY_USES + n + 1)
            if n % 4 == 0:
                act.wait_ge(stage_zeroed, min(b, 1) + 1)
                if b >= 2:
                    act.wait_ge(values_stored[b % 2], 16 * (b // 2))
            for dst, src in value_ops(n):
                ins = act.activation(dst(HI), src, ACT.Copy)
            ins.then_inc(bank_hi, 1)

    @block.scalar
    def _(act):
        act.wait_ge(small_loaded, 64)
        act.activation(tanh_g[:, :], gains[:, :], ACT.Tanh).then_inc(gains_ready, 1)
        for n, (w, _, chunks) in enumerate(weights):
            if n == 2:
                context_hi(act)
            size = w.shape[2] * w.shape[3]
            act.wait_ge(raw_loaded[n % 2], 16 * (n // 2 + 1))
            act.activation(w[:, HI, :, :].rearrange("p c n -> p (c n)"), raw[n % 2][:, 0:size], ACT.Copy).then_inc(raw_hi, 1)
        keys_hi(act)

    @block.vector
    def _(dve):
        dve.wait_ge(gains_ready, 1)
        dve.tensor_scalar(bias[:, :], bias[:, :], tanh_g[:, 0:1], None, ALU.mult).then_inc(bias_ready, 1)
        for n, (w, _, chunks) in enumerate(weights):
            if n == 2:
                for c in range(CC + 1):
                    dve.wait_ge(ctxT_hi, c + 1)
                    src = psum[:, c, 0:RT * P] if c < CC else psum[:, c, 0:CC * RL].rearrange("p (c n) -> p c n", c=CC)
                    at = lambda s: ctxT[:, s, c, 0:RT * P] if c < CC else ctxT[:, s, :, RT * P:ROWS]
                    dve.tensor_tensor(at(LO), src, at(HI).bitcast(F32), ALU.subtract).then_inc(ctxT_lo, 1)
                dve.wait_ge(ctxT_lo, CC + 1)
                dve.wait_ge(last_zeroed, 1)
                for s in (HI, LO):
                    for c in range(CC):
                        src = ctxT[:, s, c, :].bitcast(F32).rearrange("p (b m) -> p b m", b=B)[:, :, P:M]
                        for j in range(4):
                            dve.tensor_copy(ctx_last[:, s, c, :, j, 0:REM], src).then_inc(last_ready, 1)
            dve.wait_ge(raw_hi, n + 1)
            size = w.shape[2] * w.shape[3]
            dve.tensor_tensor(w[:, LO, :, :].rearrange("p c n -> p (c n)"), raw[n % 2][:, 0:size],
                              w[:, HI, :, :].rearrange("p c n -> p (c n)").bitcast(F32), ALU.subtract).then_inc(raw_split, 1)
        for n in range(KEY_USES):
            dve.wait_ge(bank_hi, n + 1)
            for (rows, lo), (_, hi) in zip(key_rows(LO, n, None), key_rows(HI, n, None)):
                ins = dve.tensor_tensor(lo, psum[rows, 4 + n % 4, 0:PAIR].rearrange("p (b m) -> p b m", b=2),
                                        hi.bitcast(F32), ALU.subtract)
            ins.then_inc(bank_lo, 1)
        for n in range(4 * B):
            dve.wait_ge(bank_hi, KEY_USES + n + 1)
            for dst, src in value_ops(n):
                ins = dve.tensor_tensor(dst(LO), src, dst(HI).bitcast(F32), ALU.subtract)
            ins.then_inc(bank_lo, 1)

    @block.tensor
    def _(pe):
        pe.wait_ge(consts_shaped, 1)
        pe.wait_ge(ctx_loaded, 32)
        for c in range(CC):
            for t in range(RT):
                ins = pe.transpose(psum[:, c, P * t:P * (t + 1)], ctx_sb[:, t, P * c:P * (c + 1)], ident[:, :])
            ins.then_inc(ctxT_ready, 1)
        for c in range(CC):
            ins = pe.transpose(psum[:, CC, RL * c:RL * (c + 1)], ctx_sb[0:RL, RT, P * c:P * (c + 1)], ident[0:RL, 0:RL])
        ins.then_inc(ctxT_ready, 1)
        pe.wait_ge(raw_split, 1)
        pe.wait_ge(ctxT_lo, CC + 1)
        for n in range(KEY_USES):
            q, i, hb = n // 4, n // 2 % 2, n % 2
            if n >= 4:
                pe.wait_ge(bank_lo, n - 3)
            k = 2 * q + i
            for c in range(CC):
                ins = split_matmul(pe, psum[:, 4 + n % 4, 0:PAIR], lambda s: wk[:, s, c, P * k:P * (k + 1)],
                                   lambda s: ctxT[:, s, c, PAIR * hb:PAIR * (hb + 1)], c == 0, c == CC - 1)
            ins.then_inc(bank_ready, 1)
        pe.wait_ge(raw_split, 2)
        pe.wait_ge(last_ready, 8 * CC)
        for n in range(4 * B):
            b, half, last = n // 4, n // 2 % 2, n % 2
            pe.wait_ge(bank_lo, KEY_USES + n - 3)
            for c in range(CC):
                rows = (lambda s: ctx_last[:, s, c, b, :, :].rearrange("p j n -> p (j n)")) if last else (
                    lambda s: ctxT[:, s, c, M * b:M * b + P])
                ins = split_matmul(pe, psum[:, 4 + n % 4, :], rows,
                                   lambda s: wv[:, s, c, 512 * half:512 * (half + 1)], c == 0, c == CC - 1)
            ins.then_inc(bank_ready, 1)


def attention_block(nc, stack, sb, env):
    (psum, ident, tanh_g, half_neg, wq, wo, bias, wr, ones, upto, weight8, token) = [env[k] for k in (
        "psum", "ident", "tanh_g", "half_neg", "wq", "wo", "bias", "wr", "ones", "upto", "weight8", "token")]
    (B, M, KC, D, E, T, NG, GPB, CAP) = [env[k] for k in ("B", "M", "KC", "D", "E", "T", "NG", "GPB", "CAP")]
    (PAIR, KQ, VP, VQ, SCALE) = [env[k] for k in ("PAIR", "KQ", "VP", "VQ", "SCALE")]
    keys_dram, values_dram, slots_dram = env["keys_dram"], env["values_dram"], env["slots_dram"]
    x_tiles, out_tiles, x1_tiles = env["x_tiles"], env["out_tiles"], env["x1_tiles"]

    keys = sb(stack, "keys", [P, QUADS, 2, KQ], F32R)
    values = sb(stack, "values", [P, QUADS, 2, VQ], F32R)
    x_in = sb(stack, "x_in", [P, TILES, D], F32)
    xT = sb(stack, "xT", [P, 2, KC, GN], F32R)
    qT = sb(stack, "qT", [P, 2, 2, 2, GN], F32R)
    exp_scores = sb(stack, "exp_scores", [P, 2, 4, M], F32)
    probs = sb(stack, "probs", [P, 4 * HP], F32)
    probsT = sb(stack, "probsT", [P, 2, 5, GN], F32R)
    attnT = sb(stack, "attnT", [P, 2, 2, GN], F32R)
    partial = sb(stack, "partial", [P, TILES, D], F32)
    x1 = sb(stack, "x1", [P, TILES, D], F32)
    xn2 = sb(stack, "xn2", [P, 2, D], F32)
    xn2T = sb(stack, "xn2T", [P, 2, D], F32)
    neg_max = sb(stack, "neg_max", [P, 2, 4], F32)
    sums = sb(stack, "sums", [P, 2, 4], F32)
    inv_sums = sb(stack, "inv_sums", [P, 2, 4], F32)
    stats = sb(stack, "stats", [P, TILES, 6], F32)
    mean_var = sb(stack, "mean_var", [P, 2, TILES, 2], F32)
    var_eps = sb(stack, "var_eps", [P, 2, TILES], F32)
    rstd = sb(stack, "rstd", [P, 2, TILES], F32)
    logits = sb(stack, "logits", [P, TILES, E], F32)
    shifted = sb(stack, "shifted", [P, TILES, E], F32)
    exps = sb(stack, "exps", [P, TILES, E], F32)
    top = sb(stack, "top", [P, TILES], F32)
    marked = sb(stack, "marked", [P, TILES, E], F32)
    first8 = sb(stack, "first8", [P, TILES], F32)
    chosen = sb(stack, "chosen", [P, TILES, E], BF16)
    chosen_sum = sb(stack, "chosen_sum", [P, E], F32)
    before = sb(stack, "before", [P, E], BF16)
    placed = sb(stack, "placed", [P, TILES, E], F32)
    place = sb(stack, "place", [P, TILES], F32)
    over = sb(stack, "over", [P, TILES], F32)
    slot = sb(stack, "slot", [P, TILES], F32)
    slot_index = sb(stack, "slot_index", [P, TILES], U32)
    denom = sb(stack, "denom", [P, TILES], F32)
    gate = sb(stack, "gate", [P, TILES], F32)
    entry = sb(stack, "entry", [P, TILES, 2], U32)

    TRANSPOSED, LAST, WIDE, SPLIT = 4, 5, 6, 7
    logits_ps = psum[:, WIDE, 0:E]
    place_ps = psum[:, WIDE, 0:TILES * E].rearrange("p (t e) -> p t e", e=E)

    sem = lambda name: stack.enter_context(nc.semaphore(name))
    keys_loaded = [sem(f"keys_loaded{q}") for q in range(QUADS)]
    values_loaded = [sem(f"values_loaded{q}") for q in range(QUADS)]
    x_loaded = sem("x_loaded")
    partial_loaded = [sem(f"partial_loaded{t}") for t in range(TILES)]
    partial_biased = sem("partial_biased")
    x1_stored = sem("x1_stored")
    slots_stored = sem("slots_stored")
    probs_zeroed = sem("probs_zeroed")
    stat_step = sem("stat_step")
    norm1_stats, norm1_rstd, norm1_done = sem("norm1_stats"), sem("norm1_rstd"), sem("norm1_done")
    norm2_stats, norm2_rstd, norm2_done = sem("norm2_stats"), sem("norm2_rstd"), sem("norm2_done")
    scores_ready, max_ready, exp_done = sem("scores_ready"), sem("max_ready"), sem("exp_done")
    sums_inverted, probs_ready = sem("sums_inverted"), sem("probs_ready")
    probsT_ready, probsT_hi, probsT_lo = sem("probsT_ready"), sem("probsT_hi"), sem("probsT_lo")
    last_hi, last_lo = sem("last_hi"), sem("last_lo")
    split_ready, split_hi, split_lo = sem("split_ready"), sem("split_hi"), sem("split_lo")
    wide_ready, wide_done = sem("wide_ready"), sem("wide_done")
    chosen_ready = sem("chosen_ready")
    shifted_ready, exps_ready = sem("shifted_ready"), sem("exps_ready")
    route_step, entry_ready = sem("route_step"), sem("entry_ready")
    dve_waits_met, pool_waits_met = sem("dve_waits_met"), sem("pool_waits_met")

    SPLIT_N, SPLIT_0 = 2 * QUADS + 2 * QUADS + KC, KC
    WIDE_N, WIDE_SKIPPED = TILES * QUADS + 2 * TILES + 1, 3 * TILES + 1
    UNITS = QUADS * TILES
    ROUTE = 14

    def split_base(g, prev):
        skipped = KC + 2 if isinstance(g, int) and g == NG else 0
        return SPLIT_N * g + SPLIT_0 + (0 if prev else 2) - skipped

    def wide_base(g, prev):
        return WIDE_N * g - WIDE_SKIPPED if prev else 0

    def norm2_use(t, cur):
        return (6, 9, 13, 14)[t] if cur else (4, 5, 8, 9)[t]

    ROUTING = {(6, 2): ("norm", 0), (8, 0): ("norm", 1), (8, 1): ("logits", 0), (8, 2): ("logits", 1),
               (9, 2): ("norm", 2), (10, 0): ("norm", 3), (10, 2): ("logits", 2), (12, 0): ("logits", 3),
               (13, 2): ("places", 0)}

    def over_groups(engine, body):
        body(0, False, True, True)
        with engine.Fori(1, NG - 1) as g:
            body(g, True, True, True)
        body(NG - 1, True, True, False)
        body(NG, True, False, False)

    block = stack.enter_context(nc.Block())

    @block.sync
    def _(sp):
        def load_keys(b, q):
            sp.dma_start(keys[:, q, :, :].rearrange("p s n -> p (s n)").bitcast(F32),
                         keys_dram[bass.ds(b, 1), q].rearrange("b p n -> (b p) n")).then_inc(keys_loaded[q], 16)

        def load_values(b, q):
            sp.dma_start(values[:, q, :, :].rearrange("p s n -> p (s n)").bitcast(F32),
                         values_dram[bass.ds(b, 1), q].rearrange("b p n -> (b p) n")).then_inc(values_loaded[q], 16)

        def load_x(g):
            sp.dma_start(x_in[:, :, :], x_tiles[:, bass.ds(g * TILES, TILES), :]).then_inc(x_loaded, 16)

        def load_partial(g, t):
            sp.dma_start(partial[:, t, :], x_tiles[:, bass.ds(g * TILES + t, 1), :].rearrange("p t d -> p (t d)")).then_inc(partial_loaded[t], 16)

        def iteration(g, more_partial, more_x, reload, last_values):
            base = split_base(g + 1, True)
            x1_base = wide_base(g + 1, True)
            if last_values:
                sp.wait_ge(split_ready, base + 2)
                load_values(g // GPB + 1, QUADS - 1)
            for t in range(TILES):
                if more_partial:
                    sp.wait_ge(wide_done, x1_base + t + 1)
                    load_partial(g + 1, t)
                if t == 0 and reload:
                    sp.wait_ge(scores_ready, UNITS * (g + 1) + TILES)
                    load_keys(g // GPB + 1, 0)
            sp.wait_ge(wide_done, x1_base + TILES)
            sp.dma_start(x1_tiles[:, bass.ds(g * TILES, TILES), :], x1[:, :, :]).then_inc(x1_stored, 16)
            sp.dma_start(out_tiles[:, bass.ds(g * TILES, TILES), :], x1[:, :, :]).then_inc(x1_stored, 16)
            if reload:
                sp.wait_ge(split_ready, base + 6)
                load_values(g // GPB + 1, 0)
                sp.wait_ge(scores_ready, UNITS * (g + 1) + 2 * TILES)
                load_keys(g // GPB + 1, 1)
                sp.wait_ge(split_ready, base + 10)
                load_values(g // GPB + 1, 1)
                sp.wait_ge(scores_ready, UNITS * (g + 1) + 3 * TILES)
                load_keys(g // GPB + 1, 2)
            if more_x:
                sp.wait_ge(split_ready, base + 12 + KC)
                load_x(g + 3)
            if reload:
                sp.wait_ge(split_ready, base + 14 + KC)
                load_values(g // GPB + 1, 2)
                sp.wait_ge(scores_ready, UNITS * (g + 1) + 4 * TILES)
                load_keys(g // GPB + 1, 3)

        load_x(0)
        for q in range(QUADS):
            load_keys(0, q)
            if q == 0:
                sp.wait_ge(split_ready, KC)
                load_x(1)
        for q in range(QUADS):
            load_values(0, q)
        for t in range(TILES):
            load_partial(0, t)
        sp.wait_ge(split_ready, split_base(0, False) + 10 + KC)
        load_x(2)
        with sp.Fori(0, B - 1) as b:
            for j in range(GPB):
                iteration(b * GPB + j, True, True, j == GPB - 2, j == GPB - 1)
        for g in range(NG - GPB, NG):
            iteration(g, g + 1 < NG, g + 3 < NG, False, False)
        sp.wait_ge(x1_stored, 32 * NG)

    @block.tensor
    def _(pe):
        uses = {"split": 0, "wide": 0}

        def split_bank(count):
            pe.wait_ge(split_lo, count)

        def transposes_x(g, c):
            if c == 0:
                pe.wait_ge(norm1_done, TILES * (g + 1))
            for t in range(TILES):
                ins = pe.transpose(psum[:, SPLIT, P * t:P * (t + 1)], x_in[:, t, P * c:P * (c + 1)], ident[:, :])
            ins.then_inc(split_ready, 1)

        def queries(q, i):
            k = 2 * q + i
            for c in range(KC):
                ins = split_matmul(pe, psum[:, SPLIT, :], lambda s: wq[:, s, c, P * k:P * (k + 1)],
                                   lambda s: xT[:, s, c, :], c == 0, c == KC - 1)
            ins.then_inc(split_ready, 1)

        def scores(g, u, queries_done):
            q, t = u // TILES, u % TILES
            if t == 0:
                pe.wait_ge(split_lo, queries_done)
                pe.wait_ge(keys_loaded[q], 16 * (g // GPB + 1))
            if not (isinstance(g, int) and g == 0 and u < 2):
                pe.wait_ge(exp_done, UNITS * g + u - 1)
            for i in range(2):
                ins = split_matmul(pe, psum[:, 2 * (u % 2) + i, 0:PAIR],
                                   lambda s: qT[:, q % 2, s, i, P * t:P * (t + 1)],
                                   lambda s: keys[:, q, s, PAIR * i:PAIR * (i + 1)], True, True)
            ins.then_inc(scores_ready, 1)

        def transposes_probs(g, u):
            q, t = u // TILES, u % TILES
            pe.wait_ge(probs_ready, UNITS * g + u + 1)
            if t == 0 and not (isinstance(g, int) and g == 0 and q == 0):
                pe.wait_ge(last_lo, QUADS * g + q)
            pe.transpose(psum[:, LAST, P * t:P * (t + 1)], probs[:, 4 * P:4 * HP], ident[:, :])
            if not (isinstance(g, int) and g == 0 and u < 1):
                pe.wait_ge(probsT_lo, UNITS * g + u)
            for h in range(4):
                ins = pe.transpose(psum[:, TRANSPOSED, P * h:P * (h + 1)], probs[:, P * h:P * (h + 1)], ident[:, :])
            ins.then_inc(probsT_ready, 1)

        def attend(g, q, i):
            if i == 0:
                pe.wait_ge(probsT_lo, UNITS * g + TILES * (q + 1))
                pe.wait_ge(last_lo, QUADS * g + q + 1)
                pe.wait_ge(values_loaded[q], 16 * (g // GPB + 1))
            parts = ((VP * i, 2 * i), (VP * i + DH, 2 * i + 1), (2 * VP + P * i, 4))
            for n, (col, chunk) in enumerate(parts):
                ins = split_matmul(pe, psum[:, SPLIT, :], lambda s: values[:, q, s, col:col + P],
                                   lambda s: probsT[:, s, chunk, :], n == 0, n == 2)
            ins.then_inc(split_ready, 1)

        def project(q, t, attend_done):
            if t == 0:
                pe.wait_ge(split_lo, attend_done)
            for i in range(2):
                ins = split_matmul(pe, psum[:, WIDE, :], lambda s: attnT[:, s, i, P * t:P * (t + 1)],
                                   lambda s: wo[:, s, 2 * q + i, :], i == 0, i == 1)
            ins.then_inc(wide_ready, 1)

        def transposes_norm2(g, t):
            pe.wait_ge(norm2_done, TILES * g + t + 1)
            for c in range(KC):
                ins = pe.transpose(psum[:, WIDE, P * c:P * (c + 1)], xn2[:, t % 2, P * c:P * (c + 1)], ident[:, :])
            ins.then_inc(wide_ready, 1)

        def route(t):
            for c in range(KC):
                ins = pe.matmul(logits_ps, xn2T[:, t % 2, P * c:P * (c + 1)], wr[:, c, :],
                                start=c == 0, stop=c == KC - 1)
            ins.then_inc(wide_ready, 1)

        def places(g):
            pe.wait_ge(chosen_ready, g + 1)
            for t in range(TILES):
                pe.matmul(place_ps[:, t, :], upto[:, :], chosen[:, t, :], start=True, stop=False)
                for s in range(t):
                    pe.matmul(place_ps[:, t, :], ones[:, :], chosen[:, s, :], start=False, stop=False)
                ins = pe.matmul(place_ps[:, t, :], ones[:, :], before[:, :], start=False, stop=True)
            ins.then_inc(wide_ready, 1)

        def group(g, prev, cur, nxt):
            split_n, wide_n = split_base(g, prev), wide_base(g, prev)

            def in_split(what, *args):
                nonlocal split_n
                pe.wait_ge(split_lo, split_n)
                what(*args)
                split_n = split_n + 1

            def in_wide(what, *args):
                nonlocal wide_n
                if not (isinstance(wide_n, int) and wide_n == 0):
                    pe.wait_ge(wide_done, wide_n)
                what(*args)
                wide_n = wide_n + 1

            def routing(u, when):
                if prev and (u, when) in ROUTING:
                    what, tile = ROUTING[u, when]
                    if what == "norm":
                        in_wide(transposes_norm2, g - 1, tile)
                    elif what == "logits":
                        in_wide(route, tile)
                    else:
                        in_wide(places, g - 1)

            for u in range(UNITS):
                q, t = u // TILES, u % TILES
                q1, g1, do1 = (q - 1, g, cur) if q else (QUADS - 1, g - 1, prev)
                u2, g2, do2 = (u + 2, g, cur) if u + 2 < UNITS else (u + 2 - UNITS, g + 1, nxt)
                q3, do3 = (q + 1, cur) if q + 1 < QUADS else (0, nxt)
                routing(u, 0)
                if t == 0 and do1:
                    in_split(attend, g1, q1, 0)
                routing(u, 1)
                if t == 2 and do3:
                    in_split(queries, q3, 1)
                if cur:
                    transposes_probs(g, u)
                if t > 0 and do1:
                    in_wide(project, q1, t - 1, split_n - (1 if t == 2 else 0))
                if t == 0:
                    if do2:
                        scores(g2, u2, split_n)
                    if do1:
                        in_split(attend, g1, q1, 1)
                elif t == 1:
                    if do2:
                        scores(g2, u2, split_n)
                    if do3:
                        in_split(queries, q3, 0)
                elif t == 2:
                    if do2:
                        scores(g2, u2, split_n)
                else:
                    if do2:
                        scores(g2, u2, split_n)
                    if do1:
                        in_wide(project, q1, 3, split_n)
                if u == 11 and nxt:
                    for c in range(KC):
                        in_split(transposes_x, g + 1, c)
                routing(u, 2)

        for c in range(KC):
            if c:
                split_bank(c)
            transposes_x(0, c)
        for i in range(2):
            split_bank(KC + i)
            queries(0, i)
        scores(0, 0, KC + 2)
        scores(0, 1, KC + 2)
        over_groups(pe, group)

    @block.scalar
    def _(act):
        def hi(dst, src, count, scale=1.0):
            act.wait_ge(split_ready, count + 1)
            act.activation(dst, src, ACT.Copy, scale=scale).then_inc(split_hi, 1)

        def exp(g, u):
            act.wait_ge(max_ready, UNITS * g + u + 1)
            if not (isinstance(g, int) and g == 0 and u < 2):
                act.wait_ge(probs_ready, UNITS * g + u - 1)
            for h in range(4):
                ins = act.activation(exp_scores[:, u % 2, h, :],
                                     psum[:, 2 * (u % 2) + h // 2, M * (h % 2):M * (h % 2 + 1)], ACT.Exp,
                                     bias=neg_max[:, u % 2, h:h + 1], accum_out=sums[:, u % 2, h:h + 1])
            ins.then_inc(exp_done, 1)

        def probs_hi(g, u):
            t = u % TILES
            act.wait_ge(probsT_ready, UNITS * g + u + 1)
            act.activation(probsT[:, HI, 0:4, P * t:P * (t + 1)],
                           psum[:, TRANSPOSED, :].rearrange("p (h n) -> p h n", h=4), ACT.Copy).then_inc(probsT_hi, 1)
            if t == TILES - 1:
                act.activation(probsT[:, HI, 4, :].rearrange("p (t n) -> p t n", t=TILES), psum[:, LAST, :].rearrange("p (t n) -> p t n", t=TILES), ACT.Copy).then_inc(last_hi, 1)

        def group(g, prev, cur, nxt):
            split_n = split_base(g, prev)

            def routing(u, when):
                what, tile = ROUTING.get((u, when), (None, None)) if prev else (None, None)
                if what == "norm":
                    act.wait_ge(wide_ready, wide_base(g, prev) + norm2_use(tile, cur) + 1)
                    act.activation(xn2T[:, tile % 2, :], psum[:, WIDE, :], ACT.Copy).then_inc(wide_done, 1)

            for u in range(UNITS):
                q, t = u // TILES, u % TILES
                do1 = cur if q else prev
                u2, g2, do2 = (u + 2, g, cur) if u + 2 < UNITS else (u + 2 - UNITS, g + 1, nxt)
                q3, do3 = (q + 1, cur) if q + 1 < QUADS else (0, nxt)
                routing(u, 0)
                if t == 0 and do1:
                    hi(attnT[:, HI, 0, :], psum[:, SPLIT, :], split_n)
                    split_n = split_n + 1
                if t == 2 and do3:
                    hi(qT[:, q3 % 2, HI, 1, :], psum[:, SPLIT, :], split_n, SCALE)
                    split_n = split_n + 1
                if t > 0 and cur:
                    probs_hi(g, u)
                if do2:
                    exp(g2, u2)
                if t == 0 and do1:
                    hi(attnT[:, HI, 1, :], psum[:, SPLIT, :], split_n)
                    split_n = split_n + 1
                if t == 0 and cur:
                    probs_hi(g, u)
                if t == 1 and do3:
                    hi(qT[:, q3 % 2, HI, 0, :], psum[:, SPLIT, :], split_n, SCALE)
                    split_n = split_n + 1
                if u == 11 and nxt:
                    for c in range(KC):
                        hi(xT[:, HI, c, :], psum[:, SPLIT, :], split_n)
                        split_n = split_n + 1
                routing(u, 2)
                if prev and u == 13:
                    act.wait_ge(shifted_ready, g)
                    act.activation(exps[:, :, :], shifted[:, :, :], ACT.Exp).then_inc(exps_ready, 1)

        for c in range(KC):
            hi(xT[:, HI, c, :], psum[:, SPLIT, :], c)
        for i in range(2):
            hi(qT[:, 0, HI, i, :], psum[:, SPLIT, :], KC + i, SCALE)
        exp(0, 0)
        exp(0, 1)
        over_groups(act, group)

    @block.vector
    def _(dve):
        def lo(which, src, count, scale=None):
            dve.wait_ge(split_hi, count + 1)
            if scale is None:
                ins = dve.tensor_tensor(which(LO), src, which(HI).bitcast(F32), ALU.subtract)
            else:
                ins = dve.scalar_tensor_tensor(out=which(LO), in0=src, scalar=scale, in1=which(HI).bitcast(F32),
                                               op0=ALU.mult, op1=ALU.subtract)
            ins.then_inc(split_lo, 1)

        def row_max(g, u):
            dve.wait_ge(scores_ready, UNITS * g + u + 1)
            src = psum[:, 2 * (u % 2):2 * (u % 2) + 2, 0:PAIR].rearrange("p i (h m) -> p i h m", h=2)
            dve.tensor_reduce(neg_max[:, u % 2, :].rearrange("p (i h) -> p i h", i=2), src, AX.X, ALU.max,
                              negate=True).then_inc(max_ready, 1)

        def invert(g, u):
            dve.wait_ge(exp_done, UNITS * g + u + 1)
            dve.reciprocal(inv_sums[:, u % 2, :], sums[:, u % 2, :]).then_inc(sums_inverted, 1)

        def probs_lo(g, u):
            t = u % TILES
            dve.wait_ge(probsT_hi, UNITS * g + u + 1)
            dve.tensor_tensor(probsT[:, LO, 0:4, P * t:P * (t + 1)],
                              psum[:, TRANSPOSED, :].rearrange("p (h n) -> p h n", h=4),
                              probsT[:, HI, 0:4, P * t:P * (t + 1)].bitcast(F32), ALU.subtract).then_inc(probsT_lo, 1)
            if t == TILES - 1:
                dve.wait_ge(last_hi, QUADS * g + u // TILES + 1)
                dve.tensor_tensor(probsT[:, LO, 4, :].rearrange("p (t n) -> p t n", t=TILES), psum[:, LAST, :].rearrange("p (t n) -> p t n", t=TILES),
                                  probsT[:, HI, 4, :].bitcast(F32).rearrange("p (t n) -> p t n", t=TILES),
                                  ALU.subtract).then_inc(last_lo, 1)

        def add_projection(g, q, t, count):
            dve.wait_ge(wide_ready, count + 1)
            if q == 0:
                dve.wait_ge(partial_biased, TILES * g + t + 1)
            last = q == QUADS - 1
            if last and t == 0 and not (isinstance(g, int) and g == 0):
                dve.wait_ge(x1_stored, 32 * g)
                dve.wait_ge(norm2_done, TILES * g)
            ins = dve.scalar_tensor_tensor(out=(x1 if last else partial)[:, t, :], in0=psum[:, WIDE, :],
                                           scalar=tanh_g[:, 0:1], in1=partial[:, t, :], op0=ALU.mult, op1=ALU.add)
            ins.then_inc(wide_done, 1)

        def group(g, prev, cur, nxt):
            split_n, wide_n = split_base(g, prev), wide_base(g, prev)
            stat_n = STATS_OF(g)

            def stat(ins):
                nonlocal stat_n
                ins.then_inc(stat_step, 1)
                stat_n = stat_n + 1
                dve.wait_ge(stat_step, stat_n)
                alone(dve, dve_waits_met)

            def norm_stats(which, t, src):
                stat(dve.bn_stats(stats[:, t, :], src))
                stat(dve.bn_aggr(mean_var[:, which, t, :], stats[:, t, :]))
                if t == TILES - 1:
                    dve.tensor_scalar(var_eps[:, which, :], mean_var[:, which, :, 1], EPS, None, ALU.add)\
                       .then_inc((norm1_stats, norm2_stats)[which], 1)

            places_n = None

            def routing(u, when):
                nonlocal wide_n, places_n
                what, tile = ROUTING.get((u, when), (None, None)) if prev else (None, None)
                if what == "logits":
                    dve.wait_ge(wide_ready, wide_n + 1)
                    dve.tensor_copy(logits[:, tile, :], logits_ps).then_inc(wide_done, 1)
                if what == "places":
                    places_n = wide_n
                if what:
                    wide_n = wide_n + 1
                return wide_n

            for u in range(UNITS):
                q, t = u // TILES, u % TILES
                q1, g1, do1 = (q - 1, g, cur) if q else (QUADS - 1, g - 1, prev)
                u2, g2, do2 = (u + 2, g, cur) if u + 2 < UNITS else (u + 2 - UNITS, g + 1, nxt)
                q3, do3 = (q + 1, cur) if q + 1 < QUADS else (0, nxt)
                routing(u, 0)
                logits_n = wide_n
                if t == 0 and do1:
                    lo(lambda s: attnT[:, s, 0, :], psum[:, SPLIT, :], split_n)
                    split_n = split_n + 1
                routing(u, 1)
                if t == 2 and do3:
                    lo(lambda s: qT[:, q3 % 2, s, 1, :], psum[:, SPLIT, :], split_n, SCALE)
                    split_n = split_n + 1
                if t > 0 and cur:
                    probs_lo(g, u)
                if t > 0 and do1:
                    add_projection(g1, q1, t - 1, wide_n)
                    wide_n = wide_n + 1
                if do2:
                    row_max(g2, u2)
                if t == 0 and do1:
                    lo(lambda s: attnT[:, s, 1, :], psum[:, SPLIT, :], split_n)
                    split_n = split_n + 1
                if t == 0 and cur:
                    probs_lo(g, u)
                if t == 1 and do3:
                    lo(lambda s: qT[:, q3 % 2, s, 0, :], psum[:, SPLIT, :], split_n, SCALE)
                    split_n = split_n + 1
                if t == 3 and do1:
                    add_projection(g1, q1, 3, wide_n)
                    wide_n = wide_n + 1
                if u == 11 and nxt:
                    for c in range(KC):
                        lo(lambda s: xT[:, s, c, :], psum[:, SPLIT, :], split_n)
                        split_n = split_n + 1
                routing(u, 2)
                if do2:
                    invert(g2, u2)
                if prev and u in (2, 3, 4):
                    for s in {2: (0,), 3: (1,), 4: (2, 3)}[u]:
                        norm_stats(1, s, x1[:, s, :])
                if nxt and 5 <= u < 5 + TILES:
                    if u == 5:
                        dve.wait_ge(x_loaded, 16 * (g + 2))
                    norm_stats(0, u - 5, x_in[:, u - 5, :])
                if prev and u == 12:
                    choose(g - 1, logits_n)
                if prev and u == 13:
                    assign(g - 1, places_n)

        def step(g, n, ins):
            ins.then_inc(route_step, 1)
            dve.wait_ge(route_step, ROUTE * g + n + 1)

        def each(t):
            return t[:, :].unsqueeze(2).to_broadcast([P, TILES, E])

        def choose(g, logits_n):
            dve.wait_ge(wide_done, logits_n)
            step(g, 0, dve.tensor_reduce(top[:, :], logits[:, :, :], AX.X, ALU.max))
            dve.tensor_tensor(shifted[:, :, :], logits[:, :, :], each(top), ALU.subtract).then_inc(shifted_ready, 1)
            step(g, 1, dve.tensor_tensor(marked[:, :, :], logits[:, :, :], each(top), ALU.is_equal))
            step(g, 2, dve.tensor_tensor(marked[:, :, :], marked[:, :, :],
                                         weight8[:, :].unsqueeze(1).to_broadcast([P, TILES, E]), ALU.mult))
            step(g, 3, dve.tensor_reduce(first8[:, :], marked[:, :, :], AX.X, ALU.max))
            dve.tensor_tensor(chosen[:, :, :], marked[:, :, :], each(first8), ALU.is_equal).then_inc(chosen_ready, 1)

        def assign(g, places_n):
            dve.wait_ge(wide_ready, places_n + 1)
            dve.tensor_tensor(placed[:, :, :], place_ps, chosen[:, :, :], ALU.mult).then_inc(wide_done, 1)
            dve.wait_ge(wide_done, places_n + 1)
            step(g, 4, dve.tensor_reduce(place[:, :], placed[:, :, :], AX.X, ALU.add))
            step(g, 5, dve.tensor_reduce(chosen_sum[:, :], chosen[:, :, :].rearrange("p t e -> p e t"), AX.X, ALU.add))
            step(g, 6, dve.tensor_tensor(before[:, :], before[:, :], chosen_sum[:, :], ALU.add))
            step(g, 7, dve.tensor_scalar(over[:, :], place[:, :], float(CAP), float(2 * T), ALU.is_gt, ALU.mult))
            step(g, 8, dve.scalar_tensor_tensor(out=slot[:, :], in0=first8[:, :], scalar=-float(CAP), in1=place[:, :],
                                                 op0=ALU.mult, op1=ALU.add))
            if not (isinstance(g, int) and g == 0):
                dve.wait_ge(slots_stored, 16 * TILES * g)
            step(g, 9, dve.scalar_tensor_tensor(out=slot[:, :], in0=slot[:, :], scalar=float(T - 1), in1=over[:, :],
                                                 op0=ALU.add, op1=ALU.add))
            dve.wait_ge(exps_ready, g + 1)
            step(g, 10, dve.tensor_reduce(denom[:, :], exps[:, :, :], AX.X, ALU.add))
            step(g, 11, dve.reciprocal(gate[:, :], denom[:, :]))
            dve.tensor_copy(slot_index[:, :], slot[:, :]).then_inc(entry_ready, 1)
            dve.tensor_scalar(entry[:, :, 1].bitcast(F32), gate[:, :], tanh_g[:, 1:2], None, ALU.mult).then_inc(entry_ready, 1)
            step(g, 12, dve.tensor_copy(entry[:, :, 0], token[:, :]))
            step(g, 13, dve.tensor_scalar(token[:, :], token[:, :], float(GN), None, ALU.add))

        def STATS_OF(g):
            if isinstance(g, int) and g == 0:
                return 2 * TILES
            return 4 * TILES * g - (2 * TILES if isinstance(g, int) and g == NG else 0)

        dve.memset(probs[:, :], 0.0).then_inc(probs_zeroed, 1)
        dve.memset(before[:, :], 0.0).then_inc(probs_zeroed, 1)
        dve.wait_ge(x_loaded, 16)
        for t in range(TILES):
            dve.bn_stats(stats[:, t, :], x_in[:, t, :]).then_inc(stat_step, 1)
            dve.wait_ge(stat_step, 2 * t + 1)
            dve.bn_aggr(mean_var[:, 0, t, :], stats[:, t, :]).then_inc(stat_step, 1)
        dve.wait_ge(stat_step, 2 * TILES)
        dve.tensor_scalar(var_eps[:, 0, :], mean_var[:, 0, :, 1], EPS, None, ALU.add).then_inc(norm1_stats, 1)
        for c in range(KC):
            lo(lambda s: xT[:, s, c, :], psum[:, SPLIT, :], c)
        for i in range(2):
            lo(lambda s: qT[:, 0, s, i, :], psum[:, SPLIT, :], KC + i, SCALE)
        row_max(0, 0)
        row_max(0, 1)
        invert(0, 0)
        invert(0, 1)
        over_groups(dve, group)

    @block.gpsimd
    def _(pool):
        def normalise(g, u):
            pool.wait_ge(sums_inverted, UNITS * g + u + 1)
            if not (isinstance(g, int) and g == 0 and u < 1):
                pool.wait_ge(probsT_ready, UNITS * g + u)
            for cols, first, n, wide in ((slice(0, 4 * P), 0, P, P), (slice(4 * P, 4 * HP), P, M - P, HP - P)):
                ins = pool.tensor_tensor(probs[:, cols].rearrange("p (h n) -> p h n", n=wide)[:, :, 0:n],
                                         exp_scores[:, u % 2, :, first:first + n],
                                         inv_sums[:, u % 2, :].unsqueeze(2).to_broadcast([P, 4, n]), ALU.mult)
            ins.then_inc(probs_ready, 1)

        def root(which, g):
            pool.wait_ge((norm1_stats, norm2_stats)[which], g + 1)
            pool.tensor_tensor(rstd[:, which, :], var_eps[:, which, :], half_neg[:, :], ALU.pow)\
                .then_inc((norm1_rstd, norm2_rstd)[which], 1)
            pool.wait_ge((norm1_rstd, norm2_rstd)[which], g + 1)
            alone(pool, pool_waits_met)

        def norm1(t):
            pool.tensor_scalar(x_in[:, t, :], x_in[:, t, :], mean_var[:, 0, t, 0:1], rstd[:, 0, t:t + 1],
                               ALU.subtract, ALU.mult).then_inc(norm1_done, 1)

        def norm2(g, t, cur):
            if t >= 2:
                pool.wait_ge(wide_done, wide_base(g + 1, True) + norm2_use(t - 2, cur) + 1)
                alone(pool, pool_waits_met)
            pool.tensor_scalar(xn2[:, t % 2, :], x1[:, t, :], mean_var[:, 1, t, 0:1], rstd[:, 1, t:t + 1],
                               ALU.subtract, ALU.mult).then_inc(norm2_done, 1)

        def add_bias(g, t):
            pool.wait_ge(partial_loaded[t], 16 * (g + 1))
            pool.tensor_tensor(partial[:, t, :], partial[:, t, :], bias[:, :], ALU.add).then_inc(partial_biased, 1)

        def group(g, prev, cur, nxt):
            for u in range(UNITS):
                u2, g2, do2 = (u + 1, g, cur) if u + 1 < UNITS else (0, g + 1, nxt)
                if do2:
                    normalise(g2, u2)
                if cur and u in (2, 3, 4):
                    for t in {2: (0,), 3: (1,), 4: (2, 3)}[u]:
                        add_bias(g, t)
                if prev and u == 5:
                    root(1, g - 1)
                if prev and 5 <= u < 5 + TILES:
                    norm2(g - 1, u - 5, cur)
                if nxt and u == 9:
                    root(0, g + 1)
                if nxt and u in (9, 10):
                    for t in (2 * (u - 9), 2 * (u - 9) + 1):
                        norm1(t)
                if prev and u == 15:
                    pool.wait_ge(entry_ready, 2 * g)
                    pool.wait_ge(route_step, ROUTE * g)
                    alone(pool, pool_waits_met)
                    for t in range(TILES):
                        pool.indirect_dma_start(out=slots_dram[:, :], out_offset=bass.IndirectOffsetOnAxis(
                            ap=slot_index[:, t:t + 1], axis=0), in_=entry[:, t, :], in_offset=None,
                            bounds_check=T - 1, oob_is_err=False).then_inc(slots_stored, 16)

        pool.wait_ge(probs_zeroed, 2)
        root(0, 0)
        for t in range(TILES):
            norm1(t)
        normalise(0, 0)
        over_groups(pool, group)
        pool.wait_ge(slots_stored, 16 * TILES * NG)


def ffn_block(nc, stack, sb, env):
    psum, ident, half_neg = env["psum"], env["ident"], env["half_neg"]
    (KC, D, E, F, T, CAP) = [env[k] for k in ("KC", "D", "E", "F", "T", "CAP")]
    w1, w2, x1_dram, slots_dram, out_rows = [env[k] for k in ("w1", "w2", "x1_dram", "slots_dram", "out_rows")]
    FC = F // P
    PAIRS = FC // 2
    PW = 2 * P
    HALVES = CAP // GN
    SLOTS = CAP // P
    assert HALVES == 2

    wh1 = sb(stack, "wh1", [P, 2, KC, F], F32R)
    wh2 = sb(stack, "wh2", [P, 2, FC, D], F32R)
    raw1 = sb(stack, "w1_raw", [P, 2, KC, PW], F32)
    raw2 = sb(stack, "w2_raw", [P, 2, 2, D], F32)
    slots = sb(stack, "slots", [P, E, SLOTS, 2], U32)
    index = sb(stack, "index", [P, HALVES, TILES], U32)
    coef = sb(stack, "coef", [P, HALVES, TILES], U32)
    rows = sb(stack, "rows", [P, HALVES, TILES, D], F32)
    normed = sb(stack, "normed", [P, TILES, D], F32)
    sT = sb(stack, "sT", [P, 2, KC, GN], F32R)
    hidden = sb(stack, "hidden", [P, 2, GN], F32)
    hT = sb(stack, "hT", [P, 2, 2, GN], F32R)
    stats2 = sb(stack, "stats2", [P, TILES, 6], F32)
    mean_var2 = sb(stack, "mean_var2", [P, TILES, 2], F32)
    var_eps2 = sb(stack, "var_eps2", [P, TILES], F32)
    rstd2 = sb(stack, "rstd2", [P, TILES], F32)

    sem = lambda name: stack.enter_context(nc.semaphore(name))
    slots_loaded = sem("slots_loaded")
    raw_loaded = [sem("w_raw_loaded0"), sem("w_raw_loaded1")]
    w_hi, w_lo = sem("w_hi"), sem("w_lo")
    index_ready = sem("index_ready")
    gathered = [sem("gathered0"), sem("gathered1")]
    scattered = [sem("scattered0"), sem("scattered1")]
    slot_step = sem("slot_step")
    s_stats, s_rstd, s_normed = sem("s_stats"), sem("s_rstd"), sem("s_normed")
    sT_ready, sT_hi, sT_lo = sem("sT_ready"), sem("sT_hi"), sem("sT_lo")
    hid_ready, gelu_done, hT_hi, hT_lo, hT_used = sem("hid_ready"), sem("gelu_done"), sem("hT_hi"), sem("hT_lo"), sem("hT_used")
    y_done = sem("y_done")
    dve_waits_met, pool_waits_met = sem("dve_waits_met2"), sem("pool_waits_met2")

    def over_experts(engine, body):
        body(0, True, True)
        with engine.Fori(1, E - 1) as e:
            body(e, False, True)
        body(E - 1, False, False)

    def weight_pairs(first, nxt, half, f):
        if half == 0 and f % 2 == 0:
            if first and f // 2 + 2 < PAIRS:
                return [(0, f // 2 + 2)]
            if not first and f == 0:
                return [(0, PAIRS - 1)]
        if half == 1 and nxt and f % 2 == 0 and f >= 2:
            return [(1, f // 2 - 1)]
        return []

    block = stack.enter_context(nc.Block())

    @block.sync
    def _(sp):
        sp.dma_start(slots[:, :, :, :].rearrange("p e k c -> p e (k c)"),
                     slots_dram.rearrange("(e p k) c -> p e (k c)", e=E, p=P)).then_inc(slots_loaded, 16)
        w1_v = w1.rearrange("e (c p) f -> p e c f", p=P)
        w2_v = w2.rearrange("e (f p) d -> p e f d", p=P)

        def load_pair(e, j2, s):
            sp.dma_start(raw1[:, s, :, :], w1_v[:, bass.ds(e, 1), :, bass.ds(j2 * 2 * PW + s * PW, PW)].rearrange(
                "p e c f -> p (e c) f")).then_inc(raw_loaded[s], 16)
            sp.dma_start(raw2[:, s, :, :], w2_v[:, bass.ds(e, 1), bass.ds(j2 * 4 + s * 2, 2), :].rearrange(
                "p e f d -> p (e f) d")).then_inc(raw_loaded[s], 16)

        load_pair(0, 0, 0)
        load_pair(0, 0, 1)
        for j2 in range(1, PAIRS // 2):
            for s in range(2):
                sp.wait_ge(w_lo, 2 * j2 + s - 1)
                load_pair(0, j2, s)
        with sp.Fori(1, E) as e:
            with sp.Fori(0, PAIRS // 2) as j2:
                for s in range(2):
                    sp.wait_ge(w_lo, PAIRS * e + 2 * j2 + s - 1)
                    load_pair(e, j2, s)

    @block.tensor
    def _(pe):
        def transposes(G, t):
            pe.wait_ge(s_normed, TILES * G + t + 1)
            if not (isinstance(G, int) and G == 0 and t < 2):
                pe.wait_ge(sT_lo, TILES * G + t - 1)
            for c in range(KC):
                ins = pe.transpose(psum[:, 6 + t % 2, P * c:P * (c + 1)], normed[:, t, P * c:P * (c + 1)], ident[:, :])
            ins.then_inc(sT_ready, 1)

        def up(e, half, f):
            if f == 0:
                pe.wait_ge(sT_lo, TILES * (2 * e + half + 1))
            if half == 0 and f % 2 == 0:
                pe.wait_ge(w_lo, PAIRS * e + f // 2 + 1)
            n = FC * (2 * e + half) + f
            if not (isinstance(n, int) and n < 2):
                pe.wait_ge(gelu_done, n - 1)
            for c in range(KC):
                ins = split_matmul(pe, psum[:, 4 + f % 2, :], lambda s: wh1[:, s, c, P * f:P * (f + 1)],
                                   lambda s: sT[:, s, c, :], c == 0, c == KC - 1)
            ins.then_inc(hid_ready, 1)

        def down(e, half, f, tiles):
            G = 2 * e + half
            for t in tiles:
                if f == 0 and not (isinstance(G, int) and G == 0):
                    pe.wait_ge(y_done, TILES * (G - 1) + t + 1)
                if t == 0:
                    pe.wait_ge(hT_lo, FC * G + f + 1)
                ins = split_matmul(pe, psum[:, t, :], lambda s: hT[:, f % 2, s, P * t:P * (t + 1)],
                                   lambda s: wh2[:, s, f, :], f == 0, f == FC - 1)
            if tiles[-1] == TILES - 1:
                ins.then_inc(hT_used, 1)

        def expert(e, first, nxt):
            for half in range(HALVES):
                more = half == 0 or nxt
                e2, half2 = (e, 1) if half == 0 else (e + 1, 0)
                for f in range(FC):
                    if f + 1 < FC:
                        up(e, half, f + 1)
                    elif more:
                        up(e2, half2, 0)
                    if f == FC - 2 and more:
                        transposes(2 * e2 + half2, 0)
                        transposes(2 * e2 + half2, 1)
                        down(e, half, f, (0, 1))
                        transposes(2 * e2 + half2, 2)
                        transposes(2 * e2 + half2, 3)
                        down(e, half, f, (2, 3))
                    else:
                        down(e, half, f, range(TILES))

        for t in range(TILES):
            transposes(0, t)
        up(0, 0, 0)
        over_experts(pe, expert)

    @block.scalar
    def _(act):
        def rows_hi(G, t):
            act.wait_ge(sT_ready, TILES * G + t + 1)
            act.activation(sT[:, HI, :, P * t:P * (t + 1)], psum[:, 6 + t % 2, :].rearrange("p (c n) -> p c n", c=KC),
                           ACT.Copy).then_inc(sT_hi, 1)

        def gelu(G, f):
            n = FC * G + f
            act.wait_ge(hid_ready, n + 1)
            if not (isinstance(n, int) and n < 2):
                act.wait_ge(hT_lo, n - 1)
                act.wait_ge(hT_used, n - 1)
            act.activation(hidden[:, f % 2, :], psum[:, 4 + f % 2, :], ACT.Gelu_apprx_tanh).then_inc(gelu_done, 1)
            act.wait_ge(gelu_done, n + 1)
            act.activation(hT[:, f % 2, HI, :], hidden[:, f % 2, :], ACT.Copy).then_inc(hT_hi, 1)

        def expert(e, first, nxt):
            for half in range(HALVES):
                more = half == 0 or nxt
                G = 2 * e + half
                for f in range(FC):
                    if f + 1 < FC:
                        gelu(G, f + 1)
                    elif more:
                        gelu(G + 1, 0)
                    if f == FC - 2 and more:
                        for t in range(TILES):
                            rows_hi(G + 1, t)

        for t in range(TILES):
            rows_hi(0, t)
        gelu(0, 0)
        over_experts(act, expert)

    @block.vector
    def _(dve):
        def split_hi(e, j):
            dve.wait_ge(raw_loaded[j % 2], 32 * (PAIRS // 2 * e + j // 2 + 1))
            if not (isinstance(e, int) and e == 0):
                dve.wait_ge(hT_used, FC * (2 * e - 1) + 2 * j + 2)
            dve.tensor_copy(wh1[:, HI, :, PW * j:PW * (j + 1)], raw1[:, j % 2, :, :]).then_inc(w_hi, 1)
            dve.tensor_copy(wh2[:, HI, 2 * j:2 * j + 2, :], raw2[:, j % 2, :, :]).then_inc(w_hi, 1)

        def fetch(e, half):
            G = 2 * e + half
            if not (isinstance(G, int) and G < 2):
                dve.wait_ge(scattered[half], 16 * TILES * e)
            src = slots[:, bass.ds(e, 1), TILES * half:TILES * (half + 1), :].rearrange("p e k c -> p (e k) c")
            dve.tensor_copy(index[:, half, :], src[:, :, 0]).then_inc(index_ready, 1)
            dve.tensor_copy(coef[:, half, :], src[:, :, 1]).then_inc(index_ready, 1)

        def step(G, n, ins):
            ins.then_inc(slot_step, 1)
            dve.wait_ge(slot_step, 2 * TILES * G + n + 1)
            alone(dve, dve_waits_met)

        def statistics(G, half, t):
            if t == 0:
                dve.wait_ge(gathered[half], 16 * TILES * (G // 2 + 1))
            step(G, 2 * t, dve.bn_stats(stats2[:, t, :], rows[:, half, t, :]))
            step(G, 2 * t + 1, dve.bn_aggr(mean_var2[:, t, :], stats2[:, t, :]))
            if t == TILES - 1:
                dve.tensor_scalar(var_eps2[:, :], mean_var2[:, :, 1], EPS, None, ALU.add).then_inc(s_stats, 1)

        def rows_lo(G, t):
            dve.wait_ge(sT_hi, TILES * G + t + 1)
            dve.tensor_tensor(sT[:, LO, :, P * t:P * (t + 1)], psum[:, 6 + t % 2, :].rearrange("p (c n) -> p c n", c=KC),
                              sT[:, HI, :, P * t:P * (t + 1)].bitcast(F32), ALU.subtract).then_inc(sT_lo, 1)

        def hidden_lo(G, f):
            dve.wait_ge(hT_hi, FC * G + f + 1)
            dve.tensor_tensor(hT[:, f % 2, LO, :], hidden[:, f % 2, :], hT[:, f % 2, HI, :].bitcast(F32),
                              ALU.subtract).then_inc(hT_lo, 1)

        def outputs(G, half):
            dve.wait_ge(hT_used, FC * (G + 1))
            for t in range(TILES):
                dve.scalar_tensor_tensor(out=rows[:, half, t, :], in0=psum[:, t, :],
                                         scalar=coef[:, half, t:t + 1].bitcast(F32), in1=rows[:, half, t, :],
                                         op0=ALU.mult, op1=ALU.add).then_inc(y_done, 1)

        def expert(e, first, nxt):
            for half in range(HALVES):
                more = half == 0 or nxt
                G = 2 * e + half
                e2, half2 = (e, 1) if half == 0 else (e + 1, 0)
                for f in range(FC):
                    if f + 1 < FC:
                        hidden_lo(G, f + 1)
                    elif more:
                        hidden_lo(G + 1, 0)
                    if f == 0 and half == 1:
                        outputs(G - 1, 0)
                    if f == 0 and half == 0 and not first:
                        outputs(G - 1, 1)
                    if f == 4 and more:
                        fetch(e2, half2)
                    if 8 <= f < 8 + TILES and more:
                        statistics(G + 1, half2, f - 8)
                    for ahead, j in weight_pairs(first, nxt, half, f):
                        split_hi(e + ahead, j)
                    if f == FC - 2 and more:
                        for t in range(TILES):
                            rows_lo(G + 1, t)

        dve.wait_ge(slots_loaded, 16)
        fetch(0, 0)
        for j in range(2):
            split_hi(0, j)
        for t in range(TILES):
            statistics(0, 0, t)
        for t in range(TILES):
            rows_lo(0, t)
        hidden_lo(0, 0)
        over_experts(dve, expert)
        outputs(2 * E - 1, 1)

    @block.gpsimd
    def _(pool):
        def split_lo(e, j):
            pool.wait_ge(w_hi, 2 * (PAIRS * e + j + 1))
            pool.tensor_tensor(wh1[:, LO, :, PW * j:PW * (j + 1)], raw1[:, j % 2, :, :],
                               wh1[:, HI, :, PW * j:PW * (j + 1)].bitcast(F32), ALU.subtract)
            pool.tensor_tensor(wh2[:, LO, 2 * j:2 * j + 2, :], raw2[:, j % 2, :, :],
                               wh2[:, HI, 2 * j:2 * j + 2, :].bitcast(F32), ALU.subtract).then_inc(w_lo, 1)

        def gather(G, half):
            pool.wait_ge(index_ready, 2 * (G + 1))
            alone(pool, pool_waits_met)
            for t in range(TILES):
                pool.indirect_dma_start(out=rows[:, half, t, :], out_offset=None, in_=x1_dram[:, :],
                                        in_offset=bass.IndirectOffsetOnAxis(ap=index[:, half, t:t + 1], axis=0),
                                        bounds_check=T, oob_is_err=False).then_inc(gathered[half], 16)

        def scatter(G, half):
            pool.wait_ge(y_done, TILES * (G + 1))
            alone(pool, pool_waits_met)
            for t in range(TILES):
                pool.indirect_dma_start(out=out_rows[:, :], in_=rows[:, half, t, :], in_offset=None,
                                        out_offset=bass.IndirectOffsetOnAxis(ap=index[:, half, t:t + 1], axis=0),
                                        bounds_check=T - 1, oob_is_err=False).then_inc(scattered[half], 16)

        def root(G):
            pool.wait_ge(s_stats, G + 1)
            pool.tensor_tensor(rstd2[:, :], var_eps2[:, :], half_neg[:, :], ALU.pow).then_inc(s_rstd, 1)
            pool.wait_ge(s_rstd, G + 1)
            alone(pool, pool_waits_met)

        def norm(G, half, t):
            if not (isinstance(G, int) and G == 0):
                pool.wait_ge(sT_ready, TILES * G)
                alone(pool, pool_waits_met)
            pool.tensor_scalar(normed[:, t, :], rows[:, half, t, :], mean_var2[:, t, 0:1], rstd2[:, t:t + 1],
                               ALU.subtract, ALU.mult).then_inc(s_normed, 1)

        def expert(e, first, nxt):
            for half in range(HALVES):
                more = half == 0 or nxt
                G = 2 * e + half
                for f in range(FC):
                    if f == 1 and half == 1:
                        scatter(G - 1, 0)
                    if f == 1 and half == 0 and not first:
                        scatter(G - 1, 1)
                    if f == 4 and more:
                        gather(G + 1, 1 - half)
                    for ahead, j in weight_pairs(first, nxt, half, f):
                        split_lo(e + ahead, j)
                    if f == 12 and more:
                        root(G + 1)
                    if f in (12, 13) and more:
                        norm(G + 1, 1 - half, 2 * (f - 12))
                        norm(G + 1, 1 - half, 2 * (f - 12) + 1)

        gather(0, 0)
        split_lo(0, 0)
        split_lo(0, 1)
        root(0)
        for t in range(TILES):
            norm(0, 0, t)
        over_experts(pool, expert)
        scatter(2 * E - 1, 1)
        for s in scattered:
            pool.wait_ge(s, 16 * TILES * E)


_INS = ["x", "ctx_768", "g_xattn", "g_ffn", "L0_xattn_Wq", "L0_xattn_Wk", "L0_xattn_Wv", "L0_xattn_Wo",
        "L0_xattn_bo", "L0_ffn_router_w", "L0_ffn_w1", "L0_ffn_w2"]


def kernel(**inputs):
    import numpy as _np
    import concourse.bacc as _bacc
    from concourse import mybir as _mybir
    from concourse.bass_utils import run_bass_kernel_spmd as _run

    nc = _bacc.Bacc("TRN2", target_bir_lowering=False, num_devices=1)
    arrays, args = {}, []
    for name in _INS:
        a = _np.ascontiguousarray(inputs[name])
        arrays[f"in_{name}_dram"] = a
        args.append(nc.dram_tensor(f"in_{name}_dram", a.shape, _mybir.dt.from_np(a.dtype), kind="ExternalInput").ap())
    args.append(nc.dram_tensor("out_0_dram", inputs["x"].shape, F32, kind="ExternalOutput").ap())
    flamingo_block(nc, *args)
    r = _run(nc, [arrays], core_ids=[0])
    return r.results[0]["out_0_dram"]
```

```python
from contextlib import ExitStack

import concourse.bass as bass
from concourse import mybir

F32 = mybir.dt.float32
F32R = mybir.dt.float32r
BF16 = mybir.dt.bfloat16
U32 = mybir.dt.uint32
ALU = mybir.AluOpType
ACT = mybir.ActivationFunctionType
AX = mybir.AxisListType

P = 128
HEADS = 16
DH = 64
TILES = 4
GN = TILES * P
QUADS = HEADS // 4
HP = 160
EPS = 1e-5

HI, LO = 0, 1
PASSES = ((LO, HI), (HI, LO), (HI, HI))


def split_matmul(pe, out, stationary, moving, first, last):
    for n, (s, m) in enumerate(PASSES):
        ins = pe.matmul(out, stationary(s), moving(m), start=first and n == 0,
                        stop=last and n == len(PASSES) - 1)
    return ins


def alone(engine, waits_met):
    engine.sem_inc(waits_met, 1)


def flamingo_block(nc, x, ctx_in, g_xattn, g_ffn, Wq, Wk, Wv, Wo, bo, router_w, w1, w2, out):
    B, N, D = x.shape
    _, M, DC = ctx_in.shape
    INNER = Wq.shape[1]
    E, _, F = w1.shape
    T = B * N
    CAP = T // E
    NG = T // GN
    GPB = NG // B
    KC, CC, IC = D // P, DC // P, INNER // P
    REM = M - P
    assert INNER == HEADS * DH and P < M <= P + 32 and CAP % GN == 0 and GPB == 4 and E == 8
    ROWS = B * M
    RT = ROWS // P
    RL = ROWS - RT * P
    PAIR = 2 * M
    KQ = 2 * PAIR
    VP = 3 * DH
    VQ = 2 * VP + 2 * P
    SCALE = float(DH) ** -0.5

    x_rows = x.rearrange("b n d -> (b n) d")
    out_rows = out.rearrange("b n d -> (b n) d")
    x_tiles = x_rows.rearrange("(t p) d -> p t d", p=P)
    out_tiles = out_rows.rearrange("(t p) d -> p t d", p=P)

    keys_dram = nc.dram_tensor("keys_dram", (B, QUADS, P, 2 * KQ), F32, kind="Internal").ap()
    values_dram = nc.dram_tensor("values_dram", (B, QUADS, P, 2 * VQ), F32, kind="Internal").ap()
    x1_dram = nc.dram_tensor("x1_dram", (T + 1, D), F32, kind="Internal").ap()
    slots_dram = nc.dram_tensor("slots_dram", (T, 2), U32, kind="Internal").ap()
    x1_tiles = x1_dram[0:T, :].rearrange("(t p) d -> p t d", p=P)

    outer = ExitStack()
    sb = lambda stack, name, shape, dt: stack.enter_context(nc.sbuf_tensor(name, shape, dt))
    with outer:
        psum = outer.enter_context(nc.psum_tensor("psum", [P, 8, 512], F32))
        ident = sb(outer, "ident", [P, P], F32)
        tanh_g = sb(outer, "tanh_g", [P, 2], F32)
        half_neg = sb(outer, "half_neg", [P, TILES], F32)
        with ExitStack() as attention:
            wq = sb(attention, "wq", [P, 2, KC, INNER], F32R)
            wo = sb(attention, "wo", [P, 2, IC, D], F32R)
            bias = sb(attention, "bias", [P, D], F32)
            wr = sb(attention, "wr", [P, KC, E], F32)
            ones = sb(attention, "ones", [P, P], BF16)
            upto = sb(attention, "upto", [P, P], BF16)
            weight8 = sb(attention, "weight8", [P, E], F32)
            token = sb(attention, "token", [P, TILES], F32)
            with ExitStack() as stack:
                setup_block(nc, stack, sb, locals())
            with ExitStack() as stack:
                attention_block(nc, stack, sb, locals())
        with ExitStack() as stack:
            ffn_block(nc, stack, sb, locals())


def setup_block(nc, stack, sb, env):
    (psum, ident, tanh_g, half_neg, wq, wo, bias, wr, ones, upto, weight8, token) = [env[k] for k in (
        "psum", "ident", "tanh_g", "half_neg", "wq", "wo", "bias", "wr", "ones", "upto", "weight8", "token")]
    (B, M, KC, CC, IC, INNER, D, E, T) = [env[k] for k in ("B", "M", "KC", "CC", "IC", "INNER", "D", "E", "T")]
    (RT, RL, ROWS, REM, PAIR, KQ, VP, VQ) = [env[k] for k in ("RT", "RL", "ROWS", "REM", "PAIR", "KQ", "VP", "VQ")]
    ctx_in, keys_dram, values_dram, x1_dram, slots_dram = [env[k] for k in (
        "ctx_in", "keys_dram", "values_dram", "x1_dram", "slots_dram")]

    raw = [sb(stack, f"raw{i}", [P, 4096], F32) for i in range(2)]
    wk = sb(stack, "wk", [P, 2, CC, INNER], F32R)
    wv = sb(stack, "wv", [P, 2, CC, INNER], F32R)
    ctx_sb = sb(stack, "ctx_sb", [P, RT + 1, CC * P], F32)
    ctxT = sb(stack, "ctxT", [P, 2, CC, ROWS], F32R)
    ctx_last = sb(stack, "ctx_last", [P, 2, CC, B, 4, 32], F32R)
    stage = sb(stack, "stage", [P, QUADS * 2 * VQ], F32R)
    empty_slots = sb(stack, "empty_slots", [P, T // P, 2], U32)
    zero_row = sb(stack, "zero_row", [1, D], F32)
    gains = sb(stack, "gains", [P, 2], F32)
    keys_stage = stage[:, 0:B * 2 * KQ].rearrange("p (b s n) -> p b s n", b=B, s=2)
    stages = [t.rearrange("p (q s n) -> p q s n", q=QUADS, s=2) for t in (
        wk[:, :, :, :].rearrange("p s c n -> p (s c n)")[:, 0:QUADS * 2 * VQ], stage[:, :])]
    wk_flat = wk[:, :, :, :].rearrange("p s c n -> p (s c n)").bitcast(F32)

    sem = lambda name: stack.enter_context(nc.semaphore(name))
    ctx_loaded, small_loaded = sem("ctx_loaded"), sem("small_loaded")
    raw_loaded = [sem("raw_loaded0"), sem("raw_loaded1")]
    raw_split = sem("raw_split")
    raw_hi = sem("raw_hi")
    consts_set, consts_shaped = sem("consts_set"), sem("consts_shaped")
    gains_ready, bias_ready = sem("gains_ready"), sem("bias_ready")
    ctxT_ready, ctxT_hi, ctxT_lo = sem("ctxT_ready"), sem("ctxT_hi"), sem("ctxT_lo")
    last_zeroed, last_ready = sem("last_zeroed"), sem("last_ready")
    bank_ready, bank_hi, bank_lo = sem("bank_ready"), sem("bank_hi"), sem("bank_lo")
    stage_zeroed, keys_zeroed = sem("stage_zeroed"), sem("keys_zeroed")
    keys_stored = sem("keys_stored")
    values_stored = [sem("values_stored0"), sem("values_stored1")]
    misc_stored = sem("misc_stored")
    KEY_USES = QUADS * 2 * 2
    weights = ((wk, env["Wk"], CC), (wv, env["Wv"], CC), (wq, env["Wq"], KC), (wo, env["Wo"], IC))

    block = stack.enter_context(nc.Block())

    @block.sync
    def _(sp):
        rows = ctx_in.rearrange("b m d -> (b m) d")
        sp.dma_start(ctx_sb[:, 0:RT, :], rows[0:RT * P, :].rearrange("(t p) d -> p t d", p=P)).then_inc(ctx_loaded, 16)
        sp.dma_start(ctx_sb[0:RL, RT, :], rows[RT * P:ROWS, :]).then_inc(ctx_loaded, 16)
        for n, (_, w, chunks) in enumerate(weights):
            if n >= 2:
                sp.wait_ge(raw_split, n - 1)
            size = w.shape[0] * w.shape[1] // P
            sp.dma_start(raw[n % 2][:, 0:size].rearrange("p (c n) -> p c n", c=chunks),
                         w.rearrange("(c p) n -> p c n", p=P)).then_inc(raw_loaded[n % 2], 16)
            if n == 0:
                sp.dma_start(gains[:, 0:1], env["g_xattn"].rearrange("(a n) -> a n", a=1).to_broadcast([P, 1])).then_inc(small_loaded, 16)
                sp.dma_start(gains[:, 1:2], env["g_ffn"].rearrange("(a n) -> a n", a=1).to_broadcast([P, 1])).then_inc(small_loaded, 16)
                sp.dma_start(bias[:, :], env["bo"].rearrange("(a n) -> a n", a=1).to_broadcast([P, D])).then_inc(small_loaded, 16)
                sp.dma_start(wr[:, :, :], env["router_w"].rearrange("(c p) e -> p c e", p=P)).then_inc(small_loaded, 16)
        sp.wait_ge(consts_set, 9)
        sp.dma_start(slots_dram.rearrange("(p n) c -> p n c", p=P), empty_slots[:, :, :]).then_inc(misc_stored, 16)
        sp.dma_start(x1_dram[T:T + 1, :], zero_row[:, :]).then_inc(misc_stored, 16)
        for q in range(QUADS):
            sp.wait_ge(bank_lo, 4 * (q + 1))
            sp.dma_start(keys_dram[:, q].rearrange("b p n -> p b n"),
                         stage[:, 0:B * 2 * KQ].bitcast(F32).rearrange("p (b n) -> p b n", b=B)).then_inc(keys_stored, 16)
        for b in range(B):
            sp.wait_ge(bank_lo, KEY_USES + 4 * (b + 1))
            sp.dma_start(values_dram[b].rearrange("q p n -> p q n"),
                         stages[b % 2].rearrange("p q s n -> p q (s n)").bitcast(F32)).then_inc(values_stored[b % 2], 16)
        sp.wait_ge(misc_stored, 32)
        sp.wait_ge(keys_stored, 16 * QUADS)
        for s in values_stored:
            sp.wait_ge(s, 16 * (B // 2))

    @block.gpsimd
    def _(pool):
        pool.memset(ident[:, :], 0.0).then_inc(consts_set, 1)
        pool.memset(upto[:, :], 1.0).then_inc(consts_set, 1)
        pool.memset(ones[:, :], 1.0).then_inc(consts_set, 1)
        pool.memset(half_neg[:, :], -0.5).then_inc(consts_set, 1)
        pool.memset(zero_row[:, :], 0.0).then_inc(consts_set, 1)
        pool.memset(empty_slots[:, :, 0:1], T).then_inc(consts_set, 1)
        pool.memset(empty_slots[:, :, 1:2], 0).then_inc(consts_set, 1)
        pool.iota(weight8[:, :], [[-1, E]], base=E, channel_multiplier=0,
                  allow_small_or_imprecise_dtypes=True).then_inc(consts_set, 1)
        pool.iota(token[:, :], [[P, TILES]], base=0, channel_multiplier=1,
                  allow_small_or_imprecise_dtypes=True).then_inc(consts_set, 1)
        pool.wait_ge(consts_set, 9)
        pool.affine_select(out=ident[:, :], in_=ident[:, :], compare_op=ALU.not_equal, fill=1.0, base=0,
                           pattern=[[-1, P]], channel_multiplier=1).then_inc(consts_shaped, 1)
        pool.affine_select(out=upto[:, :], in_=upto[:, :], compare_op=ALU.is_ge, fill=0.0, base=0,
                           pattern=[[1, P]], channel_multiplier=-1).then_inc(consts_shaped, 1)
        pool.memset(ctx_last[:, :, :, :, :, :].rearrange("p s c b j n -> p (s c b j n)").bitcast(F32), 0.0).then_inc(last_zeroed, 1)
        pool.memset(stage[:, :].bitcast(F32), 0.0).then_inc(keys_zeroed, 1)
        pool.wait_ge(bank_ready, KEY_USES)
        pool.memset(wk_flat, 0.0).then_inc(stage_zeroed, 1)
        pool.wait_ge(keys_stored, 16 * QUADS)
        pool.memset(stage[:, :].bitcast(F32), 0.0).then_inc(stage_zeroed, 1)

    def key_rows(which, n, src_of):
        q, i, hb = n // 4, n // 2 % 2, n % 2
        for r in range(2):
            rows = slice(DH * r, DH * (r + 1))
            dst = keys_stage[rows, 2 * hb:2 * hb + 2, which, PAIR * i + M * r:PAIR * i + M * (r + 1)]
            yield rows, dst

    def value_ops(n):
        b, half, last = n // 4, n // 2 % 2, n % 2
        to = stages[b % 2]
        bank = psum[:, 4 + n % 4, :]
        ops = []
        if not last:
            for q in range(2):
                for i in range(2):
                    ops.append((
                        lambda s, q=q, i=i: to[:, 2 * half + q, s, VP * i:VP * (i + 1)].rearrange(
                            "p (c d) -> p c d", d=DH)[:, 0:3:2, :],
                        bank[:, 256 * q + 128 * i:256 * q + 128 * (i + 1)].rearrange("p (c d) -> p c d", d=DH)))
        else:
            for j in range(4):
                rows = slice(32 * j, 32 * j + 32)
                col = 2 * VP + P * (j // 2) + DH * (j % 2)
                ops.append((
                    lambda s, rows=rows, col=col: to[rows, 2 * half:2 * half + 2, s, col:col + DH],
                    bank[rows, :].rearrange("p (q n) -> p q n", q=2)[:, :, DH * j:DH * (j + 1)]))
        return ops

    def context_hi(act):
        for c in range(CC + 1):
            act.wait_ge(ctxT_ready, c + 1)
            src = psum[:, c, 0:RT * P] if c < CC else psum[:, c, 0:CC * RL].rearrange("p (c n) -> p c n", c=CC)
            dst = ctxT[:, HI, c, 0:RT * P] if c < CC else ctxT[:, HI, :, RT * P:ROWS]
            act.activation(dst, src, ACT.Copy).then_inc(ctxT_hi, 1)

    def keys_hi(act):
        act.wait_ge(keys_zeroed, 1)
        for n in range(KEY_USES):
            act.wait_ge(bank_ready, n + 1)
            if n % 4 == 0 and n:
                act.wait_ge(keys_stored, 16 * (n // 4))
            for rows, dst in key_rows(HI, n, None):
                ins = act.activation(dst, psum[rows, 4 + n % 4, 0:PAIR].rearrange("p (b m) -> p b m", b=2), ACT.Copy)
            ins.then_inc(bank_hi, 1)
        for n in range(4 * B):
            b = n // 4
            act.wait_ge(bank_ready, KEY_USES + n + 1)
            if n % 4 == 0:
                act.wait_ge(stage_zeroed, min(b, 1) + 1)
                if b >= 2:
                    act.wait_ge(values_stored[b % 2], 16 * (b // 2))
            for dst, src in value_ops(n):
                ins = act.activation(dst(HI), src, ACT.Copy)
            ins.then_inc(bank_hi, 1)

    @block.scalar
    def _(act):
        act.wait_ge(small_loaded, 64)
        act.activation(tanh_g[:, :], gains[:, :], ACT.Tanh).then_inc(gains_ready, 1)
        for n, (w, _, chunks) in enumerate(weights):
            if n == 2:
                context_hi(act)
            size = w.shape[2] * w.shape[3]
            act.wait_ge(raw_loaded[n % 2], 16 * (n // 2 + 1))
            act.activation(w[:, HI, :, :].rearrange("p c n -> p (c n)"), raw[n % 2][:, 0:size], ACT.Copy).then_inc(raw_hi, 1)
        keys_hi(act)

    @block.vector
    def _(dve):
        dve.wait_ge(gains_ready, 1)
        dve.tensor_scalar(bias[:, :], bias[:, :], tanh_g[:, 0:1], None, ALU.mult).then_inc(bias_ready, 1)
        for n, (w, _, chunks) in enumerate(weights):
            if n == 2:
                for c in range(CC + 1):
                    dve.wait_ge(ctxT_hi, c + 1)
                    src = psum[:, c, 0:RT * P] if c < CC else psum[:, c, 0:CC * RL].rearrange("p (c n) -> p c n", c=CC)
                    at = lambda s: ctxT[:, s, c, 0:RT * P] if c < CC else ctxT[:, s, :, RT * P:ROWS]
                    dve.tensor_tensor(at(LO), src, at(HI).bitcast(F32), ALU.subtract).then_inc(ctxT_lo, 1)
                dve.wait_ge(ctxT_lo, CC + 1)
                dve.wait_ge(last_zeroed, 1)
                for s in (HI, LO):
                    for c in range(CC):
                        src = ctxT[:, s, c, :].bitcast(F32).rearrange("p (b m) -> p b m", b=B)[:, :, P:M]
                        for j in range(4):
                            dve.tensor_copy(ctx_last[:, s, c, :, j, 0:REM], src).then_inc(last_ready, 1)
            dve.wait_ge(raw_hi, n + 1)
            size = w.shape[2] * w.shape[3]
            dve.tensor_tensor(w[:, LO, :, :].rearrange("p c n -> p (c n)"), raw[n % 2][:, 0:size],
                              w[:, HI, :, :].rearrange("p c n -> p (c n)").bitcast(F32), ALU.subtract).then_inc(raw_split, 1)
        for n in range(KEY_USES):
            dve.wait_ge(bank_hi, n + 1)
            for (rows, lo), (_, hi) in zip(key_rows(LO, n, None), key_rows(HI, n, None)):
                ins = dve.tensor_tensor(lo, psum[rows, 4 + n % 4, 0:PAIR].rearrange("p (b m) -> p b m", b=2),
                                        hi.bitcast(F32), ALU.subtract)
            ins.then_inc(bank_lo, 1)
        for n in range(4 * B):
            dve.wait_ge(bank_hi, KEY_USES + n + 1)
            for dst, src in value_ops(n):
                ins = dve.tensor_tensor(dst(LO), src, dst(HI).bitcast(F32), ALU.subtract)
            ins.then_inc(bank_lo, 1)

    @block.tensor
    def _(pe):
        pe.wait_ge(consts_shaped, 1)
        pe.wait_ge(ctx_loaded, 32)
        for c in range(CC):
            for t in range(RT):
                ins = pe.transpose(psum[:, c, P * t:P * (t + 1)], ctx_sb[:, t, P * c:P * (c + 1)], ident[:, :])
            ins.then_inc(ctxT_ready, 1)
        for c in range(CC):
            ins = pe.transpose(psum[:, CC, RL * c:RL * (c + 1)], ctx_sb[0:RL, RT, P * c:P * (c + 1)], ident[0:RL, 0:RL])
        ins.then_inc(ctxT_ready, 1)
        pe.wait_ge(raw_split, 1)
        pe.wait_ge(ctxT_lo, CC + 1)
        for n in range(KEY_USES):
            q, i, hb = n // 4, n // 2 % 2, n % 2
            if n >= 4:
                pe.wait_ge(bank_lo, n - 3)
            k = 2 * q + i
            for c in range(CC):
                ins = split_matmul(pe, psum[:, 4 + n % 4, 0:PAIR], lambda s: wk[:, s, c, P * k:P * (k + 1)],
                                   lambda s: ctxT[:, s, c, PAIR * hb:PAIR * (hb + 1)], c == 0, c == CC - 1)
            ins.then_inc(bank_ready, 1)
        pe.wait_ge(raw_split, 2)
        pe.wait_ge(last_ready, 8 * CC)
        for n in range(4 * B):
            b, half, last = n // 4, n // 2 % 2, n % 2
            pe.wait_ge(bank_lo, KEY_USES + n - 3)
            for c in range(CC):
                rows = (lambda s: ctx_last[:, s, c, b, :, :].rearrange("p j n -> p (j n)")) if last else (
                    lambda s: ctxT[:, s, c, M * b:M * b + P])
                ins = split_matmul(pe, psum[:, 4 + n % 4, :], rows,
                                   lambda s: wv[:, s, c, 512 * half:512 * (half + 1)], c == 0, c == CC - 1)
            ins.then_inc(bank_ready, 1)


def attention_block(nc, stack, sb, env):
    (psum, ident, tanh_g, half_neg, wq, wo, bias, wr, ones, upto, weight8, token) = [env[k] for k in (
        "psum", "ident", "tanh_g", "half_neg", "wq", "wo", "bias", "wr", "ones", "upto", "weight8", "token")]
    (B, M, KC, D, E, T, NG, GPB, CAP) = [env[k] for k in ("B", "M", "KC", "D", "E", "T", "NG", "GPB", "CAP")]
    (PAIR, KQ, VP, VQ, SCALE) = [env[k] for k in ("PAIR", "KQ", "VP", "VQ", "SCALE")]
    keys_dram, values_dram, slots_dram = env["keys_dram"], env["values_dram"], env["slots_dram"]
    x_tiles, out_tiles, x1_tiles = env["x_tiles"], env["out_tiles"], env["x1_tiles"]

    keys = sb(stack, "keys", [P, QUADS, 2, KQ], F32R)
    values = sb(stack, "values", [P, QUADS, 2, VQ], F32R)
    x_in = sb(stack, "x_in", [P, TILES, D], F32)
    xT = sb(stack, "xT", [P, 2, KC, GN], F32R)
    qT = sb(stack, "qT", [P, 2, 2, 2, GN], F32R)
    exp_scores = sb(stack, "exp_scores", [P, 2, 4, M], F32)
    probs = sb(stack, "probs", [P, 4 * HP], F32)
    probsT = sb(stack, "probsT", [P, 2, 5, GN], F32R)
    attnT = sb(stack, "attnT", [P, 2, 2, GN], F32R)
    partial = sb(stack, "partial", [P, TILES, D], F32)
    x1 = sb(stack, "x1", [P, TILES, D], F32)
    xn2 = sb(stack, "xn2", [P, 2, D], F32)
    xn2T = sb(stack, "xn2T", [P, 2, D], F32)
    neg_max = sb(stack, "neg_max", [P, 2, 4], F32)
    sums = sb(stack, "sums", [P, 2, 4], F32)
    inv_sums = sb(stack, "inv_sums", [P, 2, 4], F32)
    stats = sb(stack, "stats", [P, TILES, 6], F32)
    mean_var = sb(stack, "mean_var", [P, 2, TILES, 2], F32)
    var_eps = sb(stack, "var_eps", [P, 2, TILES], F32)
    rstd = sb(stack, "rstd", [P, 2, TILES], F32)
    logits = sb(stack, "logits", [P, TILES, E], F32)
    shifted = sb(stack, "shifted", [P, TILES, E], F32)
    exps = sb(stack, "exps", [P, TILES, E], F32)
    top = sb(stack, "top", [P, TILES], F32)
    marked = sb(stack, "marked", [P, TILES, E], F32)
    first8 = sb(stack, "first8", [P, TILES], F32)
    chosen = sb(stack, "chosen", [P, TILES, E], BF16)
    chosen_sum = sb(stack, "chosen_sum", [P, E], F32)
    before = sb(stack, "before", [P, E], BF16)
    placed = sb(stack, "placed", [P, TILES, E], F32)
    place = sb(stack, "place", [P, TILES], F32)
    over = sb(stack, "over", [P, TILES], F32)
    slot = sb(stack, "slot", [P, TILES], F32)
    slot_index = sb(stack, "slot_index", [P, TILES], U32)
    denom = sb(stack, "denom", [P, TILES], F32)
    gate = sb(stack, "gate", [P, TILES], F32)
    entry = sb(stack, "entry", [P, TILES, 2], U32)

    TRANSPOSED, LAST, ODD, EVEN = 4, 5, 6, 7
    ATTEND_BANK, PROJECT_BANK, QUERY_BANK = (EVEN, ODD), (ODD, ODD, EVEN, ODD), EVEN
    X_BANK, LOGITS_BANK = (EVEN, TRANSPOSED, EVEN, ODD), ODD
    logits_ps = psum[:, LOGITS_BANK, 0:2 * E].rearrange("p (t e) -> p t e", e=E)
    place_ps = psum[:, TRANSPOSED, 0:TILES * E].rearrange("p (t e) -> p t e", e=E)

    sem = lambda name: stack.enter_context(nc.semaphore(name))
    keys_loaded = [sem(f"keys_loaded{q}") for q in range(QUADS)]
    values_loaded = [sem(f"values_loaded{q}") for q in range(QUADS)]
    x_loaded = sem("x_loaded")
    partial_loaded = [sem(f"partial_loaded{t}") for t in range(TILES)]
    partial_biased = sem("partial_biased")
    x1_stored = sem("x1_stored")
    slots_stored = sem("slots_stored")
    probs_zeroed = sem("probs_zeroed")
    stat_step = sem("stat_step")
    norm1_stats, norm1_rstd, norm1_done = sem("norm1_stats"), sem("norm1_rstd"), sem("norm1_done")
    norm2_stats, norm2_rstd, norm2_done = sem("norm2_stats"), sem("norm2_rstd"), sem("norm2_done")
    scores_ready, max_ready, exp_done = sem("scores_ready"), sem("max_ready"), sem("exp_done")
    sums_inverted, probs_ready = sem("sums_inverted"), sem("probs_ready")
    probsT_ready, probsT_hi, probsT_lo = sem("probsT_ready"), sem("probsT_hi"), sem("probsT_lo")
    last_hi, last_lo = sem("last_hi"), sem("last_lo")
    xT_ready, xT_hi, xT_lo = sem("xT_ready"), sem("xT_hi"), sem("xT_lo")
    query_ready, query_hi, query_lo = sem("query_ready"), sem("query_hi"), sem("query_lo")
    attn_ready, attn_hi, attn_lo = sem("attn_ready"), sem("attn_hi"), sem("attn_lo")
    proj_ready, proj_added = sem("proj_ready"), sem("proj_added")
    norm2T_ready, norm2T_copied = sem("norm2T_ready"), sem("norm2T_copied")
    logits_ready, logits_copied = sem("logits_ready"), sem("logits_copied")
    places_ready, places_read = sem("places_ready"), sem("places_read")
    chosen_ready = sem("chosen_ready")
    shifted_ready, exps_ready = sem("shifted_ready"), sem("exps_ready")
    route_step, entry_ready = sem("route_step"), sem("entry_ready")
    dve_waits_met, pool_waits_met = sem("dve_waits_met"), sem("pool_waits_met")

    UNITS = QUADS * TILES
    ROUTE = 14
    ROUTING = {5: ("norm", 0), 6: ("norm", 1), 7: ("logits", 0), 9: ("norm", 2), 10: ("norm", 3),
               11: ("logits", 1), 13: ("places", 0)}

    def over_groups(engine, body):
        body(0, False, True, True)
        with engine.Fori(1, NG - 1) as g:
            body(g, True, True, True)
        body(NG - 1, True, True, False)
        body(NG, True, False, False)

    block = stack.enter_context(nc.Block())

    @block.sync
    def _(sp):
        def load_keys(b, q):
            sp.dma_start(keys[:, q, :, :].rearrange("p s n -> p (s n)").bitcast(F32),
                         keys_dram[bass.ds(b, 1), q].rearrange("b p n -> (b p) n")).then_inc(keys_loaded[q], 16)

        def load_values(b, q):
            sp.dma_start(values[:, q, :, :].rearrange("p s n -> p (s n)").bitcast(F32),
                         values_dram[bass.ds(b, 1), q].rearrange("b p n -> (b p) n")).then_inc(values_loaded[q], 16)

        def load_x(g):
            sp.dma_start(x_in[:, :, :], x_tiles[:, bass.ds(g * TILES, TILES), :]).then_inc(x_loaded, 16)

        def load_partial(g, t):
            sp.dma_start(partial[:, t, :], x_tiles[:, bass.ds(g * TILES + t, 1), :].rearrange("p t d -> p (t d)")).then_inc(partial_loaded[t], 16)

        def iteration(g, more_partial, more_x, reload, last_values):
            used = 2 * QUADS * (g + 1)
            added = TILES * (QUADS * g + QUADS - 1)
            if last_values:
                sp.wait_ge(attn_ready, used)
                load_values(g // GPB + 1, QUADS - 1)
            for t in range(TILES):
                if more_partial:
                    sp.wait_ge(proj_added, added + t + 1)
                    load_partial(g + 1, t)
                if t == 0 and reload:
                    sp.wait_ge(scores_ready, UNITS * (g + 1) + TILES)
                    load_keys(g // GPB + 1, 0)
            sp.wait_ge(proj_added, added + TILES)
            sp.dma_start(x1_tiles[:, bass.ds(g * TILES, TILES), :], x1[:, :, :]).then_inc(x1_stored, 16)
            sp.dma_start(out_tiles[:, bass.ds(g * TILES, TILES), :], x1[:, :, :]).then_inc(x1_stored, 16)
            if reload:
                sp.wait_ge(attn_ready, used + 2)
                load_values(g // GPB + 1, 0)
                sp.wait_ge(scores_ready, UNITS * (g + 1) + 2 * TILES)
                load_keys(g // GPB + 1, 1)
                sp.wait_ge(attn_ready, used + 4)
                load_values(g // GPB + 1, 1)
                sp.wait_ge(scores_ready, UNITS * (g + 1) + 3 * TILES)
                load_keys(g // GPB + 1, 2)
            if more_x:
                sp.wait_ge(xT_ready, KC * (g + 3))
                load_x(g + 3)
            if reload:
                sp.wait_ge(attn_ready, used + 6)
                load_values(g // GPB + 1, 2)
                sp.wait_ge(scores_ready, UNITS * (g + 1) + 4 * TILES)
                load_keys(g // GPB + 1, 3)

        load_x(0)
        for q in range(QUADS):
            load_keys(0, q)
            if q == 0:
                sp.wait_ge(xT_ready, KC)
                load_x(1)
        for q in range(QUADS):
            load_values(0, q)
        for t in range(TILES):
            load_partial(0, t)
        sp.wait_ge(xT_ready, 2 * KC)
        load_x(2)
        with sp.Fori(0, B - 1) as b:
            for j in range(GPB):
                iteration(b * GPB + j, True, True, j == GPB - 2, j == GPB - 1)
        for g in range(NG - GPB, NG):
            iteration(g, g + 1 < NG, g + 3 < NG, False, False)
        sp.wait_ge(x1_stored, 32 * NG)

    @block.tensor
    def _(pe):
        def transposes_x(g, c):
            if c == 0:
                pe.wait_ge(norm1_done, TILES * (g + 1))
            for t in range(TILES):
                ins = pe.transpose(psum[:, X_BANK[c], P * t:P * (t + 1)], x_in[:, t, P * c:P * (c + 1)], ident[:, :])
            ins.then_inc(xT_ready, 1)

        def queries(g, q, i):
            k, n = 2 * q + i, QUADS * g + q
            if i == 1:
                pe.wait_ge(query_lo, 2 * n + 1)
            elif isinstance(n, int) and n < 2:
                pe.wait_ge(xT_lo, KC * (g + 1))
            else:
                pe.wait_ge(attn_lo, 2 * (n - 2) + 1)
                if q == 0:
                    pe.wait_ge(xT_lo, KC * (g + 1))
            for c in range(KC):
                ins = split_matmul(pe, psum[:, QUERY_BANK, :], lambda s: wq[:, s, c, P * k:P * (k + 1)],
                                   lambda s: xT[:, s, c, :], c == 0, c == KC - 1)
            ins.then_inc(query_ready, 1)

        def scores(g, u):
            q, t = u // TILES, u % TILES
            if t == 0:
                pe.wait_ge(query_lo, 2 * (QUADS * g + q) + 2)
                pe.wait_ge(keys_loaded[q], 16 * (g // GPB + 1))
            if not (isinstance(g, int) and g == 0 and u < 2):
                pe.wait_ge(exp_done, UNITS * g + u - 1)
            for i in range(2):
                ins = split_matmul(pe, psum[:, 2 * (u % 2) + i, 0:PAIR],
                                   lambda s: qT[:, q % 2, s, i, P * t:P * (t + 1)],
                                   lambda s: keys[:, q, s, PAIR * i:PAIR * (i + 1)], True, True)
            ins.then_inc(scores_ready, 1)

        def transposes_probs(g, u, aux):
            q, t = u // TILES, u % TILES
            pe.wait_ge(probs_ready, UNITS * g + u + 1)
            if aux:
                pe.wait_ge(*aux)
            elif not (isinstance(g, int) and g == 0 and u < 1):
                pe.wait_ge(probsT_lo, UNITS * g + u)
            for h in range(4):
                pe.transpose(psum[:, TRANSPOSED, P * h:P * (h + 1)], probs[:, P * h:P * (h + 1)], ident[:, :])
            if t == 0 and not (isinstance(g, int) and g == 0 and q == 0):
                pe.wait_ge(last_lo, QUADS * g + q)
            pe.transpose(psum[:, LAST, P * t:P * (t + 1)], probs[:, 4 * P:4 * HP], ident[:, :]).then_inc(probsT_ready, 1)

        def attend(g, q, i):
            n = QUADS * g + q
            if i == 0:
                pe.wait_ge(probsT_lo, UNITS * g + TILES * (q + 1))
                pe.wait_ge(last_lo, n + 1)
                pe.wait_ge(values_loaded[q], 16 * (g // GPB + 1))
            if not (isinstance(n, int) and n == 0):
                pe.wait_ge(proj_added, TILES * (n - 1) + 3 + i)
            parts = ((VP * i, 2 * i), (VP * i + DH, 2 * i + 1), (2 * VP + P * i, 4))
            for m, (col, chunk) in enumerate(parts):
                ins = split_matmul(pe, psum[:, ATTEND_BANK[i], :], lambda s: values[:, q, s, col:col + P],
                                   lambda s: probsT[:, s, chunk, :], m == 0, m == 2)
            ins.then_inc(attn_ready, 1)

        def project(g, q, t, more_queries):
            n = QUADS * g + q
            if t == 0:
                pe.wait_ge(attn_lo, 2 * n + 2)
            elif t == 2 and more_queries:
                pe.wait_ge(query_lo, 2 * (n + 2) + 2)
            elif t != 2:
                pe.wait_ge(proj_added, TILES * n + (1 if t == 1 else 2))
            for i in range(2):
                ins = split_matmul(pe, psum[:, PROJECT_BANK[t], :], lambda s: attnT[:, s, i, P * t:P * (t + 1)],
                                   lambda s: wo[:, s, 2 * q + i, :], i == 0, i == 1)
            ins.then_inc(proj_ready, 1)

        def transposes_norm2(g, t):
            pe.wait_ge(norm2_done, TILES * g + t + 1)
            for c in range(KC):
                ins = pe.transpose(psum[:, TRANSPOSED, P * c:P * (c + 1)], xn2[:, t % 2, P * c:P * (c + 1)], ident[:, :])
            ins.then_inc(norm2T_ready, 1)

        def route(g, half):
            pe.wait_ge(norm2T_copied, TILES * g + 2 * half + 2)
            if half:
                pe.wait_ge(logits_copied, 2 * g + 1)
            for t in range(2):
                for c in range(KC):
                    ins = pe.matmul(logits_ps[:, t, :], xn2T[:, t, P * c:P * (c + 1)], wr[:, c, :],
                                    start=c == 0, stop=c == KC - 1)
            ins.then_inc(logits_ready, 1)

        def places(g):
            pe.wait_ge(chosen_ready, g + 1)
            for t in range(TILES):
                pe.matmul(place_ps[:, t, :], upto[:, :], chosen[:, t, :], start=True, stop=False)
                for s in range(t):
                    pe.matmul(place_ps[:, t, :], ones[:, :], chosen[:, s, :], start=False, stop=False)
                ins = pe.matmul(place_ps[:, t, :], ones[:, :], before[:, :], start=False, stop=True)
            ins.then_inc(places_ready, 1)

        def group(g, prev, cur, nxt):
            aux = None

            def routing(u):
                nonlocal aux
                what, n = ROUTING.get(u, (None, None)) if prev else (None, None)
                if what in ("norm", "places"):
                    if aux:
                        pe.wait_ge(*aux)
                    else:
                        pe.wait_ge(probsT_lo, UNITS * g + (u if cur else 0))
                if what == "norm":
                    transposes_norm2(g - 1, n)
                    aux = norm2T_copied, TILES * (g - 1) + n + 1
                elif what == "places":
                    places(g - 1)
                    aux = places_read, g

            def probabilities(u):
                nonlocal aux
                if cur:
                    transposes_probs(g, u, aux)
                    aux = None

            for u in range(UNITS):
                q, t = u // TILES, u % TILES
                q1, g1, do1 = (q - 1, g, cur) if q else (QUADS - 1, g - 1, prev)
                n1 = QUADS * g1 + q1
                u2, g2, do2 = (u + 2, g, cur) if u + 2 < UNITS else (u + 2 - UNITS, g + 1, nxt)
                q3, g3, do3 = (q + 1, g, cur) if q + 1 < QUADS else (0, g + 1, nxt)
                if t == 0:
                    if do2:
                        scores(g2, u2)
                    probabilities(u)
                    if u == 12 and nxt:
                        pe.wait_ge(proj_added, TILES * (n1 - 1) + 4)
                        transposes_x(g + 1, 3)
                        pe.wait_ge(xT_lo, KC * (g + 1) + 3)
                    if do1:
                        attend(g1, q1, 0)
                        if u == 12 and nxt:
                            pe.wait_ge(xT_lo, KC * (g + 2))
                        attend(g1, q1, 1)
                elif t == 1:
                    if do3:
                        queries(g3, q3, 0)
                    routing(u)
                    if do2:
                        scores(g2, u2)
                    probabilities(u)
                    if do1:
                        project(g1, q1, 0, do3)
                elif t == 2:
                    routing(u)
                    if do3:
                        queries(g3, q3, 1)
                    probabilities(u)
                    if do1:
                        project(g1, q1, 1, do3)
                    if u == 10 and nxt:
                        pe.wait_ge(query_lo, 2 * (n1 + 2) + 2)
                        transposes_x(g + 1, 0)
                    if do2:
                        scores(g2, u2)
                else:
                    probabilities(u)
                    if prev and u in ROUTING:
                        if do1:
                            pe.wait_ge(proj_added, TILES * n1 + 2)
                        route(g - 1, ROUTING[u][1])
                    if do1:
                        if u == 11 and nxt:
                            pe.wait_ge(xT_lo, KC * (g + 1) + 1)
                        project(g1, q1, 2, do3)
                    if do2:
                        scores(g2, u2)
                    if u == 11 and nxt:
                        pe.wait_ge(probsT_lo, UNITS * g + u + 1)
                        transposes_x(g + 1, 1)
                        aux = xT_lo, KC * (g + 1) + 2
                    if do1:
                        if prev and u in ROUTING:
                            pe.wait_ge(logits_copied, 2 * (g - 1) + ROUTING[u][1] + 1)
                        project(g1, q1, 3, do3)
                    if u == 11 and nxt:
                        pe.wait_ge(proj_added, TILES * n1 + 3)
                        transposes_x(g + 1, 2)

        for c in range(KC):
            if c == 2:
                pe.wait_ge(xT_lo, 1)
            transposes_x(0, c)
        for i in range(2):
            queries(0, 0, i)
        scores(0, 0)
        scores(0, 1)
        over_groups(pe, group)

    @block.scalar
    def _(act):
        def hi(dst, bank, ready, done, n, scale=1.0):
            act.wait_ge(ready, n + 1)
            act.activation(dst, psum[:, bank, :], ACT.Copy, scale=scale).then_inc(done, 1)

        def x_hi(g, c):
            hi(xT[:, HI, c, :], X_BANK[c], xT_ready, xT_hi, KC * g + c)

        def query_part(g, q, i):
            hi(qT[:, q % 2, HI, i, :], QUERY_BANK, query_ready, query_hi, 2 * (QUADS * g + q) + i, SCALE)

        def attn_part(g, q, i):
            hi(attnT[:, HI, i, :], ATTEND_BANK[i], attn_ready, attn_hi, 2 * (QUADS * g + q) + i)

        def exp(g, u):
            act.wait_ge(max_ready, UNITS * g + u + 1)
            if not (isinstance(g, int) and g == 0 and u < 2):
                act.wait_ge(probs_ready, UNITS * g + u - 1)
            for h in range(4):
                ins = act.activation(exp_scores[:, u % 2, h, :],
                                     psum[:, 2 * (u % 2) + h // 2, M * (h % 2):M * (h % 2 + 1)], ACT.Exp,
                                     bias=neg_max[:, u % 2, h:h + 1], accum_out=sums[:, u % 2, h:h + 1])
            ins.then_inc(exp_done, 1)

        def probs_hi(g, u):
            t = u % TILES
            act.wait_ge(probsT_ready, UNITS * g + u + 1)
            if t == 0 and not (isinstance(g, int) and g == 0 and u == 0):
                act.wait_ge(attn_ready, 2 * (QUADS * g + u // TILES))
            act.activation(probsT[:, HI, 0:4, P * t:P * (t + 1)],
                           psum[:, TRANSPOSED, :].rearrange("p (h n) -> p h n", h=4), ACT.Copy).then_inc(probsT_hi, 1)

        def last_part(g, q):
            act.wait_ge(probsT_ready, UNITS * g + TILES * (q + 1))
            act.activation(probsT[:, HI, 4, :].rearrange("p (t n) -> p t n", t=TILES),
                           psum[:, LAST, :].rearrange("p (t n) -> p t n", t=TILES), ACT.Copy).then_inc(last_hi, 1)

        def group(g, prev, cur, nxt):
            def routing(u):
                what, n = ROUTING.get(u, (None, None)) if prev else (None, None)
                if what == "norm":
                    act.wait_ge(norm2T_ready, TILES * (g - 1) + n + 1)
                    act.activation(xn2T[:, n % 2, :], psum[:, TRANSPOSED, :], ACT.Copy).then_inc(norm2T_copied, 1)

            for u in range(UNITS):
                q, t = u // TILES, u % TILES
                q1, g1, do1 = (q - 1, g, cur) if q else (QUADS - 1, g - 1, prev)
                u2, g2, do2 = (u + 2, g, cur) if u + 2 < UNITS else (u + 2 - UNITS, g + 1, nxt)
                q3, g3, do3 = (q + 1, g, cur) if q + 1 < QUADS else (0, g + 1, nxt)
                if t == 0:
                    if u == 12 and nxt:
                        x_hi(g + 1, 3)
                    if do2:
                        exp(g2, u2)
                    if do1:
                        attn_part(g1, q1, 0)
                        attn_part(g1, q1, 1)
                    if cur:
                        probs_hi(g, u)
                elif t == 1:
                    if do3:
                        query_part(g3, q3, 0)
                    routing(u)
                    if cur:
                        probs_hi(g, u)
                    if do2:
                        exp(g2, u2)
                elif t == 2:
                    routing(u)
                    if do3:
                        query_part(g3, q3, 1)
                    if cur:
                        probs_hi(g, u)
                    if u == 10 and nxt:
                        x_hi(g + 1, 0)
                else:
                    if cur:
                        probs_hi(g, u)
                    if nxt or (cur and u < UNITS - 1):
                        exp(*before_last)
                    if cur:
                        last_part(g, q)
                    if u == 11 and nxt:
                        x_hi(g + 1, 1)
                    if do2:
                        exp(g2, u2)
                    if u == 11 and nxt:
                        x_hi(g + 1, 2)
                before_last = g2, u2
                if prev and u == 12:
                    act.wait_ge(shifted_ready, g)
                    act.activation(exps[:, :, :], shifted[:, :, :], ACT.Exp).then_inc(exps_ready, 1)

        for c in range(KC):
            x_hi(0, c)
        for i in range(2):
            query_part(0, 0, i)
        exp(0, 0)
        exp(0, 1)
        over_groups(act, group)

    @block.vector
    def _(dve):
        def lo(which, bank, hi_done, done, n, scale=None):
            dve.wait_ge(hi_done, n + 1)
            if scale is None:
                ins = dve.tensor_tensor(which(LO), psum[:, bank, :], which(HI).bitcast(F32), ALU.subtract)
            else:
                ins = dve.scalar_tensor_tensor(out=which(LO), in0=psum[:, bank, :], scalar=scale,
                                               in1=which(HI).bitcast(F32), op0=ALU.mult, op1=ALU.subtract)
            ins.then_inc(done, 1)

        def x_lo(g, c):
            lo(lambda s: xT[:, s, c, :], X_BANK[c], xT_hi, xT_lo, KC * g + c)

        def query_part(g, q, i):
            lo(lambda s: qT[:, q % 2, s, i, :], QUERY_BANK, query_hi, query_lo, 2 * (QUADS * g + q) + i, SCALE)

        def attn_part(g, q, i):
            lo(lambda s: attnT[:, s, i, :], ATTEND_BANK[i], attn_hi, attn_lo, 2 * (QUADS * g + q) + i)

        def row_max(g, u):
            dve.wait_ge(scores_ready, UNITS * g + u + 1)
            src = psum[:, 2 * (u % 2):2 * (u % 2) + 2, 0:PAIR].rearrange("p i (h m) -> p i h m", h=2)
            dve.tensor_reduce(neg_max[:, u % 2, :].rearrange("p (i h) -> p i h", i=2), src, AX.X, ALU.max,
                              negate=True).then_inc(max_ready, 1)

        def invert(g, u):
            dve.wait_ge(exp_done, UNITS * g + u + 1)
            dve.reciprocal(inv_sums[:, u % 2, :], sums[:, u % 2, :]).then_inc(sums_inverted, 1)

        def probs_lo(g, u):
            t = u % TILES
            dve.wait_ge(probsT_hi, UNITS * g + u + 1)
            dve.tensor_tensor(probsT[:, LO, 0:4, P * t:P * (t + 1)],
                              psum[:, TRANSPOSED, :].rearrange("p (h n) -> p h n", h=4),
                              probsT[:, HI, 0:4, P * t:P * (t + 1)].bitcast(F32), ALU.subtract).then_inc(probsT_lo, 1)

        def last_part(g, q):
            dve.wait_ge(last_hi, QUADS * g + q + 1)
            dve.tensor_tensor(probsT[:, LO, 4, :].rearrange("p (t n) -> p t n", t=TILES), psum[:, LAST, :].rearrange("p (t n) -> p t n", t=TILES),
                              probsT[:, HI, 4, :].bitcast(F32).rearrange("p (t n) -> p t n", t=TILES),
                              ALU.subtract).then_inc(last_lo, 1)

        def add_projection(g, q, t):
            dve.wait_ge(proj_ready, TILES * (QUADS * g + q) + t + 1)
            if q == 0:
                dve.wait_ge(partial_biased, TILES * g + t + 1)
            last = q == QUADS - 1
            if last and t == 0 and not (isinstance(g, int) and g == 0):
                dve.wait_ge(x1_stored, 32 * g)
            ins = dve.scalar_tensor_tensor(out=(x1 if last else partial)[:, t, :], in0=psum[:, PROJECT_BANK[t], :],
                                           scalar=tanh_g[:, 0:1], in1=partial[:, t, :], op0=ALU.mult, op1=ALU.add)
            ins.then_inc(proj_added, 1)

        def normalise(which, g, t):
            dve.wait_ge((norm1_rstd, norm2_rstd)[which], g + 1)
            if which == 1 and t >= 2:
                dve.wait_ge(norm2T_ready, TILES * g + t - 1)
            dst, src = ((x_in[:, t, :], x_in[:, t, :]), (xn2[:, t % 2, :], x1[:, t, :]))[which]
            dve.tensor_scalar(dst, src, mean_var[:, which, t, 0:1], rstd[:, which, t:t + 1],
                              ALU.subtract, ALU.mult).then_inc((norm1_done, norm2_done)[which], 1)

        def group(g, prev, cur, nxt):
            stat_n = STATS_OF(g)

            def step_stat(ins):
                nonlocal stat_n
                ins.then_inc(stat_step, 1)
                stat_n = stat_n + 1

            def tile_stats(which, t):
                src = (x_in, x1)[which]
                if which == 0 and t == 0:
                    dve.wait_ge(x_loaded, 16 * (g + 2))
                if which == 1:
                    dve.wait_ge(proj_added, TILES * (QUADS * g - 1) + t + 1)
                    alone(dve, dve_waits_met)
                step_stat(dve.bn_stats(stats[:, t, :], src[:, t, :]))

            def norm_stats(which):
                dve.wait_ge(stat_step, stat_n)
                alone(dve, dve_waits_met)
                for t in range(TILES):
                    step_stat(dve.bn_aggr(mean_var[:, which, t, :], stats[:, t, :]))
                dve.wait_ge(stat_step, stat_n)
                dve.tensor_scalar(var_eps[:, which, :], mean_var[:, which, :, 1], EPS, None, ALU.add)\
                   .then_inc((norm1_stats, norm2_stats)[which], 1)

            def routing(u):
                what, n = ROUTING.get(u, (None, None)) if prev else (None, None)
                if what == "logits":
                    dve.wait_ge(logits_ready, 2 * (g - 1) + n + 1)
                    dve.tensor_copy(logits[:, 2 * n:2 * n + 2, :], logits_ps).then_inc(logits_copied, 1)
                elif what == "places":
                    dve.wait_ge(places_ready, g)
                    dve.tensor_tensor(placed[:, :, :], place_ps, chosen[:, :, :], ALU.mult).then_inc(places_read, 1)

            for u in range(UNITS):
                q, t = u // TILES, u % TILES
                q1, g1, do1 = (q - 1, g, cur) if q else (QUADS - 1, g - 1, prev)
                u2, g2, do2 = (u + 2, g, cur) if u + 2 < UNITS else (u + 2 - UNITS, g + 1, nxt)
                q3, g3, do3 = (q + 1, g, cur) if q + 1 < QUADS else (0, g + 1, nxt)
                if t == 0:
                    if do2:
                        row_max(g2, u2)
                    if u == 12 and nxt:
                        x_lo(g + 1, 3)
                    if prev and u == 12:
                        choose(g - 1)
                    if prev and u == 4:
                        tile_stats(1, 3)
                        norm_stats(1)
                    if nxt and u == 8:
                        tile_stats(0, 3)
                    if do1:
                        attn_part(g1, q1, 0)
                    if do2:
                        invert(g2, u2)
                    if do1:
                        attn_part(g1, q1, 1)
                    if cur:
                        probs_lo(g, u)
                    if prev and u == 4:
                        normalise(1, g - 1, 0)
                        normalise(1, g - 1, 1)
                    if nxt and u == 8:
                        norm_stats(0)
                elif t == 1:
                    if u == 13:
                        routing(u)
                    if do3:
                        query_part(g3, q3, 0)
                    if do2:
                        row_max(g2, u2)
                    if cur:
                        probs_lo(g, u)
                    if do1:
                        add_projection(g1, q1, 0)
                    if do2:
                        invert(g2, u2)
                    if prev and u == 1:
                        tile_stats(1, 0)
                    if prev and u == 5:
                        normalise(1, g - 1, 2)
                    if nxt and u == 5:
                        tile_stats(0, 0)
                        tile_stats(0, 1)
                    if nxt and u == 9:
                        for s in range(TILES):
                            normalise(0, g + 1, s)
                    if prev and u == 13:
                        assign(g - 1)
                elif t == 2:
                    if do3:
                        query_part(g3, q3, 1)
                    if cur:
                        probs_lo(g, u)
                    if do1:
                        add_projection(g1, q1, 1)
                    if u == 10 and nxt:
                        x_lo(g + 1, 0)
                    if do2:
                        row_max(g2, u2)
                    if prev and u == 2:
                        tile_stats(1, 1)
                    if prev and u == 6:
                        normalise(1, g - 1, 3)
                    if nxt and u == 6:
                        tile_stats(0, 2)
                    if prev and u == 14:
                        enter(g - 1)
                else:
                    if cur:
                        probs_lo(g, u)
                    if nxt or (cur and u < UNITS - 1):
                        invert(*before_last)
                    routing(u)
                    if do1:
                        add_projection(g1, q1, 2)
                    if do2:
                        row_max(g2, u2)
                    if u == 11 and nxt:
                        x_lo(g + 1, 1)
                    if cur:
                        last_part(g, q)
                    if prev and u == 3:
                        tile_stats(1, 2)
                    if do1:
                        add_projection(g1, q1, 3)
                    if do2:
                        invert(g2, u2)
                    if u == 11 and nxt:
                        x_lo(g + 1, 2)
                before_last = g2, u2

        def step(g, n, ins):
            ins.then_inc(route_step, 1)
            dve.wait_ge(route_step, ROUTE * g + n + 1)

        def each(t):
            return t[:, :].unsqueeze(2).to_broadcast([P, TILES, E])

        def choose(g):
            dve.wait_ge(logits_copied, 2 * (g + 1))
            step(g, 0, dve.tensor_reduce(top[:, :], logits[:, :, :], AX.X, ALU.max))
            dve.tensor_tensor(shifted[:, :, :], logits[:, :, :], each(top), ALU.subtract).then_inc(shifted_ready, 1)
            step(g, 1, dve.tensor_tensor(marked[:, :, :], logits[:, :, :], each(top), ALU.is_equal))
            step(g, 2, dve.tensor_tensor(marked[:, :, :], marked[:, :, :],
                                         weight8[:, :].unsqueeze(1).to_broadcast([P, TILES, E]), ALU.mult))
            step(g, 3, dve.tensor_reduce(first8[:, :], marked[:, :, :], AX.X, ALU.max))
            dve.tensor_tensor(chosen[:, :, :], marked[:, :, :], each(first8), ALU.is_equal).then_inc(chosen_ready, 1)

        def assign(g):
            dve.wait_ge(places_read, g + 1)
            step(g, 4, dve.tensor_reduce(place[:, :], placed[:, :, :], AX.X, ALU.add))
            step(g, 5, dve.tensor_reduce(chosen_sum[:, :], chosen[:, :, :].rearrange("p t e -> p e t"), AX.X, ALU.add))
            step(g, 6, dve.tensor_tensor(before[:, :], before[:, :], chosen_sum[:, :], ALU.add))
            step(g, 7, dve.tensor_scalar(over[:, :], place[:, :], float(CAP), float(2 * T), ALU.is_gt, ALU.mult))
            step(g, 8, dve.scalar_tensor_tensor(out=slot[:, :], in0=first8[:, :], scalar=-float(CAP), in1=place[:, :],
                                                 op0=ALU.mult, op1=ALU.add))
            if not (isinstance(g, int) and g == 0):
                dve.wait_ge(slots_stored, 16 * TILES * g)
            step(g, 9, dve.scalar_tensor_tensor(out=slot[:, :], in0=slot[:, :], scalar=float(T - 1), in1=over[:, :],
                                                 op0=ALU.add, op1=ALU.add))

        def enter(g):
            dve.wait_ge(exps_ready, g + 1)
            step(g, 10, dve.tensor_reduce(denom[:, :], exps[:, :, :], AX.X, ALU.add))
            step(g, 11, dve.reciprocal(gate[:, :], denom[:, :]))
            dve.tensor_copy(slot_index[:, :], slot[:, :]).then_inc(entry_ready, 1)
            dve.tensor_scalar(entry[:, :, 1].bitcast(F32), gate[:, :], tanh_g[:, 1:2], None, ALU.mult).then_inc(entry_ready, 1)
            step(g, 12, dve.tensor_copy(entry[:, :, 0], token[:, :]))
            step(g, 13, dve.tensor_scalar(token[:, :], token[:, :], float(GN), None, ALU.add))

        def STATS_OF(g):
            if isinstance(g, int) and g == 0:
                return 2 * TILES
            return 4 * TILES * g - (2 * TILES if isinstance(g, int) and g == NG else 0)

        dve.memset(probs[:, :], 0.0).then_inc(probs_zeroed, 1)
        dve.memset(before[:, :], 0.0).then_inc(probs_zeroed, 1)
        dve.wait_ge(x_loaded, 16)
        for t in range(TILES):
            dve.bn_stats(stats[:, t, :], x_in[:, t, :]).then_inc(stat_step, 1)
            dve.wait_ge(stat_step, 2 * t + 1)
            dve.bn_aggr(mean_var[:, 0, t, :], stats[:, t, :]).then_inc(stat_step, 1)
        dve.wait_ge(stat_step, 2 * TILES)
        dve.tensor_scalar(var_eps[:, 0, :], mean_var[:, 0, :, 1], EPS, None, ALU.add).then_inc(norm1_stats, 1)
        for t in range(TILES):
            normalise(0, 0, t)
        for c in range(KC):
            x_lo(0, c)
        for i in range(2):
            query_part(0, 0, i)
        row_max(0, 0)
        row_max(0, 1)
        invert(0, 0)
        invert(0, 1)
        over_groups(dve, group)

    @block.gpsimd
    def _(pool):
        def normalise(g, u):
            pool.wait_ge(sums_inverted, UNITS * g + u + 1)
            if not (isinstance(g, int) and g == 0 and u < 1):
                pool.wait_ge(probsT_ready, UNITS * g + u)
            for cols, first, n, wide in ((slice(0, 4 * P), 0, P, P), (slice(4 * P, 4 * HP), P, M - P, HP - P)):
                ins = pool.tensor_tensor(probs[:, cols].rearrange("p (h n) -> p h n", n=wide)[:, :, 0:n],
                                         exp_scores[:, u % 2, :, first:first + n],
                                         inv_sums[:, u % 2, :].unsqueeze(2).to_broadcast([P, 4, n]), ALU.mult)
            ins.then_inc(probs_ready, 1)

        def root(which, g):
            pool.wait_ge((norm1_stats, norm2_stats)[which], g + 1)
            pool.tensor_tensor(rstd[:, which, :], var_eps[:, which, :], half_neg[:, :], ALU.pow)\
                .then_inc((norm1_rstd, norm2_rstd)[which], 1)

        def add_bias(g, t):
            pool.wait_ge(partial_loaded[t], 16 * (g + 1))
            pool.tensor_tensor(partial[:, t, :], partial[:, t, :], bias[:, :], ALU.add).then_inc(partial_biased, 1)

        def group(g, prev, cur, nxt):
            for u in range(UNITS):
                u2, g2, do2 = (u + 1, g, cur) if u + 1 < UNITS else (0, g + 1, nxt)
                if nxt and u == 9:
                    root(0, g + 1)
                if do2:
                    normalise(g2, u2)
                if cur and u in (3, 5, 6):
                    for t in {3: (0,), 5: (1, 2), 6: (3,)}[u]:
                        add_bias(g, t)
                if prev and u == 4:
                    root(1, g - 1)
                if prev and u == 15:
                    pool.wait_ge(entry_ready, 2 * g)
                    pool.wait_ge(route_step, ROUTE * g)
                    alone(pool, pool_waits_met)
                    for t in range(TILES):
                        pool.indirect_dma_start(out=slots_dram[:, :], out_offset=bass.IndirectOffsetOnAxis(
                            ap=slot_index[:, t:t + 1], axis=0), in_=entry[:, t, :], in_offset=None,
                            bounds_check=T - 1, oob_is_err=False).then_inc(slots_stored, 16)

        pool.wait_ge(probs_zeroed, 2)
        root(0, 0)
        normalise(0, 0)
        over_groups(pool, group)
        pool.wait_ge(slots_stored, 16 * TILES * NG)


def ffn_block(nc, stack, sb, env):
    psum, ident, half_neg = env["psum"], env["ident"], env["half_neg"]
    (KC, D, E, F, T, CAP) = [env[k] for k in ("KC", "D", "E", "F", "T", "CAP")]
    w1, w2, x1_dram, slots_dram, out_rows = [env[k] for k in ("w1", "w2", "x1_dram", "slots_dram", "out_rows")]
    FC = F // P
    PAIRS = FC // 2
    PW = 2 * P
    HALVES = CAP // GN
    SLOTS = CAP // P
    assert HALVES == 2

    wh1 = sb(stack, "wh1", [P, 2, KC, F], F32R)
    wh2 = sb(stack, "wh2", [P, 2, FC, D], F32R)
    raw1 = sb(stack, "w1_raw", [P, 2, KC, PW], F32)
    raw2 = sb(stack, "w2_raw", [P, 2, 2, D], F32)
    slots = sb(stack, "slots", [P, E, SLOTS, 2], U32)
    index = sb(stack, "index", [P, HALVES, TILES], U32)
    coef = sb(stack, "coef", [P, HALVES, TILES], U32)
    rows = sb(stack, "rows", [P, HALVES, TILES, D], F32)
    normed = sb(stack, "normed", [P, TILES, D], F32)
    sT = sb(stack, "sT", [P, 2, KC, GN], F32R)
    hidden = sb(stack, "hidden", [P, 2, GN], F32)
    hT = sb(stack, "hT", [P, 2, 2, GN], F32R)
    stats2 = sb(stack, "stats2", [P, TILES, 6], F32)
    mean_var2 = sb(stack, "mean_var2", [P, TILES, 2], F32)
    var_eps2 = sb(stack, "var_eps2", [P, TILES], F32)
    rstd2 = sb(stack, "rstd2", [P, TILES], F32)

    sem = lambda name: stack.enter_context(nc.semaphore(name))
    slots_loaded = sem("slots_loaded")
    raw_loaded = [sem("w_raw_loaded0"), sem("w_raw_loaded1")]
    w_hi, w_lo = sem("w_hi"), sem("w_lo")
    index_ready = sem("index_ready")
    gathered = [sem("gathered0"), sem("gathered1")]
    scattered = [sem("scattered0"), sem("scattered1")]
    slot_step = sem("slot_step")
    s_stats, s_rstd, s_normed = sem("s_stats"), sem("s_rstd"), sem("s_normed")
    sT_ready, sT_hi, sT_lo = sem("sT_ready"), sem("sT_hi"), sem("sT_lo")
    hid_ready, gelu_done, hT_hi, hT_lo, hT_used = sem("hid_ready"), sem("gelu_done"), sem("hT_hi"), sem("hT_lo"), sem("hT_used")
    y_done = sem("y_done")
    dve_waits_met, pool_waits_met = sem("dve_waits_met2"), sem("pool_waits_met2")

    def over_experts(engine, body):
        body(0, True, True)
        with engine.Fori(1, E - 1) as e:
            body(e, False, True)
        body(E - 1, False, False)

    def weight_pairs(first, nxt, half, f):
        if half == 0 and f % 2 == 0:
            if first and f // 2 + 2 < PAIRS:
                return [(0, f // 2 + 2)]
            if not first and f == 0:
                return [(0, PAIRS - 1)]
        if half == 1 and nxt and f % 2 == 0 and f >= 2:
            return [(1, f // 2 - 1)]
        return []

    block = stack.enter_context(nc.Block())

    @block.sync
    def _(sp):
        sp.dma_start(slots[:, :, :, :].rearrange("p e k c -> p e (k c)"),
                     slots_dram.rearrange("(e p k) c -> p e (k c)", e=E, p=P)).then_inc(slots_loaded, 16)
        w1_v = w1.rearrange("e (c p) f -> p e c f", p=P)
        w2_v = w2.rearrange("e (f p) d -> p e f d", p=P)

        def load_pair(e, j2, s):
            sp.dma_start(raw1[:, s, :, :], w1_v[:, bass.ds(e, 1), :, bass.ds(j2 * 2 * PW + s * PW, PW)].rearrange(
                "p e c f -> p (e c) f")).then_inc(raw_loaded[s], 16)
            sp.dma_start(raw2[:, s, :, :], w2_v[:, bass.ds(e, 1), bass.ds(j2 * 4 + s * 2, 2), :].rearrange(
                "p e f d -> p (e f) d")).then_inc(raw_loaded[s], 16)

        load_pair(0, 0, 0)
        load_pair(0, 0, 1)
        for j2 in range(1, PAIRS // 2):
            for s in range(2):
                sp.wait_ge(w_lo, 2 * j2 + s - 1)
                load_pair(0, j2, s)
        with sp.Fori(1, E) as e:
            with sp.Fori(0, PAIRS // 2) as j2:
                for s in range(2):
                    sp.wait_ge(w_lo, PAIRS * e + 2 * j2 + s - 1)
                    load_pair(e, j2, s)

    @block.tensor
    def _(pe):
        def transposes(G, t):
            pe.wait_ge(s_normed, TILES * G + t + 1)
            if not (isinstance(G, int) and G == 0 and t < 2):
                pe.wait_ge(sT_lo, TILES * G + t - 1)
            for c in range(KC):
                ins = pe.transpose(psum[:, 6 + t % 2, P * c:P * (c + 1)], normed[:, t, P * c:P * (c + 1)], ident[:, :])
            ins.then_inc(sT_ready, 1)

        def up(e, half, f):
            if f == 0:
                pe.wait_ge(sT_lo, TILES * (2 * e + half + 1))
            if half == 0 and f % 2 == 0:
                pe.wait_ge(w_lo, PAIRS * e + f // 2 + 1)
            n = FC * (2 * e + half) + f
            if not (isinstance(n, int) and n < 2):
                pe.wait_ge(gelu_done, n - 1)
            for c in range(KC):
                ins = split_matmul(pe, psum[:, 4 + f % 2, :], lambda s: wh1[:, s, c, P * f:P * (f + 1)],
                                   lambda s: sT[:, s, c, :], c == 0, c == KC - 1)
            ins.then_inc(hid_ready, 1)

        def down(e, half, f, tiles):
            G = 2 * e + half
            for t in tiles:
                if f == 0 and not (isinstance(G, int) and G == 0):
                    pe.wait_ge(y_done, TILES * (G - 1) + t + 1)
                if t == 0:
                    pe.wait_ge(hT_lo, FC * G + f + 1)
                ins = split_matmul(pe, psum[:, t, :], lambda s: hT[:, f % 2, s, P * t:P * (t + 1)],
                                   lambda s: wh2[:, s, f, :], f == 0, f == FC - 1)
            if tiles[-1] == TILES - 1:
                ins.then_inc(hT_used, 1)

        def expert(e, first, nxt):
            for half in range(HALVES):
                more = half == 0 or nxt
                e2, half2 = (e, 1) if half == 0 else (e + 1, 0)
                for f in range(FC - 2):
                    if f > 0:
                        up(e, half, f + 1)
                    down(e, half, f, range(TILES))
                if more:
                    transposes(2 * e2 + half2, 0)
                    transposes(2 * e2 + half2, 1)
                up(e, half, FC - 1)
                down(e, half, FC - 2, range(TILES))
                if more:
                    transposes(2 * e2 + half2, 2)
                    down(e, half, FC - 1, (0,))
                    transposes(2 * e2 + half2, 3)
                    down(e, half, FC - 1, range(1, TILES))
                    up(e2, half2, 0)
                    up(e2, half2, 1)
                else:
                    down(e, half, FC - 1, range(TILES))

        for t in range(TILES):
            transposes(0, t)
        up(0, 0, 0)
        up(0, 0, 1)
        over_experts(pe, expert)

    @block.scalar
    def _(act):
        def rows_hi(G, t):
            act.wait_ge(sT_ready, TILES * G + t + 1)
            act.activation(sT[:, HI, :, P * t:P * (t + 1)], psum[:, 6 + t % 2, :].rearrange("p (c n) -> p c n", c=KC),
                           ACT.Copy).then_inc(sT_hi, 1)

        def gelu(G, f):
            n = FC * G + f
            act.wait_ge(hid_ready, n + 1)
            if not (isinstance(n, int) and n < 2):
                act.wait_ge(hT_lo, n - 1)
                act.wait_ge(hT_used, n - 1)
            act.activation(hidden[:, f % 2, :], psum[:, 4 + f % 2, :], ACT.Gelu_apprx_tanh).then_inc(gelu_done, 1)
            act.wait_ge(gelu_done, n + 1)
            act.activation(hT[:, f % 2, HI, :], hidden[:, f % 2, :], ACT.Copy).then_inc(hT_hi, 1)

        def expert(e, first, nxt):
            for half in range(HALVES):
                more = half == 0 or nxt
                G = 2 * e + half
                for f in range(FC):
                    if f + 1 < FC:
                        gelu(G, f + 1)
                    elif more:
                        gelu(G + 1, 0)
                    if f == FC - 2 and more:
                        for t in range(TILES):
                            rows_hi(G + 1, t)

        for t in range(TILES):
            rows_hi(0, t)
        gelu(0, 0)
        over_experts(act, expert)

    @block.vector
    def _(dve):
        def split_hi(e, j):
            dve.wait_ge(raw_loaded[j % 2], 32 * (PAIRS // 2 * e + j // 2 + 1))
            if not (isinstance(e, int) and e == 0):
                dve.wait_ge(hT_used, FC * (2 * e - 1) + 2 * j + 2)
            dve.tensor_copy(wh1[:, HI, :, PW * j:PW * (j + 1)], raw1[:, j % 2, :, :]).then_inc(w_hi, 1)
            dve.tensor_copy(wh2[:, HI, 2 * j:2 * j + 2, :], raw2[:, j % 2, :, :]).then_inc(w_hi, 1)

        def fetch(e, half):
            G = 2 * e + half
            if not (isinstance(G, int) and G < 2):
                dve.wait_ge(scattered[half], 16 * TILES * e)
            src = slots[:, bass.ds(e, 1), TILES * half:TILES * (half + 1), :].rearrange("p e k c -> p (e k) c")
            dve.tensor_copy(index[:, half, :], src[:, :, 0]).then_inc(index_ready, 1)
            dve.tensor_copy(coef[:, half, :], src[:, :, 1]).then_inc(index_ready, 1)

        def step(G, n, ins):
            ins.then_inc(slot_step, 1)
            dve.wait_ge(slot_step, 2 * TILES * G + n + 1)
            alone(dve, dve_waits_met)

        def statistics(G, half, t):
            if t == 0:
                dve.wait_ge(gathered[half], 16 * TILES * (G // 2 + 1))
            step(G, 2 * t, dve.bn_stats(stats2[:, t, :], rows[:, half, t, :]))
            step(G, 2 * t + 1, dve.bn_aggr(mean_var2[:, t, :], stats2[:, t, :]))
            if t == TILES - 1:
                dve.tensor_scalar(var_eps2[:, :], mean_var2[:, :, 1], EPS, None, ALU.add).then_inc(s_stats, 1)

        def normalise(G, half, t):
            dve.wait_ge(s_rstd, G + 1)
            if not (isinstance(G, int) and G == 0):
                dve.wait_ge(sT_ready, TILES * G)
            dve.tensor_scalar(normed[:, t, :], rows[:, half, t, :], mean_var2[:, t, 0:1], rstd2[:, t:t + 1],
                              ALU.subtract, ALU.mult).then_inc(s_normed, 1)

        def rows_lo(G, t):
            dve.wait_ge(sT_hi, TILES * G + t + 1)
            dve.tensor_tensor(sT[:, LO, :, P * t:P * (t + 1)], psum[:, 6 + t % 2, :].rearrange("p (c n) -> p c n", c=KC),
                              sT[:, HI, :, P * t:P * (t + 1)].bitcast(F32), ALU.subtract).then_inc(sT_lo, 1)

        def hidden_lo(G, f):
            dve.wait_ge(hT_hi, FC * G + f + 1)
            dve.tensor_tensor(hT[:, f % 2, LO, :], hidden[:, f % 2, :], hT[:, f % 2, HI, :].bitcast(F32),
                              ALU.subtract).then_inc(hT_lo, 1)

        def outputs(G, half):
            dve.wait_ge(hT_used, FC * (G + 1))
            for t in range(TILES):
                dve.scalar_tensor_tensor(out=rows[:, half, t, :], in0=psum[:, t, :],
                                         scalar=coef[:, half, t:t + 1].bitcast(F32), in1=rows[:, half, t, :],
                                         op0=ALU.mult, op1=ALU.add).then_inc(y_done, 1)

        def expert(e, first, nxt):
            for half in range(HALVES):
                more = half == 0 or nxt
                G = 2 * e + half
                e2, half2 = (e, 1) if half == 0 else (e + 1, 0)
                for f in range(FC):
                    if f + 1 < FC:
                        hidden_lo(G, f + 1)
                    else:
                        outputs(G, half)
                        if more:
                            hidden_lo(G + 1, 0)
                    if f == 4 and more:
                        fetch(e2, half2)
                    if 8 <= f < 8 + TILES and more:
                        statistics(G + 1, half2, f - 8)
                    if f in (12, 13) and more:
                        normalise(G + 1, half2, 2 * (f - 12))
                        normalise(G + 1, half2, 2 * (f - 12) + 1)
                    for ahead, j in weight_pairs(first, nxt, half, f):
                        split_hi(e + ahead, j)
                    if f == FC - 2 and more:
                        for t in range(TILES):
                            rows_lo(G + 1, t)

        dve.wait_ge(slots_loaded, 16)
        fetch(0, 0)
        for j in range(2):
            split_hi(0, j)
        for t in range(TILES):
            statistics(0, 0, t)
        for t in range(TILES):
            normalise(0, 0, t)
        for t in range(TILES):
            rows_lo(0, t)
        hidden_lo(0, 0)
        over_experts(dve, expert)

    @block.gpsimd
    def _(pool):
        def split_lo(e, j):
            pool.wait_ge(w_hi, 2 * (PAIRS * e + j + 1))
            pool.tensor_tensor(wh1[:, LO, :, PW * j:PW * (j + 1)], raw1[:, j % 2, :, :],
                               wh1[:, HI, :, PW * j:PW * (j + 1)].bitcast(F32), ALU.subtract)
            pool.tensor_tensor(wh2[:, LO, 2 * j:2 * j + 2, :], raw2[:, j % 2, :, :],
                               wh2[:, HI, 2 * j:2 * j + 2, :].bitcast(F32), ALU.subtract).then_inc(w_lo, 1)

        def gather(G, half):
            pool.wait_ge(index_ready, 2 * (G + 1))
            alone(pool, pool_waits_met)
            for t in range(TILES):
                pool.indirect_dma_start(out=rows[:, half, t, :], out_offset=None, in_=x1_dram[:, :],
                                        in_offset=bass.IndirectOffsetOnAxis(ap=index[:, half, t:t + 1], axis=0),
                                        bounds_check=T, oob_is_err=False).then_inc(gathered[half], 16)

        def scatter(G, half):
            pool.wait_ge(y_done, TILES * (G + 1))
            alone(pool, pool_waits_met)
            for t in range(TILES):
                pool.indirect_dma_start(out=out_rows[:, :], in_=rows[:, half, t, :], in_offset=None,
                                        out_offset=bass.IndirectOffsetOnAxis(ap=index[:, half, t:t + 1], axis=0),
                                        bounds_check=T - 1, oob_is_err=False).then_inc(scattered[half], 16)

        def root(G):
            pool.wait_ge(s_stats, G + 1)
            pool.tensor_tensor(rstd2[:, :], var_eps2[:, :], half_neg[:, :], ALU.pow).then_inc(s_rstd, 1)

        def expert(e, first, nxt):
            for half in range(HALVES):
                more = half == 0 or nxt
                G = 2 * e + half
                for f in range(FC):
                    if f == 1 and half == 1:
                        scatter(G - 1, 0)
                    if f == 1 and half == 0 and not first:
                        scatter(G - 1, 1)
                    if f == 4 and more:
                        gather(G + 1, 1 - half)
                    for ahead, j in weight_pairs(first, nxt, half, f):
                        split_lo(e + ahead, j)
                    if f == 11 and more:
                        root(G + 1)

        gather(0, 0)
        split_lo(0, 0)
        split_lo(0, 1)
        root(0)
        over_experts(pool, expert)
        scatter(2 * E - 1, 1)
        for s in scattered:
            pool.wait_ge(s, 16 * TILES * E)


_INS = ["x", "ctx_768", "g_xattn", "g_ffn", "L0_xattn_Wq", "L0_xattn_Wk", "L0_xattn_Wv", "L0_xattn_Wo",
        "L0_xattn_bo", "L0_ffn_router_w", "L0_ffn_w1", "L0_ffn_w2"]


def kernel(**inputs):
    import numpy as _np
    import concourse.bacc as _bacc
    from concourse import mybir as _mybir
    from concourse.bass_utils import run_bass_kernel_spmd as _run

    nc = _bacc.Bacc("TRN2", target_bir_lowering=False, num_devices=1)
    arrays, args = {}, []
    for name in _INS:
        a = _np.ascontiguousarray(inputs[name])
        arrays[f"in_{name}_dram"] = a
        args.append(nc.dram_tensor(f"in_{name}_dram", a.shape, _mybir.dt.from_np(a.dtype), kind="ExternalInput").ap())
    args.append(nc.dram_tensor("out_0_dram", inputs["x"].shape, F32, kind="ExternalOutput").ap())
    flamingo_block(nc, *args)
    r = _run(nc, [arrays], core_ids=[0])
    return r.results[0]["out_0_dram"]
```

```python
from contextlib import ExitStack

import concourse.bass as bass
from concourse import mybir

F32 = mybir.dt.float32
F32R = mybir.dt.float32r
BF16 = mybir.dt.bfloat16
U32 = mybir.dt.uint32
ALU = mybir.AluOpType
ACT = mybir.ActivationFunctionType
AX = mybir.AxisListType

P = 128
HEADS = 16
DH = 64
TILES = 4
GN = TILES * P
QUADS = HEADS // 4
HP = 160
EPS = 1e-5

HI, LO = 0, 1
PASSES = ((LO, HI), (HI, LO), (HI, HI))


def split_matmul(pe, out, stationary, moving, first, last):
    for n, (s, m) in enumerate(PASSES):
        ins = pe.matmul(out, stationary(s), moving(m), start=first and n == 0,
                        stop=last and n == len(PASSES) - 1)
    return ins


def alone(engine, waits_met):
    engine.sem_inc(waits_met, 1)


def flamingo_block(nc, x, ctx_in, g_xattn, g_ffn, Wq, Wk, Wv, Wo, bo, router_w, w1, w2, out):
    B, N, D = x.shape
    _, M, DC = ctx_in.shape
    INNER = Wq.shape[1]
    E, _, F = w1.shape
    T = B * N
    CAP = T // E
    NG = T // GN
    GPB = NG // B
    KC, CC, IC = D // P, DC // P, INNER // P
    REM = M - P
    assert INNER == HEADS * DH and P < M <= P + 32 and CAP % GN == 0 and GPB == 4 and E == 8
    ROWS = B * M
    RT = ROWS // P
    RL = ROWS - RT * P
    PAIR = 2 * M
    KQ = 2 * PAIR
    VP = 3 * DH
    VL = 4 * VP
    VQ = VL + 4 * P
    KN = 2 * 2 * M
    VN = 2 * 4 * DH + 2 * DH
    SCALE = float(DH) ** -0.5

    x_rows = x.rearrange("b n d -> (b n) d")
    out_rows = out.rearrange("b n d -> (b n) d")
    x_tiles = x_rows.rearrange("(t p) d -> p t d", p=P)
    out_tiles = out_rows.rearrange("(t p) d -> p t d", p=P)

    keys_dram = nc.dram_tensor("keys_dram", (B, QUADS, P, KN), F32, kind="Internal").ap()
    values_dram = nc.dram_tensor("values_dram", (B, QUADS, P, VN), F32, kind="Internal").ap()
    x1_dram = nc.dram_tensor("x1_dram", (T + 1, D), F32, kind="Internal").ap()
    slots_dram = nc.dram_tensor("slots_dram", (T, 2), U32, kind="Internal").ap()
    x1_tiles = x1_dram[0:T, :].rearrange("(t p) d -> p t d", p=P)

    outer = ExitStack()
    sb = lambda stack, name, shape, dt: stack.enter_context(nc.sbuf_tensor(name, shape, dt))
    with outer:
        psum = outer.enter_context(nc.psum_tensor("psum", [P, 8, 512], F32))
        ident = sb(outer, "ident", [P, P], F32)
        tanh_g = sb(outer, "tanh_g", [P, 2], F32)
        half_neg = sb(outer, "half_neg", [P, TILES], F32)
        with ExitStack() as attention:
            wq = sb(attention, "wq", [P, 2, KC, INNER], F32R)
            wo = sb(attention, "wo", [P, 2, IC, D], F32R)
            bias = sb(attention, "bias", [P, D], F32)
            wr = sb(attention, "wr", [P, KC, E], F32)
            ones = sb(attention, "ones", [P, P], BF16)
            upto = sb(attention, "upto", [P, P], BF16)
            weight8 = sb(attention, "weight8", [P, E], F32)
            token = sb(attention, "token", [P, TILES], F32)
            x_in = sb(attention, "x_in", [P, TILES, D], F32)
            xT = sb(attention, "xT", [P, 2, KC, GN], F32R)
            with ExitStack() as stack:
                setup_block(nc, stack, sb, locals())
            with ExitStack() as stack:
                attention_block(nc, stack, sb, locals())
        with ExitStack() as stack:
            ffn_block(nc, stack, sb, locals())


def setup_block(nc, stack, sb, env):
    (psum, ident, tanh_g, half_neg, wq, wo, bias, wr, ones, upto, weight8, token) = [env[k] for k in (
        "psum", "ident", "tanh_g", "half_neg", "wq", "wo", "bias", "wr", "ones", "upto", "weight8", "token")]
    (B, M, KC, CC, INNER, D, E, T) = [env[k] for k in ("B", "M", "KC", "CC", "INNER", "D", "E", "T")]
    (RT, RL, ROWS, REM, PAIR, KN, VN) = [env[k] for k in ("RT", "RL", "ROWS", "REM", "PAIR", "KN", "VN")]
    ctx_in, keys_dram, values_dram, x1_dram, slots_dram = [env[k] for k in (
        "ctx_in", "keys_dram", "values_dram", "x1_dram", "slots_dram")]
    x_in, xT, x_tiles = env["x_in"], env["xT"], env["x_tiles"]

    RAW = 2048
    raw = sb(stack, "raw", [P, 2, RAW], F32)
    wk = sb(stack, "wk", [P, 2, CC, INNER], F32R)
    wv = sb(stack, "wv", [P, 2, CC, INNER], F32R)
    ctxT = sb(stack, "ctxT", [P, 2, CC, ROWS], F32R)
    ctx_last = sb(stack, "ctx_last", [P, 2, CC, B, 4, 32], F32R)
    STAGE = max(B * KN, QUADS * VN)
    stage = sb(stack, "stage", [P, 2, STAGE], F32R)
    ctx_sb = stage[:, 1, 0:(RT + 1) * CC * P].bitcast(F32).rearrange("p (t d) -> p t d", t=RT + 1)
    empty_slots = sb(stack, "empty_slots", [P, T // P, 2], U32)
    zero_row = sb(stack, "zero_row", [1, D], F32)
    gains = sb(stack, "gains", [P, 2], F32)
    stats0 = sb(stack, "stats0", [P, TILES, 6], F32)
    mean_var0 = sb(stack, "mean_var0", [P, TILES, 2], F32)
    var_eps0 = sb(stack, "var_eps0", [P, TILES], F32)
    rstd0 = sb(stack, "rstd0", [P, TILES], F32)

    sem = lambda name: stack.enter_context(nc.semaphore(name))
    ctx_loaded, small_loaded, x0_loaded = sem("ctx_loaded"), sem("small_loaded"), sem("x0_loaded")
    raw_loaded = [sem("raw_loaded0"), sem("raw_loaded1")]
    raw_hi, raw_split = sem("raw_hi"), sem("raw_split")
    consts_set, consts_shaped = sem("consts_set"), sem("consts_shaped")
    gains_ready, bias_ready = sem("gains_ready"), sem("bias_ready")
    ctxT_ready, ctxT_hi, ctxT_lo = sem("ctxT_ready"), sem("ctxT_hi"), sem("ctxT_lo")
    last_zeroed, last_ready = sem("last_zeroed"), sem("last_ready")
    bank_ready, bank_hi, bank_lo = sem("bank_ready"), sem("bank_hi"), sem("bank_lo")
    stored = [sem("stored0"), sem("stored1")]
    misc_stored = sem("misc_stored")
    step0, stats0_ready, rstd0_ready, x0_normed = sem("step0"), sem("stats0_ready"), sem("rstd0_ready"), sem("x0_normed")
    x0T_ready, x0T_hi, x0T_lo = sem("x0T_ready"), sem("x0T_hi"), sem("x0T_lo")

    pieces = []
    for w, src, cols in ((wk, env["Wk"], INNER // 4), (wv, env["Wv"], INNER // 2), (wq, env["Wq"], INNER // 2), (wo, env["Wo"], D // 2)):
        pieces += [(w, src, slice(c, c + cols)) for c in range(0, src.shape[1], cols)]
    V_PIECE = 4
    ORDER = (("W", 0), ("W", 1), ("K", 0), ("W", 2), ("K", 1), ("W", 3), ("W", 4), ("K", 2), ("W", 5), ("K", 3),
             ("W", 6), ("V", 0), ("W", 7), ("V", 1), ("W", 8), ("V", 2), ("W", 9), ("V", 3))
    assert len(pieces) == 10 and QUADS == 4 and B == 4
    USES = 4

    def stored_by(n):
        return 16 * (min(n, QUADS) // 2 + 2 * (max(n - QUADS, 0) // 2))

    def piece_views(n):
        w, src, cols = pieces[n]
        chunks, width = w.shape[2], cols.stop - cols.start
        flat = raw[:, n % 2, 0:chunks * width].rearrange("p (c n) -> p c n", c=chunks)
        return flat, (lambda s: w[:, s, :, cols]), src.rearrange("(c p) n -> p c n", p=P)[:, :, cols]

    block = stack.enter_context(nc.Block())

    @block.sync
    def _(sp):
        def load_piece(n):
            flat, _, src = piece_views(n)
            sp.dma_start(flat, src).then_inc(raw_loaded[n % 2], 16)

        rows = ctx_in.rearrange("b m d -> (b m) d")
        sp.dma_start(ctx_sb[:, 0:RT, :], rows[0:RT * P, :].rearrange("(t p) d -> p t d", p=P)).then_inc(ctx_loaded, 16)
        sp.dma_start(ctx_sb[0:RL, RT, :], rows[RT * P:ROWS, :]).then_inc(ctx_loaded, 16)
        load_piece(0)
        load_piece(1)
        sp.dma_start(gains[:, 0:1], env["g_xattn"].rearrange("(a n) -> a n", a=1).to_broadcast([P, 1])).then_inc(small_loaded, 16)
        sp.dma_start(gains[:, 1:2], env["g_ffn"].rearrange("(a n) -> a n", a=1).to_broadcast([P, 1])).then_inc(small_loaded, 16)
        sp.dma_start(bias[:, :], env["bo"].rearrange("(a n) -> a n", a=1).to_broadcast([P, D])).then_inc(small_loaded, 16)
        sp.dma_start(wr[:, :, :], env["router_w"].rearrange("(c p) e -> p c e", p=P)).then_inc(small_loaded, 16)
        for what, n in ORDER:
            if what == "W":
                if n + 2 < len(pieces):
                    sp.wait_ge(raw_split, n + 1)
                    load_piece(n + 2)
                if n == 5:
                    sp.dma_start(x_in[:, :, :], x_tiles[:, 0:TILES, :]).then_inc(x0_loaded, 16)
            elif what == "K":
                sp.wait_ge(bank_lo, USES * (n + 1))
                sp.dma_start(keys_dram[:, n].rearrange("b p n -> p b n"),
                             stage[:, n % 2, 0:B * KN].bitcast(F32).rearrange("p (b n) -> p b n", b=B)).then_inc(stored[n % 2], 16)
            else:
                for half in range(2):
                    sp.wait_ge(bank_lo, USES * (QUADS + n) + 2 * half + 2)
                    sp.dma_start(values_dram[n, 2 * half:2 * half + 2].rearrange("q p n -> p q n"),
                                 stage[:, n % 2, 2 * half * VN:2 * (half + 1) * VN].bitcast(F32).rearrange(
                                     "p (q n) -> p q n", q=2)).then_inc(stored[n % 2], 16)
            if (what, n) == ("K", 1):
                sp.wait_ge(consts_set, 9)
                sp.dma_start(slots_dram.rearrange("(p n) c -> p n c", p=P), empty_slots[:, :, :]).then_inc(misc_stored, 16)
                sp.dma_start(x1_dram[T:T + 1, :], zero_row[:, :]).then_inc(misc_stored, 16)
        sp.wait_ge(misc_stored, 32)
        for s in stored:
            sp.wait_ge(s, stored_by(QUADS + B))

    @block.gpsimd
    def _(pool):
        pool.memset(ident[:, :], 0.0).then_inc(consts_set, 1)
        pool.memset(upto[:, :], 1.0).then_inc(consts_set, 1)
        pool.memset(ones[:, :], 1.0).then_inc(consts_set, 1)
        pool.memset(half_neg[:, :], -0.5).then_inc(consts_set, 1)
        pool.memset(zero_row[:, :], 0.0).then_inc(consts_set, 1)
        pool.memset(empty_slots[:, :, 0:1], T).then_inc(consts_set, 1)
        pool.memset(empty_slots[:, :, 1:2], 0).then_inc(consts_set, 1)
        pool.iota(weight8[:, :], [[-1, E]], base=E, channel_multiplier=0,
                  allow_small_or_imprecise_dtypes=True).then_inc(consts_set, 1)
        pool.iota(token[:, :], [[P, TILES]], base=0, channel_multiplier=1,
                  allow_small_or_imprecise_dtypes=True).then_inc(consts_set, 1)
        pool.wait_ge(consts_set, 9)
        pool.affine_select(out=ident[:, :], in_=ident[:, :], compare_op=ALU.not_equal, fill=1.0, base=0,
                           pattern=[[-1, P]], channel_multiplier=1).then_inc(consts_shaped, 1)
        pool.affine_select(out=upto[:, :], in_=upto[:, :], compare_op=ALU.is_ge, fill=0.0, base=0,
                           pattern=[[1, P]], channel_multiplier=-1).then_inc(consts_shaped, 1)
        pool.memset(ctx_last[:, :, :, :, :, :].rearrange("p s c b j n -> p (s c b j n)").bitcast(F32), 0.0).then_inc(last_zeroed, 1)
        pool.wait_ge(stats0_ready, 1)
        pool.tensor_tensor(rstd0[:, :], var_eps0[:, :], half_neg[:, :], ALU.pow).then_inc(rstd0_ready, 1)

    def key_part(q, m, s):
        i, hb = m // 2, m % 2
        return stage[:, q % 2, 0:B * KN].rearrange("p (b s i m) -> p b s i m", b=B, s=2, i=2)[:, 2 * hb:2 * hb + 2, s, i, :]

    def value_parts(b, m, s):
        half, last = m // 2, m % 2
        to = stage[:, b % 2, 0:QUADS * VN].rearrange("p (q n) -> p q n", q=QUADS)[:, 2 * half:2 * half + 2, :]
        bank = psum[:, 4 + m, :].rearrange("p (q n) -> p q n", q=2)
        if not last:
            return [(to[:, :, 4 * DH * s:4 * DH * (s + 1)], bank)]
        return [(to[32 * j:32 * j + 32, :, DH * (8 + s):DH * (9 + s)], bank[32 * j:32 * j + 32, :, DH * j:DH * (j + 1)])
                for j in range(4)]

    def ctx_views(c, s):
        if c < CC:
            return ctxT[:, s, c, 0:RT * P], psum[:, c, 0:RT * P]
        return ctxT[:, s, :, RT * P:ROWS], psum[:, c, 0:CC * RL].rearrange("p (c n) -> p c n", c=CC)

    @block.scalar
    def _(act):
        for c in range(CC + 1):
            act.wait_ge(ctxT_ready, c + 1)
            dst, src = ctx_views(c, HI)
            act.activation(dst, src, ACT.Copy).then_inc(ctxT_hi, 1)
        for what, n in ORDER:
            if what == "W":
                flat, w, _ = piece_views(n)
                act.wait_ge(raw_loaded[n % 2], 16 * (n // 2 + 1))
                act.activation(w(HI), flat, ACT.Copy).then_inc(raw_hi, 1)
                if n == 5:
                    act.wait_ge(small_loaded, 64)
                    act.activation(tanh_g[:, :], gains[:, :], ACT.Tanh).then_inc(gains_ready, 1)
                continue
            use = USES * (n if what == "K" else QUADS + n)
            if use >= 2 * USES:
                act.wait_ge(stored[n % 2], stored_by(use // USES))
            for m in range(USES):
                act.wait_ge(bank_ready, use + m + 1)
                if what == "K":
                    ins = act.activation(key_part(n, m, HI), psum[:, 4 + m, 0:PAIR].rearrange("p (b m) -> p b m", b=2), ACT.Copy)
                else:
                    for dst, src in value_parts(n, m, HI):
                        ins = act.activation(dst, src, ACT.Copy)
                ins.then_inc(bank_hi, 1)
        for c in range(KC):
            act.wait_ge(x0T_ready, c + 1)
            act.activation(xT[:, HI, c, :], psum[:, c, :], ACT.Copy).then_inc(x0T_hi, 1)

    @block.vector
    def _(dve):
        for c in range(CC + 1):
            dve.wait_ge(ctxT_hi, c + 1)
            dst, src = ctx_views(c, LO)
            dve.tensor_tensor(dst, src, ctx_views(c, HI)[0].bitcast(F32), ALU.subtract).then_inc(ctxT_lo, 1)
        for what, n in ORDER:
            if what == "W":
                flat, w, _ = piece_views(n)
                dve.wait_ge(raw_hi, n + 1)
                dve.tensor_tensor(w(LO), flat, w(HI).bitcast(F32), ALU.subtract).then_inc(raw_split, 1)
                if n == 5:
                    dve.wait_ge(gains_ready, 1)
                    dve.tensor_scalar(bias[:, :], bias[:, :], tanh_g[:, 0:1], None, ALU.mult).then_inc(bias_ready, 1)
                continue
            use = USES * (n if what == "K" else QUADS + n)
            for m in range(USES):
                dve.wait_ge(bank_hi, use + m + 1)
                if what == "K":
                    ins = dve.tensor_tensor(key_part(n, m, LO), psum[:, 4 + m, 0:PAIR].rearrange("p (b m) -> p b m", b=2),
                                            key_part(n, m, HI).bitcast(F32), ALU.subtract)
                else:
                    for (dst, src), (hi, _) in zip(value_parts(n, m, LO), value_parts(n, m, HI)):
                        ins = dve.tensor_tensor(dst, src, hi.bitcast(F32), ALU.subtract)
                ins.then_inc(bank_lo, 1)
            if (what, n) == ("K", 0):
                dve.wait_ge(ctxT_lo, CC + 1)
                dve.wait_ge(last_zeroed, 1)
                for s in (HI, LO):
                    for c in range(CC):
                        src = ctxT[:, s, c, :].bitcast(F32).rearrange("p (b m) -> p b m", b=B)[:, :, P:M]
                        for j in range(4):
                            dve.tensor_copy(ctx_last[:, s, c, :, j, 0:REM], src).then_inc(last_ready, 1)
            if (what, n) == ("V", 0):
                dve.wait_ge(x0_loaded, 16)
                for t in range(TILES):
                    dve.bn_stats(stats0[:, t, :], x_in[:, t, :]).then_inc(step0, 1)
                dve.wait_ge(step0, TILES)
                for t in range(TILES):
                    dve.bn_aggr(mean_var0[:, t, :], stats0[:, t, :]).then_inc(step0, 1)
                dve.wait_ge(step0, 2 * TILES)
                dve.tensor_scalar(var_eps0[:, :], mean_var0[:, :, 1], EPS, None, ALU.add).then_inc(stats0_ready, 1)
            if (what, n) == ("V", 1):
                dve.wait_ge(rstd0_ready, 1)
                for t in range(TILES):
                    dve.tensor_scalar(x_in[:, t, :], x_in[:, t, :], mean_var0[:, t, 0:1], rstd0[:, t:t + 1],
                                      ALU.subtract, ALU.mult).then_inc(x0_normed, 1)
        for c in range(KC):
            dve.wait_ge(x0T_hi, c + 1)
            dve.tensor_tensor(xT[:, LO, c, :], psum[:, c, :], xT[:, HI, c, :].bitcast(F32), ALU.subtract).then_inc(x0T_lo, 1)

    @block.tensor
    def _(pe):
        pe.wait_ge(consts_shaped, 1)
        pe.wait_ge(ctx_loaded, 32)
        for c in range(CC):
            for t in range(RT):
                ins = pe.transpose(psum[:, c, P * t:P * (t + 1)], ctx_sb[:, t, P * c:P * (c + 1)], ident[:, :])
            ins.then_inc(ctxT_ready, 1)
        for c in range(CC):
            ins = pe.transpose(psum[:, CC, RL * c:RL * (c + 1)], ctx_sb[0:RL, RT, P * c:P * (c + 1)], ident[0:RL, 0:RL])
        ins.then_inc(ctxT_ready, 1)
        pe.wait_ge(ctxT_lo, CC + 1)
        for q in range(QUADS):
            pe.wait_ge(raw_split, q + 1)
            for m in range(USES):
                i, hb = m // 2, m % 2
                if q:
                    pe.wait_ge(bank_lo, USES * (q - 1) + m + 1)
                k = 2 * q + i
                for c in range(CC):
                    ins = split_matmul(pe, psum[:, 4 + m, 0:PAIR], lambda s: wk[:, s, c, P * k:P * (k + 1)],
                                       lambda s: ctxT[:, s, c, PAIR * hb:PAIR * (hb + 1)], c == 0, c == CC - 1)
                ins.then_inc(bank_ready, 1)
        pe.wait_ge(last_ready, 8 * CC)
        for b in range(B):
            for m in range(USES):
                half, last = m // 2, m % 2
                if b == 0:
                    pe.wait_ge(raw_split, V_PIECE + half + 1)
                pe.wait_ge(bank_lo, USES * (QUADS + b - 1) + m + 1)
                for c in range(CC):
                    rows = (lambda s: ctx_last[:, s, c, b, :, :].rearrange("p j n -> p (j n)")) if last else (
                        lambda s: ctxT[:, s, c, M * b:M * b + P])
                    ins = split_matmul(pe, psum[:, 4 + m, :], rows,
                                       lambda s: wv[:, s, c, 512 * half:512 * (half + 1)], c == 0, c == CC - 1)
                ins.then_inc(bank_ready, 1)
        pe.wait_ge(x0_normed, TILES)
        for c in range(KC):
            for t in range(TILES):
                ins = pe.transpose(psum[:, c, P * t:P * (t + 1)], x_in[:, t, P * c:P * (c + 1)], ident[:, :])
            ins.then_inc(x0T_ready, 1)


def attention_block(nc, stack, sb, env):
    (psum, ident, tanh_g, half_neg, wq, wo, bias, wr, ones, upto, weight8, token) = [env[k] for k in (
        "psum", "ident", "tanh_g", "half_neg", "wq", "wo", "bias", "wr", "ones", "upto", "weight8", "token")]
    (B, M, KC, D, E, T, NG, GPB, CAP) = [env[k] for k in ("B", "M", "KC", "D", "E", "T", "NG", "GPB", "CAP")]
    (PAIR, KQ, VP, VL, VQ, VN, SCALE) = [env[k] for k in ("PAIR", "KQ", "VP", "VL", "VQ", "VN", "SCALE")]
    keys_dram, values_dram, slots_dram = env["keys_dram"], env["values_dram"], env["slots_dram"]
    x_tiles, out_tiles, x1_tiles = env["x_tiles"], env["out_tiles"], env["x1_tiles"]

    keys = sb(stack, "keys", [P, QUADS, 2, KQ], F32R)
    values = sb(stack, "values", [P, QUADS, VQ], F32R)
    x_in, xT = env["x_in"], env["xT"]
    qT = sb(stack, "qT", [P, 2, 2, 2, GN], F32R)
    exp_scores = sb(stack, "exp_scores", [P, 2, 4, M], F32)
    probs = sb(stack, "probs", [P, 4 * HP], F32)
    probsT = sb(stack, "probsT", [P, 2, 5, GN], F32R)
    attnT = sb(stack, "attnT", [P, 2, 2, GN], F32R)
    partial = sb(stack, "partial", [P, TILES, D], F32)
    x1 = sb(stack, "x1", [P, TILES, D], F32)
    xn2 = sb(stack, "xn2", [P, 2, D], F32)
    xn2T = sb(stack, "xn2T", [P, 2, D], F32)
    neg_max = sb(stack, "neg_max", [P, 2, 4], F32)
    sums = sb(stack, "sums", [P, 2, 4], F32)
    inv_sums = sb(stack, "inv_sums", [P, 2, 4], F32)
    stats = sb(stack, "stats", [P, TILES, 6], F32)
    mean_var = sb(stack, "mean_var", [P, 2, TILES, 2], F32)
    var_eps = sb(stack, "var_eps", [P, 2, TILES], F32)
    rstd = sb(stack, "rstd", [P, 2, TILES], F32)
    logits = sb(stack, "logits", [P, TILES, E], F32)
    shifted = sb(stack, "shifted", [P, TILES, E], F32)
    exps = sb(stack, "exps", [P, TILES, E], F32)
    top = sb(stack, "top", [P, TILES], F32)
    marked = sb(stack, "marked", [P, TILES, E], F32)
    first8 = sb(stack, "first8", [P, TILES], F32)
    chosen = sb(stack, "chosen", [P, TILES, E], BF16)
    chosen_sum = sb(stack, "chosen_sum", [P, E], F32)
    before = sb(stack, "before", [P, E], BF16)
    placed = sb(stack, "placed", [P, TILES, E], F32)
    place = sb(stack, "place", [P, TILES], F32)
    over = sb(stack, "over", [P, TILES], F32)
    slot = sb(stack, "slot", [P, TILES], F32)
    slot_index = sb(stack, "slot_index", [P, TILES], U32)
    denom = sb(stack, "denom", [P, TILES], F32)
    gate = sb(stack, "gate", [P, TILES], F32)
    entry = sb(stack, "entry", [P, TILES, 2], U32)

    TRANSPOSED, LAST, ODD, EVEN = 4, 5, 6, 7
    ATTEND_BANK, PROJECT_BANK, QUERY_BANK = (EVEN, ODD), (ODD, ODD, EVEN, ODD), EVEN
    X_BANK, LOGITS_BANK = (EVEN, TRANSPOSED, EVEN, ODD), ODD
    logits_ps = psum[:, LOGITS_BANK, 0:2 * E].rearrange("p (t e) -> p t e", e=E)
    place_ps = psum[:, TRANSPOSED, 0:TILES * E].rearrange("p (t e) -> p t e", e=E)

    sem = lambda name: stack.enter_context(nc.semaphore(name))
    keys_loaded = [sem(f"keys_loaded{q}") for q in range(QUADS)]
    values_loaded = [sem(f"values_loaded{q}") for q in range(QUADS)]
    x_loaded = sem("x_loaded")
    partial_loaded = [sem(f"partial_loaded{t}") for t in range(TILES)]
    partial_biased = sem("partial_biased")
    x1_stored = sem("x1_stored")
    slots_stored = sem("slots_stored")
    probs_zeroed, keys_zeroed, values_zeroed = sem("probs_zeroed"), sem("keys_zeroed"), sem("values_zeroed")
    stat_step = sem("stat_step")
    norm1_stats, norm1_rstd, norm1_done = sem("norm1_stats"), sem("norm1_rstd"), sem("norm1_done")
    norm2_stats, norm2_rstd, norm2_done = sem("norm2_stats"), sem("norm2_rstd"), sem("norm2_done")
    scores_ready, max_ready, exp_done = sem("scores_ready"), sem("max_ready"), sem("exp_done")
    sums_inverted, probs_ready = sem("sums_inverted"), sem("probs_ready")
    probsT_ready, probsT_hi, probsT_lo = sem("probsT_ready"), sem("probsT_hi"), sem("probsT_lo")
    last_hi, last_lo = sem("last_hi"), sem("last_lo")
    xT_ready, xT_hi, xT_lo = sem("xT_ready"), sem("xT_hi"), sem("xT_lo")
    query_ready, query_hi, query_lo = sem("query_ready"), sem("query_hi"), sem("query_lo")
    attn_ready, attn_hi, attn_lo = sem("attn_ready"), sem("attn_hi"), sem("attn_lo")
    proj_ready, proj_added = sem("proj_ready"), sem("proj_added")
    norm2T_ready, norm2T_copied = sem("norm2T_ready"), sem("norm2T_copied")
    logits_ready, logits_copied = sem("logits_ready"), sem("logits_copied")
    places_ready, places_read = sem("places_ready"), sem("places_read")
    chosen_ready = sem("chosen_ready")
    shifted_ready, exps_ready = sem("shifted_ready"), sem("exps_ready")
    route_step, entry_ready = sem("route_step"), sem("entry_ready")
    dve_waits_met, pool_waits_met = sem("dve_waits_met"), sem("pool_waits_met")

    KEY_LOADS, VALUE_LOADS = 2, 6
    UNITS = QUADS * TILES
    ROUTE = 14
    ROUTING = {5: ("norm", 0), 7: ("norm", 1), 8: ("logits", 0), 9: ("norm", 2), 10: ("norm", 3),
               11: ("logits", 1), 13: ("places", 0)}

    def routing_steps(u, prev, cur):
        if prev and not cur and u in (5, 7, 9, 10):
            return [("norm", t) for t in range(TILES)] if u == 5 else []
        return [ROUTING[u]] if prev and u in ROUTING else []

    def last_round(g, q):
        return isinstance(g, int) and g == NG - 1 and q == QUADS - 1

    def project_bank(g, q, t):
        return t if last_round(g, q) else PROJECT_BANK[t]

    def norm2_places(g, t):
        if isinstance(g, int) and g == NG - 1:
            return partial[:, t, :], (xn2T, xn2)[t // 2][:, t % 2, :], t
        return xn2[:, t % 2, :], xn2T[:, t % 2, :], TRANSPOSED

    def over_groups(engine, body):
        body(0, False, True, True)
        with engine.Fori(1, NG - 1) as g:
            body(g, True, True, True)
        body(NG - 1, True, True, False)
        body(NG, True, False, False)

    block = stack.enter_context(nc.Block())

    @block.sync
    def _(sp):
        def load_keys(b, q):
            src = keys_dram[bass.ds(b, 1), q].rearrange("b p n -> (b p) n")
            for r in range(2):
                rows = slice(DH * r, DH * (r + 1))
                sp.dma_start(keys[rows, q, :, :].rearrange("p s n -> p (s n)").bitcast(F32).rearrange(
                    "p (s r m) -> p s r m", r=2, m=M)[:, :, r, :],
                    src[rows, :].rearrange("p (s m) -> p s m", m=M)).then_inc(keys_loaded[q], 16)

        def load_values(b, q):
            src = values_dram[bass.ds(b, 1), q].rearrange("b p n -> (b p) n")
            for c in range(2):
                sp.dma_start(values[:, q, 0:VL].bitcast(F32).rearrange("p (n c d) -> p n c d", c=3, d=DH)[:, :, 2 * c, :],
                             src[:, 0:8 * DH].rearrange("p (n c d) -> p n c d", c=2, d=DH)[:, :, c, :]).then_inc(values_loaded[q], 16)
            for j in range(4):
                rows, col = slice(32 * j, 32 * j + 32), P * (j // 2) + DH * (j % 2)
                sp.dma_start(values[rows, q, VL:VQ].bitcast(F32).rearrange("p (s n) -> p s n", s=2)[:, :, col:col + DH],
                             src[rows, 8 * DH:VN].rearrange("p (s n) -> p s n", s=2)).then_inc(values_loaded[q], 16)

        def load_x(g):
            sp.dma_start(x_in[:, :, :], x_tiles[:, bass.ds(g * TILES, TILES), :]).then_inc(x_loaded, 16)

        def load_partial(g, t):
            sp.dma_start(partial[:, t, :], x_tiles[:, bass.ds(g * TILES + t, 1), :].rearrange("p t d -> p (t d)")).then_inc(partial_loaded[t], 16)

        def iteration(g, more_partial, more_x, reload, last_values):
            used = 2 * QUADS * (g + 1)
            added = TILES * (QUADS * g + QUADS - 1)
            if last_values:
                sp.wait_ge(attn_ready, used)
                load_values(g // GPB + 1, QUADS - 1)
            for t in range(TILES):
                if more_partial:
                    sp.wait_ge(proj_added, added + t + 1)
                    load_partial(g + 1, t)
                if t == 0 and reload:
                    sp.wait_ge(scores_ready, UNITS * (g + 1) + TILES)
                    load_keys(g // GPB + 1, 0)
            sp.wait_ge(proj_added, added + TILES)
            sp.dma_start(x1_tiles[:, bass.ds(g * TILES, TILES), :], x1[:, :, :]).then_inc(x1_stored, 16)
            sp.dma_start(out_tiles[:, bass.ds(g * TILES, TILES), :], x1[:, :, :]).then_inc(x1_stored, 16)
            if reload:
                sp.wait_ge(attn_ready, used + 2)
                load_values(g // GPB + 1, 0)
                sp.wait_ge(scores_ready, UNITS * (g + 1) + 2 * TILES)
                load_keys(g // GPB + 1, 1)
                sp.wait_ge(attn_ready, used + 4)
                load_values(g // GPB + 1, 1)
                sp.wait_ge(scores_ready, UNITS * (g + 1) + 3 * TILES)
                load_keys(g // GPB + 1, 2)
            if more_x:
                sp.wait_ge(xT_ready, KC * (g + 2))
                load_x(g + 3)
            if reload:
                sp.wait_ge(attn_ready, used + 6)
                load_values(g // GPB + 1, 2)
                sp.wait_ge(scores_ready, UNITS * (g + 1) + 4 * TILES)
                load_keys(g // GPB + 1, 3)

        load_x(1)
        for q in range(QUADS):
            sp.wait_ge(keys_zeroed, q + 1)
            load_keys(0, q)
        sp.wait_ge(values_zeroed, 1)
        for q in range(QUADS):
            load_values(0, q)
        for t in range(TILES):
            load_partial(0, t)
        sp.wait_ge(xT_ready, KC)
        load_x(2)
        with sp.Fori(0, B - 1) as b:
            for j in range(GPB):
                iteration(b * GPB + j, True, True, j == GPB - 2, j == GPB - 1)
        for g in range(NG - GPB, NG):
            iteration(g, g + 1 < NG, g + 3 < NG, False, False)
        sp.wait_ge(x1_stored, 32 * NG)

    @block.tensor
    def _(pe):
        def transposes_x(g, c):
            if c == 0:
                pe.wait_ge(norm1_done, TILES * g)
            for t in range(TILES):
                ins = pe.transpose(psum[:, X_BANK[c], P * t:P * (t + 1)], x_in[:, t, P * c:P * (c + 1)], ident[:, :])
            ins.then_inc(xT_ready, 1)

        def queries(g, q, i):
            k, n = 2 * q + i, QUADS * g + q
            if i == 1:
                pe.wait_ge(query_lo, 2 * n + 1)
            elif not (isinstance(n, int) and n < 2):
                pe.wait_ge(attn_lo, 2 * (n - 2) + 1)
                if q == 0:
                    pe.wait_ge(xT_lo, KC * g)
            for c in range(KC):
                ins = split_matmul(pe, psum[:, QUERY_BANK, :], lambda s: wq[:, s, c, P * k:P * (k + 1)],
                                   lambda s: xT[:, s, c, :], c == 0, c == KC - 1)
            ins.then_inc(query_ready, 1)

        def scores(g, u):
            q, t = u // TILES, u % TILES
            if t == 0:
                pe.wait_ge(query_lo, 2 * (QUADS * g + q) + 2)
                pe.wait_ge(keys_loaded[q], 16 * KEY_LOADS * (g // GPB + 1))
            if not (isinstance(g, int) and g == 0 and u < 2):
                pe.wait_ge(exp_done, UNITS * g + u - 1)
            for i in range(2):
                ins = split_matmul(pe, psum[:, 2 * (u % 2) + i, 0:PAIR],
                                   lambda s: qT[:, q % 2, s, i, P * t:P * (t + 1)],
                                   lambda s: keys[:, q, s, PAIR * i:PAIR * (i + 1)], True, True)
            ins.then_inc(scores_ready, 1)

        def transposes_probs(g, u, aux):
            q, t = u // TILES, u % TILES
            pe.wait_ge(probs_ready, UNITS * g + u + 1)
            if aux:
                pe.wait_ge(*aux)
            elif not (isinstance(g, int) and g == 0 and u < 1):
                pe.wait_ge(probsT_lo, UNITS * g + u)
            for h in range(4):
                pe.transpose(psum[:, TRANSPOSED, P * h:P * (h + 1)], probs[:, P * h:P * (h + 1)], ident[:, :])
            if t == 0 and not (isinstance(g, int) and g == 0 and q == 0):
                pe.wait_ge(last_lo, QUADS * g + q)
            pe.transpose(psum[:, LAST, P * t:P * (t + 1)], probs[:, 4 * P:4 * HP], ident[:, :]).then_inc(probsT_ready, 1)

        def attend(g, q, i):
            n = QUADS * g + q
            if i == 0:
                pe.wait_ge(probsT_lo, UNITS * g + TILES * (q + 1))
                pe.wait_ge(last_lo, n + 1)
                pe.wait_ge(values_loaded[q], 16 * VALUE_LOADS * (g // GPB + 1))
            if not (isinstance(n, int) and n == 0):
                pe.wait_ge(proj_added, TILES * (n - 1) + 3 + i)
            parts = ((VP * i, 2 * VP, 2 * i), (VP * i + DH, 2 * VP, 2 * i + 1), (VL + P * i, 2 * P, 4))
            for m, (col, per_part, chunk) in enumerate(parts):
                ins = split_matmul(pe, psum[:, ATTEND_BANK[i], :],
                                   lambda s: values[:, q, col + per_part * s:col + per_part * s + P],
                                   lambda s: probsT[:, s, chunk, :], m == 0, m == 2)
            ins.then_inc(attn_ready, 1)

        def project(g, q, t, more_queries):
            n = QUADS * g + q
            if t == 0:
                pe.wait_ge(attn_lo, 2 * n + 2)
            if last_round(g, q):
                if t == 0:
                    pe.wait_ge(exp_done, UNITS * NG)
            elif t == 2 and more_queries:
                pe.wait_ge(query_lo, 2 * (n + 2) + 2)
            elif t in (1, 3):
                pe.wait_ge(proj_added, TILES * n + (1 if t == 1 else 2))
            for i in range(2):
                ins = split_matmul(pe, psum[:, project_bank(g, q, t), :], lambda s: attnT[:, s, i, P * t:P * (t + 1)],
                                   lambda s: wo[:, s, 2 * q + i, :], i == 0, i == 1)
            ins.then_inc(proj_ready, 1)

        def transposes_norm2(g, t):
            pe.wait_ge(norm2_done, TILES * g + t + 1)
            src, _, bank = norm2_places(g, t)
            for c in range(KC):
                ins = pe.transpose(psum[:, bank, P * c:P * (c + 1)], src[:, P * c:P * (c + 1)], ident[:, :])
            ins.then_inc(norm2T_ready, 1)

        def route(g, half):
            if half:
                pe.wait_ge(logits_copied, 2 * g + 1)
            for t in range(2):
                pe.wait_ge(norm2T_copied, TILES * g + 2 * half + t + 1)
                _, transposed, _ = norm2_places(g, 2 * half + t)
                for c in range(KC):
                    ins = pe.matmul(logits_ps[:, t, :], transposed[:, P * c:P * (c + 1)], wr[:, c, :],
                                    start=c == 0, stop=c == KC - 1)
            ins.then_inc(logits_ready, 1)

        def places(g):
            pe.wait_ge(chosen_ready, g + 1)
            for t in range(TILES):
                pe.matmul(place_ps[:, t, :], upto[:, :], chosen[:, t, :], start=True, stop=False)
                for s in range(t):
                    pe.matmul(place_ps[:, t, :], ones[:, :], chosen[:, s, :], start=False, stop=False)
                ins = pe.matmul(place_ps[:, t, :], ones[:, :], before[:, :], start=False, stop=True)
            ins.then_inc(places_ready, 1)

        def group(g, prev, cur, nxt):
            aux = None

            def routing(u, transposed=0):
                nonlocal aux
                for what, n in routing_steps(u, prev, cur):
                    if what == "norm" and not cur:
                        if n == 0:
                            pe.wait_ge(exp_done, UNITS * NG)
                    elif what in ("norm", "places"):
                        if aux:
                            pe.wait_ge(*aux)
                        else:
                            pe.wait_ge(probsT_lo, UNITS * g + (u + transposed if cur else 0))
                    if what == "norm":
                        transposes_norm2(g - 1, n)
                        aux = norm2T_copied, TILES * (g - 1) + n + 1
                    elif what == "places":
                        places(g - 1)
                        aux = places_read, g

            def probabilities(u):
                nonlocal aux
                if cur:
                    transposes_probs(g, u, aux)
                    aux = None

            for u in range(UNITS):
                q, t = u // TILES, u % TILES
                q1, g1, do1 = (q - 1, g, cur) if q else (QUADS - 1, g - 1, prev)
                n1 = QUADS * g1 + q1
                u2, g2, do2 = (u + 2, g, cur) if u + 2 < UNITS else (u + 2 - UNITS, g + 1, nxt)
                q3, g3, do3 = (q + 1, g, cur) if q + 1 < QUADS else (0, g + 1, nxt)
                if t == 0:
                    if do2:
                        scores(g2, u2)
                    probabilities(u)
                    if u == 12 and nxt:
                        pe.wait_ge(proj_added, TILES * (n1 - 1) + 4)
                        transposes_x(g + 1, 3)
                        pe.wait_ge(xT_lo, KC * g + 3)
                    if prev and u == 8:
                        if do1:
                            pe.wait_ge(proj_added, TILES * (n1 - 1) + 4)
                        route(g - 1, 0)
                    if do1:
                        attend(g1, q1, 0)
                        if u == 12 and nxt:
                            pe.wait_ge(xT_lo, KC * (g + 1))
                        if prev and u == 8:
                            pe.wait_ge(logits_copied, 2 * g - 1)
                        attend(g1, q1, 1)
                elif t == 1:
                    if do3:
                        queries(g3, q3, 0)
                    routing(u)
                    if do2:
                        scores(g2, u2)
                    probabilities(u)
                    if do1:
                        project(g1, q1, 0, do3)
                elif t == 2:
                    routing(u)
                    if do3:
                        queries(g3, q3, 1)
                    probabilities(u)
                    if do1:
                        project(g1, q1, 1, do3)
                    if u == 10 and nxt:
                        pe.wait_ge(query_lo, 2 * (n1 + 2) + 2)
                        transposes_x(g + 1, 0)
                    if do2:
                        scores(g2, u2)
                else:
                    probabilities(u)
                    if prev and u == 11:
                        if do1:
                            pe.wait_ge(proj_added, TILES * n1 + 2)
                        route(g - 1, 1)
                    if do1:
                        if u == 11 and nxt:
                            pe.wait_ge(xT_lo, KC * g + 1)
                        project(g1, q1, 2, do3)
                    if do2:
                        scores(g2, u2)
                    if u == 7:
                        routing(u, 1)
                    if u == 11 and nxt:
                        pe.wait_ge(probsT_lo, UNITS * g + u + 1)
                        transposes_x(g + 1, 1)
                        aux = xT_lo, KC * g + 2
                    if do1:
                        if prev and u == 11:
                            pe.wait_ge(logits_copied, 2 * g)
                        project(g1, q1, 3, do3)
                    if u == 11 and nxt:
                        pe.wait_ge(proj_added, TILES * n1 + 3)
                        transposes_x(g + 1, 2)

        for i in range(2):
            queries(0, 0, i)
        scores(0, 0)
        scores(0, 1)
        over_groups(pe, group)

    @block.scalar
    def _(act):
        def hi(dst, bank, ready, done, n, scale=1.0):
            act.wait_ge(ready, n + 1)
            act.activation(dst, psum[:, bank, :], ACT.Copy, scale=scale).then_inc(done, 1)

        def x_hi(g, c):
            hi(xT[:, HI, c, :], X_BANK[c], xT_ready, xT_hi, KC * (g - 1) + c)

        def query_part(g, q, i):
            hi(qT[:, q % 2, HI, i, :], QUERY_BANK, query_ready, query_hi, 2 * (QUADS * g + q) + i, SCALE)

        def attn_part(g, q, i):
            hi(attnT[:, HI, i, :], ATTEND_BANK[i], attn_ready, attn_hi, 2 * (QUADS * g + q) + i)

        def exp(g, u):
            act.wait_ge(max_ready, UNITS * g + u + 1)
            if not (isinstance(g, int) and g == 0 and u < 2):
                act.wait_ge(probs_ready, UNITS * g + u - 1)
            for h in range(4):
                ins = act.activation(exp_scores[:, u % 2, h, :],
                                     psum[:, 2 * (u % 2) + h // 2, M * (h % 2):M * (h % 2 + 1)], ACT.Exp,
                                     bias=neg_max[:, u % 2, h:h + 1], accum_out=sums[:, u % 2, h:h + 1])
            ins.then_inc(exp_done, 1)

        def probs_hi(g, u):
            t = u % TILES
            act.wait_ge(probsT_ready, UNITS * g + u + 1)
            if t == 0 and not (isinstance(g, int) and g == 0 and u == 0):
                act.wait_ge(attn_ready, 2 * (QUADS * g + u // TILES))
            act.activation(probsT[:, HI, 0:4, P * t:P * (t + 1)],
                           psum[:, TRANSPOSED, :].rearrange("p (h n) -> p h n", h=4), ACT.Copy).then_inc(probsT_hi, 1)

        def last_part(g, q):
            act.wait_ge(probsT_ready, UNITS * g + TILES * (q + 1))
            act.activation(probsT[:, HI, 4, :].rearrange("p (t n) -> p t n", t=TILES),
                           psum[:, LAST, :].rearrange("p (t n) -> p t n", t=TILES), ACT.Copy).then_inc(last_hi, 1)

        def group(g, prev, cur, nxt):
            def routing(u):
                for what, n in routing_steps(u, prev, cur):
                    if what == "norm":
                        act.wait_ge(norm2T_ready, TILES * (g - 1) + n + 1)
                        _, dst, bank = norm2_places(g - 1, n)
                        act.activation(dst, psum[:, bank, :], ACT.Copy).then_inc(norm2T_copied, 1)

            for u in range(UNITS):
                q, t = u // TILES, u % TILES
                q1, g1, do1 = (q - 1, g, cur) if q else (QUADS - 1, g - 1, prev)
                u2, g2, do2 = (u + 2, g, cur) if u + 2 < UNITS else (u + 2 - UNITS, g + 1, nxt)
                q3, g3, do3 = (q + 1, g, cur) if q + 1 < QUADS else (0, g + 1, nxt)
                if t == 0:
                    if u == 12 and nxt:
                        x_hi(g + 1, 3)
                    if do2:
                        exp(g2, u2)
                    if do1:
                        attn_part(g1, q1, 0)
                        attn_part(g1, q1, 1)
                    if cur:
                        probs_hi(g, u)
                elif t == 1:
                    if do3:
                        query_part(g3, q3, 0)
                    routing(u)
                    if cur:
                        probs_hi(g, u)
                    if do2:
                        exp(g2, u2)
                elif t == 2:
                    routing(u)
                    if do3:
                        query_part(g3, q3, 1)
                    if cur:
                        probs_hi(g, u)
                    if u == 10 and nxt:
                        x_hi(g + 1, 0)
                else:
                    if cur:
                        probs_hi(g, u)
                    if nxt or (cur and u < UNITS - 1):
                        exp(*before_last)
                    if cur:
                        last_part(g, q)
                    if u == 7:
                        routing(u)
                    if u == 11 and nxt:
                        x_hi(g + 1, 1)
                    if do2:
                        exp(g2, u2)
                    if u == 11 and nxt:
                        x_hi(g + 1, 2)
                before_last = g2, u2
                if prev and u == 12:
                    act.wait_ge(shifted_ready, g)
                    act.activation(exps[:, :, :], shifted[:, :, :], ACT.Exp).then_inc(exps_ready, 1)

        for i in range(2):
            query_part(0, 0, i)
        exp(0, 0)
        exp(0, 1)
        over_groups(act, group)

    @block.vector
    def _(dve):
        def lo(which, bank, hi_done, done, n, scale=None):
            dve.wait_ge(hi_done, n + 1)
            if scale is None:
                ins = dve.tensor_tensor(which(LO), psum[:, bank, :], which(HI).bitcast(F32), ALU.subtract)
            else:
                ins = dve.scalar_tensor_tensor(out=which(LO), in0=psum[:, bank, :], scalar=scale,
                                               in1=which(HI).bitcast(F32), op0=ALU.mult, op1=ALU.subtract)
            ins.then_inc(done, 1)

        def x_lo(g, c):
            lo(lambda s: xT[:, s, c, :], X_BANK[c], xT_hi, xT_lo, KC * (g - 1) + c)

        def query_part(g, q, i):
            lo(lambda s: qT[:, q % 2, s, i, :], QUERY_BANK, query_hi, query_lo, 2 * (QUADS * g + q) + i, SCALE)

        def attn_part(g, q, i):
            lo(lambda s: attnT[:, s, i, :], ATTEND_BANK[i], attn_hi, attn_lo, 2 * (QUADS * g + q) + i)

        def row_max(g, u):
            dve.wait_ge(scores_ready, UNITS * g + u + 1)
            src = psum[:, 2 * (u % 2):2 * (u % 2) + 2, 0:PAIR].rearrange("p i (h m) -> p i h m", h=2)
            dve.tensor_reduce(neg_max[:, u % 2, :].rearrange("p (i h) -> p i h", i=2), src, AX.X, ALU.max,
                              negate=True).then_inc(max_ready, 1)

        def invert(g, u):
            dve.wait_ge(exp_done, UNITS * g + u + 1)
            dve.reciprocal(inv_sums[:, u % 2, :], sums[:, u % 2, :]).then_inc(sums_inverted, 1)

        def probs_lo(g, u):
            t = u % TILES
            dve.wait_ge(probsT_hi, UNITS * g + u + 1)
            dve.tensor_tensor(probsT[:, LO, 0:4, P * t:P * (t + 1)],
                              psum[:, TRANSPOSED, :].rearrange("p (h n) -> p h n", h=4),
                              probsT[:, HI, 0:4, P * t:P * (t + 1)].bitcast(F32), ALU.subtract).then_inc(probsT_lo, 1)

        def last_part(g, q):
            dve.wait_ge(last_hi, QUADS * g + q + 1)
            dve.tensor_tensor(probsT[:, LO, 4, :].rearrange("p (t n) -> p t n", t=TILES), psum[:, LAST, :].rearrange("p (t n) -> p t n", t=TILES),
                              probsT[:, HI, 4, :].bitcast(F32).rearrange("p (t n) -> p t n", t=TILES),
                              ALU.subtract).then_inc(last_lo, 1)

        def add_projection(g, q, t):
            dve.wait_ge(proj_ready, TILES * (QUADS * g + q) + t + 1)
            if q == 0:
                dve.wait_ge(partial_biased, TILES * g + t + 1)
            last = q == QUADS - 1
            if last and t == 0 and not (isinstance(g, int) and g == 0):
                dve.wait_ge(x1_stored, 32 * g)
            ins = dve.scalar_tensor_tensor(out=(x1 if last else partial)[:, t, :], in0=psum[:, project_bank(g, q, t), :],
                                           scalar=tanh_g[:, 0:1], in1=partial[:, t, :], op0=ALU.mult, op1=ALU.add)
            ins.then_inc(proj_added, 1)

        def normalise(which, g, t):
            dve.wait_ge((norm1_rstd, norm2_rstd)[which], g + which)
            if which == 1 and t >= 2 and not (isinstance(g, int) and g == NG - 1):
                dve.wait_ge(norm2T_ready, TILES * g + t - 1)
            dst, src = ((x_in[:, t, :], x_in[:, t, :]), (norm2_places(g, t)[0], x1[:, t, :]))[which]
            dve.tensor_scalar(dst, src, mean_var[:, which, t, 0:1], rstd[:, which, t:t + 1],
                              ALU.subtract, ALU.mult).then_inc((norm1_done, norm2_done)[which], 1)

        def group(g, prev, cur, nxt):
            stat_n = STATS_OF(g)

            def step_stat(ins):
                nonlocal stat_n
                ins.then_inc(stat_step, 1)
                stat_n = stat_n + 1

            def tile_stats(which, t):
                src = (x_in, x1)[which]
                if which == 0 and t == 0:
                    dve.wait_ge(x_loaded, 16 * (g + 1))
                if which == 1:
                    dve.wait_ge(proj_added, TILES * (QUADS * g - 1) + t + 1)
                    alone(dve, dve_waits_met)
                step_stat(dve.bn_stats(stats[:, t, :], src[:, t, :]))

            def norm_stats(which):
                dve.wait_ge(stat_step, stat_n)
                alone(dve, dve_waits_met)
                for t in range(TILES):
                    step_stat(dve.bn_aggr(mean_var[:, which, t, :], stats[:, t, :]))
                dve.wait_ge(stat_step, stat_n)
                dve.tensor_scalar(var_eps[:, which, :], mean_var[:, which, :, 1], EPS, None, ALU.add)\
                   .then_inc((norm1_stats, norm2_stats)[which], 1)

            def routing(u):
                what, n = ROUTING.get(u, (None, None)) if prev else (None, None)
                if what == "logits":
                    dve.wait_ge(logits_ready, 2 * (g - 1) + n + 1)
                    dve.tensor_copy(logits[:, 2 * n:2 * n + 2, :], logits_ps).then_inc(logits_copied, 1)
                elif what == "places":
                    dve.wait_ge(places_ready, g)
                    dve.tensor_tensor(placed[:, :, :], place_ps, chosen[:, :, :], ALU.mult).then_inc(places_read, 1)

            for u in range(UNITS):
                q, t = u // TILES, u % TILES
                q1, g1, do1 = (q - 1, g, cur) if q else (QUADS - 1, g - 1, prev)
                u2, g2, do2 = (u + 2, g, cur) if u + 2 < UNITS else (u + 2 - UNITS, g + 1, nxt)
                q3, g3, do3 = (q + 1, g, cur) if q + 1 < QUADS else (0, g + 1, nxt)
                if t == 0:
                    if do2:
                        row_max(g2, u2)
                    if cur:
                        invert(g, u + 1)
                    routing(u)
                    if u == 12 and nxt:
                        x_lo(g + 1, 3)
                    if prev and u == 12:
                        choose(g - 1)
                    if prev and u == 4:
                        tile_stats(1, 2)
                        tile_stats(1, 3)
                        norm_stats(1)
                    if nxt and u == 8:
                        tile_stats(0, 3)
                    if do1:
                        attn_part(g1, q1, 0)
                    if do1:
                        attn_part(g1, q1, 1)
                    if cur:
                        probs_lo(g, u)
                    if do2:
                        invert(g2, u2)
                    if prev and u == 4:
                        normalise(1, g - 1, 0)
                        normalise(1, g - 1, 1)
                    if nxt and u == 8:
                        norm_stats(0)
                elif t == 1:
                    if u == 13:
                        routing(u)
                    if do3:
                        query_part(g3, q3, 0)
                    if do2:
                        row_max(g2, u2)
                    if cur:
                        probs_lo(g, u)
                    if do1:
                        add_projection(g1, q1, 0)
                    if do2:
                        invert(g2, u2)
                    if prev and u == 1:
                        tile_stats(1, 0)
                    if prev and u == 5:
                        normalise(1, g - 1, 2)
                    if nxt and u == 5:
                        tile_stats(0, 0)
                        tile_stats(0, 1)
                    if nxt and u == 9:
                        for s in range(TILES):
                            normalise(0, g + 1, s)
                    if prev and u == 13:
                        assign(g - 1)
                elif t == 2:
                    if do3:
                        query_part(g3, q3, 1)
                    if cur:
                        probs_lo(g, u)
                    if do1:
                        add_projection(g1, q1, 1)
                    if u == 10 and nxt:
                        x_lo(g + 1, 0)
                    if do2:
                        row_max(g2, u2)
                    if prev and u == 2:
                        tile_stats(1, 1)
                    if nxt and u == 6:
                        tile_stats(0, 2)
                    if prev and u == 14:
                        enter(g - 1)
                else:
                    if cur:
                        probs_lo(g, u)
                    if nxt or (cur and u < UNITS - 1):
                        invert(*before_last)
                    routing(u)
                    if do1:
                        add_projection(g1, q1, 2)
                    if do2:
                        row_max(g2, u2)
                    if u == 11 and nxt:
                        x_lo(g + 1, 1)
                    if cur:
                        last_part(g, q)
                    if do1:
                        add_projection(g1, q1, 3)
                    if prev and u == 7:
                        normalise(1, g - 1, 3)
                    if u == 11 and nxt:
                        x_lo(g + 1, 2)
                before_last = g2, u2

        def step(g, n, ins):
            ins.then_inc(route_step, 1)
            dve.wait_ge(route_step, ROUTE * g + n + 1)

        def each(t):
            return t[:, :].unsqueeze(2).to_broadcast([P, TILES, E])

        def choose(g):
            dve.wait_ge(logits_copied, 2 * (g + 1))
            step(g, 0, dve.tensor_reduce(top[:, :], logits[:, :, :], AX.X, ALU.max))
            dve.tensor_tensor(shifted[:, :, :], logits[:, :, :], each(top), ALU.subtract).then_inc(shifted_ready, 1)
            step(g, 1, dve.tensor_tensor(marked[:, :, :], logits[:, :, :], each(top), ALU.is_equal))
            step(g, 2, dve.tensor_tensor(marked[:, :, :], marked[:, :, :],
                                         weight8[:, :].unsqueeze(1).to_broadcast([P, TILES, E]), ALU.mult))
            step(g, 3, dve.tensor_reduce(first8[:, :], marked[:, :, :], AX.X, ALU.max))
            dve.tensor_tensor(chosen[:, :, :], marked[:, :, :], each(first8), ALU.is_equal).then_inc(chosen_ready, 1)

        def assign(g):
            dve.wait_ge(places_read, g + 1)
            step(g, 4, dve.tensor_reduce(place[:, :], placed[:, :, :], AX.X, ALU.add))
            step(g, 5, dve.tensor_reduce(chosen_sum[:, :], chosen[:, :, :].rearrange("p t e -> p e t"), AX.X, ALU.add))
            step(g, 6, dve.tensor_tensor(before[:, :], before[:, :], chosen_sum[:, :], ALU.add))
            step(g, 7, dve.tensor_scalar(over[:, :], place[:, :], float(CAP), float(2 * T), ALU.is_gt, ALU.mult))
            step(g, 8, dve.scalar_tensor_tensor(out=slot[:, :], in0=first8[:, :], scalar=-float(CAP), in1=place[:, :],
                                                 op0=ALU.mult, op1=ALU.add))
            if not (isinstance(g, int) and g == 0):
                dve.wait_ge(slots_stored, 16 * TILES * g)
            step(g, 9, dve.scalar_tensor_tensor(out=slot[:, :], in0=slot[:, :], scalar=float(T - 1), in1=over[:, :],
                                                 op0=ALU.add, op1=ALU.add))

        def enter(g):
            dve.wait_ge(exps_ready, g + 1)
            step(g, 10, dve.tensor_reduce(denom[:, :], exps[:, :, :], AX.X, ALU.add))
            step(g, 11, dve.reciprocal(gate[:, :], denom[:, :]))
            dve.tensor_copy(slot_index[:, :], slot[:, :]).then_inc(entry_ready, 1)
            dve.tensor_scalar(entry[:, :, 1].bitcast(F32), gate[:, :], tanh_g[:, 1:2], None, ALU.mult).then_inc(entry_ready, 1)
            step(g, 12, dve.tensor_copy(entry[:, :, 0], token[:, :]))
            step(g, 13, dve.tensor_scalar(token[:, :], token[:, :], float(GN), None, ALU.add))

        def STATS_OF(g):
            if isinstance(g, int) and g == 0:
                return 0
            return 4 * TILES * g - (4 * TILES if isinstance(g, int) and g == NG else 2 * TILES)

        dve.memset(probs[:, :], 0.0).then_inc(probs_zeroed, 1)
        dve.memset(before[:, :], 0.0).then_inc(probs_zeroed, 1)
        for i in range(2):
            query_part(0, 0, i)
        row_max(0, 0)
        row_max(0, 1)
        invert(0, 0)
        over_groups(dve, group)

    @block.gpsimd
    def _(pool):
        def normalise(g, u):
            pool.wait_ge(sums_inverted, UNITS * g + u + 1)
            if not (isinstance(g, int) and g == 0 and u < 1):
                pool.wait_ge(probsT_ready, UNITS * g + u)
            for cols, first, n, wide in ((slice(0, 4 * P), 0, P, P), (slice(4 * P, 4 * HP), P, M - P, HP - P)):
                ins = pool.tensor_tensor(probs[:, cols].rearrange("p (h n) -> p h n", n=wide)[:, :, 0:n],
                                         exp_scores[:, u % 2, :, first:first + n],
                                         inv_sums[:, u % 2, :].unsqueeze(2).to_broadcast([P, 4, n]), ALU.mult)
            ins.then_inc(probs_ready, 1)

        def root(which, g):
            pool.wait_ge((norm1_stats, norm2_stats)[which], g + which)
            pool.tensor_tensor(rstd[:, which, :], var_eps[:, which, :], half_neg[:, :], ALU.pow)\
                .then_inc((norm1_rstd, norm2_rstd)[which], 1)

        def add_bias(g, t):
            pool.wait_ge(partial_loaded[t], 16 * (g + 1))
            pool.tensor_tensor(partial[:, t, :], partial[:, t, :], bias[:, :], ALU.add).then_inc(partial_biased, 1)

        def group(g, prev, cur, nxt):
            for u in range(UNITS):
                u2, g2, do2 = (u + 1, g, cur) if u + 1 < UNITS else (0, g + 1, nxt)
                if nxt and u == 9:
                    root(0, g + 1)
                if do2:
                    normalise(g2, u2)
                if cur and u in (3, 5, 6):
                    for t in {3: (0,), 5: (1, 2), 6: (3,)}[u]:
                        add_bias(g, t)
                if prev and u == 4:
                    root(1, g - 1)
                if prev and u == 15:
                    pool.wait_ge(entry_ready, 2 * g)
                    pool.wait_ge(route_step, ROUTE * g)
                    alone(pool, pool_waits_met)
                    for t in range(TILES):
                        pool.indirect_dma_start(out=slots_dram[:, :], out_offset=bass.IndirectOffsetOnAxis(
                            ap=slot_index[:, t:t + 1], axis=0), in_=entry[:, t, :], in_offset=None,
                            bounds_check=T - 1, oob_is_err=False).then_inc(slots_stored, 16)

        for q in range(QUADS):
            pool.memset(keys[:, q, :, :].rearrange("p s n -> p (s n)").bitcast(F32), 0.0).then_inc(keys_zeroed, 1)
        pool.memset(values[:, :, :].rearrange("p q n -> p (q n)").bitcast(F32), 0.0).then_inc(values_zeroed, 1)
        pool.wait_ge(probs_zeroed, 2)
        normalise(0, 0)
        over_groups(pool, group)
        pool.wait_ge(slots_stored, 16 * TILES * NG)


def ffn_block(nc, stack, sb, env):
    psum, ident, half_neg = env["psum"], env["ident"], env["half_neg"]
    (KC, D, E, F, T, CAP) = [env[k] for k in ("KC", "D", "E", "F", "T", "CAP")]
    w1, w2, x1_dram, slots_dram, out_rows = [env[k] for k in ("w1", "w2", "x1_dram", "slots_dram", "out_rows")]
    FC = F // P
    PAIRS = FC // 2
    PW = 2 * P
    HALVES = CAP // GN
    SLOTS = CAP // P
    assert HALVES == 2

    wh1 = sb(stack, "wh1", [P, 2, KC, F], F32R)
    wh2 = sb(stack, "wh2", [P, 2, FC, D], F32R)
    raw1 = sb(stack, "w1_raw", [P, 2, KC, PW], F32)
    raw2 = sb(stack, "w2_raw", [P, 2, 2, D], F32)
    slots = sb(stack, "slots", [P, E, SLOTS, 2], U32)
    index = sb(stack, "index", [P, HALVES, TILES], U32)
    coef = sb(stack, "coef", [P, HALVES, TILES], U32)
    rows = sb(stack, "rows", [P, HALVES, TILES, D], F32)
    normed = sb(stack, "normed", [P, TILES, D], F32)
    sT = sb(stack, "sT", [P, 2, KC, GN], F32R)
    hidden = sb(stack, "hidden", [P, 2, GN], F32)
    hT = sb(stack, "hT", [P, 2, 2, GN], F32R)
    stats2 = sb(stack, "stats2", [P, TILES, 6], F32)
    mean_var2 = sb(stack, "mean_var2", [P, TILES, 2], F32)
    var_eps2 = sb(stack, "var_eps2", [P, TILES], F32)
    rstd2 = sb(stack, "rstd2", [P, TILES], F32)

    sem = lambda name: stack.enter_context(nc.semaphore(name))
    slots_loaded = sem("slots_loaded")
    raw_loaded = [sem("w_raw_loaded0"), sem("w_raw_loaded1")]
    w_hi, w_lo = sem("w_hi"), sem("w_lo")
    index_ready = sem("index_ready")
    gathered = [[sem(f"gathered{h}{t}") for t in range(TILES)] for h in range(2)]
    scattered = [sem("scattered0"), sem("scattered1")]
    slot_step = sem("slot_step")
    s_stats, s_rstd, s_normed = sem("s_stats"), sem("s_rstd"), sem("s_normed")
    sT_ready, sT_hi, sT_lo = sem("sT_ready"), sem("sT_hi"), sem("sT_lo")
    hid_ready, gelu_done, hT_hi, hT_lo, hT_used = sem("hid_ready"), sem("gelu_done"), sem("hT_hi"), sem("hT_lo"), sem("hT_used")
    y_ready, y_done = sem("y_ready"), sem("y_done")
    dve_waits_met, pool_waits_met = sem("dve_waits_met2"), sem("pool_waits_met2")

    def rows_bank(G, t):
        return 4 + t if isinstance(G, int) and G == 0 else 6 + t % 2

    def over_experts(engine, body):
        body(0, True, True)
        with engine.Fori(1, E - 1) as e:
            body(e, False, True)
        body(E - 1, False, False)

    def weight_pairs(first, nxt, half, f):
        if half == 0 and f % 2 == 0:
            if first and f // 2 + 2 < PAIRS:
                return [(0, f // 2 + 2)]
            if not first and f == 0:
                return [(0, PAIRS - 1)]
        if half == 1 and nxt and f % 2 == 0 and f >= 2:
            return [(1, f // 2 - 1)]
        return []

    block = stack.enter_context(nc.Block())

    @block.sync
    def _(sp):
        sp.dma_start(slots[:, :, :, :].rearrange("p e k c -> p e (k c)"),
                     slots_dram.rearrange("(e p k) c -> p e (k c)", e=E, p=P)).then_inc(slots_loaded, 16)
        w1_v = w1.rearrange("e (c p) f -> p e c f", p=P)
        w2_v = w2.rearrange("e (f p) d -> p e f d", p=P)

        def load_pair(e, j2, s):
            sp.dma_start(raw1[:, s, :, :], w1_v[:, bass.ds(e, 1), :, bass.ds(j2 * 2 * PW + s * PW, PW)].rearrange(
                "p e c f -> p (e c) f")).then_inc(raw_loaded[s], 16)
            sp.dma_start(raw2[:, s, :, :], w2_v[:, bass.ds(e, 1), bass.ds(j2 * 4 + s * 2, 2), :].rearrange(
                "p e f d -> p (e f) d")).then_inc(raw_loaded[s], 16)

        load_pair(0, 0, 0)
        load_pair(0, 0, 1)
        for j2 in range(1, PAIRS // 2):
            for s in range(2):
                sp.wait_ge(w_lo, 2 * j2 + s - 1)
                load_pair(0, j2, s)
        with sp.Fori(1, E) as e:
            with sp.Fori(0, PAIRS // 2) as j2:
                for s in range(2):
                    sp.wait_ge(w_lo, PAIRS * e + 2 * j2 + s - 1)
                    load_pair(e, j2, s)

    @block.tensor
    def _(pe):
        def transposes(G, t):
            pe.wait_ge(s_normed, TILES * G + t + 1)
            if not (isinstance(G, int) and G == 0):
                pe.wait_ge(sT_lo, TILES * G + t - 1)
            for c in range(KC):
                ins = pe.transpose(psum[:, rows_bank(G, t), P * c:P * (c + 1)], normed[:, t, P * c:P * (c + 1)], ident[:, :])
            ins.then_inc(sT_ready, 1)

        def up(e, half, f):
            if f == 0:
                pe.wait_ge(sT_lo, TILES * (2 * e + half + 1))
            if half == 0 and f % 2 == 0:
                pe.wait_ge(w_lo, PAIRS * e + f // 2 + 1)
            n = FC * (2 * e + half) + f
            if not (isinstance(n, int) and n < 2):
                pe.wait_ge(gelu_done, n - 1)
            for c in range(KC):
                ins = split_matmul(pe, psum[:, 4 + f % 2, :], lambda s: wh1[:, s, c, P * f:P * (f + 1)],
                                   lambda s: sT[:, s, c, :], c == 0, c == KC - 1)
            ins.then_inc(hid_ready, 1)

        def down(e, half, f, tiles):
            G = 2 * e + half
            for t in tiles:
                if f == 0 and not (isinstance(G, int) and G == 0):
                    pe.wait_ge(y_done, TILES * (G - 1) + t + 1)
                if t == 0:
                    pe.wait_ge(hT_lo, FC * G + f + 1)
                ins = split_matmul(pe, psum[:, t, :], lambda s: hT[:, f % 2, s, P * t:P * (t + 1)],
                                   lambda s: wh2[:, s, f, :], f == 0, f == FC - 1)
                if t == TILES - 1:
                    ins.then_inc(hT_used, 1)
                elif f == FC - 1:
                    ins.then_inc(y_ready, 1)

        def expert(e, first, nxt):
            for half in range(HALVES):
                more = half == 0 or nxt
                e2, half2 = (e, 1) if half == 0 else (e + 1, 0)
                for f in range(FC - 2):
                    if f > 0:
                        up(e, half, f + 1)
                    down(e, half, f, range(TILES))
                if more:
                    transposes(2 * e2 + half2, 0)
                    transposes(2 * e2 + half2, 1)
                up(e, half, FC - 1)
                down(e, half, FC - 2, range(TILES))
                if more:
                    transposes(2 * e2 + half2, 2)
                    down(e, half, FC - 1, (0,))
                    transposes(2 * e2 + half2, 3)
                    down(e, half, FC - 1, range(1, TILES))
                    up(e2, half2, 0)
                    up(e2, half2, 1)
                else:
                    down(e, half, FC - 1, range(TILES))

        for t in range(TILES):
            transposes(0, t)
        up(0, 0, 0)
        up(0, 0, 1)
        over_experts(pe, expert)

    @block.scalar
    def _(act):
        def rows_hi(G, t):
            act.wait_ge(sT_ready, TILES * G + t + 1)
            act.activation(sT[:, HI, :, P * t:P * (t + 1)], psum[:, rows_bank(G, t), :].rearrange("p (c n) -> p c n", c=KC),
                           ACT.Copy).then_inc(sT_hi, 1)

        def gelu(G, f):
            n = FC * G + f
            act.wait_ge(hid_ready, n + 1)
            if not (isinstance(n, int) and n < 2):
                act.wait_ge(hT_lo, n - 1)
                act.wait_ge(hT_used, n - 1)
            act.activation(hidden[:, f % 2, :], psum[:, 4 + f % 2, :], ACT.Gelu_apprx_tanh).then_inc(gelu_done, 1)
            act.wait_ge(gelu_done, n + 1)
            act.activation(hT[:, f % 2, HI, :], hidden[:, f % 2, :], ACT.Copy).then_inc(hT_hi, 1)

        def expert(e, first, nxt):
            for half in range(HALVES):
                more = half == 0 or nxt
                G = 2 * e + half
                for f in range(FC):
                    if f == FC - 2 and more:
                        act.wait_ge(hid_ready, FC * G + FC)
                        rows_hi(G + 1, 0)
                    if f + 1 < FC:
                        gelu(G, f + 1)
                    elif more:
                        gelu(G + 1, 0)
                    if f == FC - 2 and more:
                        for t in range(1, TILES):
                            rows_hi(G + 1, t)

        for t in range(TILES):
            rows_hi(0, t)
        gelu(0, 0)
        over_experts(act, expert)

    @block.vector
    def _(dve):
        def split_hi(e, j):
            dve.wait_ge(raw_loaded[j % 2], 32 * (PAIRS // 2 * e + j // 2 + 1))
            if not (isinstance(e, int) and e == 0):
                dve.wait_ge(hT_used, FC * (2 * e - 1) + 2 * j + 2)
            dve.tensor_copy(wh1[:, HI, :, PW * j:PW * (j + 1)], raw1[:, j % 2, :, :]).then_inc(w_hi, 1)
            dve.tensor_copy(wh2[:, HI, 2 * j:2 * j + 2, :], raw2[:, j % 2, :, :]).then_inc(w_hi, 1)

        def fetch(e, half):
            G = 2 * e + half
            if not (isinstance(G, int) and G < 2):
                dve.wait_ge(scattered[half], 16 * TILES * e)
            src = slots[:, bass.ds(e, 1), TILES * half:TILES * (half + 1), :].rearrange("p e k c -> p (e k) c")
            dve.tensor_copy(index[:, half, :], src[:, :, 0]).then_inc(index_ready, 1)
            dve.tensor_copy(coef[:, half, :], src[:, :, 1]).then_inc(index_ready, 1)

        def statistics(G, half, t):
            dve.wait_ge(gathered[half][t], 16 * (G // 2 + 1))
            alone(dve, dve_waits_met)
            dve.bn_stats(stats2[:, t, :], rows[:, half, t, :]).then_inc(slot_step, 1)
            if t == TILES - 1:
                dve.wait_ge(slot_step, 2 * TILES * G + TILES)
                alone(dve, dve_waits_met)
                for a in range(TILES):
                    dve.bn_aggr(mean_var2[:, a, :], stats2[:, a, :]).then_inc(slot_step, 1)
                dve.wait_ge(slot_step, 2 * TILES * (G + 1))
                dve.tensor_scalar(var_eps2[:, :], mean_var2[:, :, 1], EPS, None, ALU.add).then_inc(s_stats, 1)

        def normalise(G, half, t):
            dve.wait_ge(s_rstd, G + 1)
            if not (isinstance(G, int) and G == 0):
                dve.wait_ge(sT_ready, TILES * G)
            dve.tensor_scalar(normed[:, t, :], rows[:, half, t, :], mean_var2[:, t, 0:1], rstd2[:, t:t + 1],
                              ALU.subtract, ALU.mult).then_inc(s_normed, 1)

        def rows_lo(G, t):
            dve.wait_ge(sT_hi, TILES * G + t + 1)
            dve.tensor_tensor(sT[:, LO, :, P * t:P * (t + 1)], psum[:, rows_bank(G, t), :].rearrange("p (c n) -> p c n", c=KC),
                              sT[:, HI, :, P * t:P * (t + 1)].bitcast(F32), ALU.subtract).then_inc(sT_lo, 1)

        def hidden_lo(G, f):
            dve.wait_ge(hT_hi, FC * G + f + 1)
            dve.tensor_tensor(hT[:, f % 2, LO, :], hidden[:, f % 2, :], hT[:, f % 2, HI, :].bitcast(F32),
                              ALU.subtract).then_inc(hT_lo, 1)

        def outputs(G, half):
            for t in range(TILES):
                if t < TILES - 1:
                    dve.wait_ge(y_ready, (TILES - 1) * G + t + 1)
                else:
                    dve.wait_ge(hT_used, FC * (G + 1))
                dve.scalar_tensor_tensor(out=rows[:, half, t, :], in0=psum[:, t, :],
                                         scalar=coef[:, half, t:t + 1].bitcast(F32), in1=rows[:, half, t, :],
                                         op0=ALU.mult, op1=ALU.add).then_inc(y_done, 1)

        def expert(e, first, nxt):
            for half in range(HALVES):
                more = half == 0 or nxt
                G = 2 * e + half
                e2, half2 = (e, 1) if half == 0 else (e + 1, 0)
                for f in range(FC):
                    if f == FC - 2 and more:
                        rows_lo(G + 1, 0)
                    if f + 1 < FC:
                        hidden_lo(G, f + 1)
                    else:
                        outputs(G, half)
                        if more:
                            hidden_lo(G + 1, 0)
                    if f == 4 and more:
                        fetch(e2, half2)
                    if 7 <= f < 7 + TILES and more:
                        statistics(G + 1, half2, f - 7)
                    if f in (11, 12) and more:
                        normalise(G + 1, half2, 2 * (f - 11))
                        normalise(G + 1, half2, 2 * (f - 11) + 1)
                    if f == FC - 2 and more:
                        for t in range(1, TILES):
                            rows_lo(G + 1, t)
                    for ahead, j in weight_pairs(first, nxt, half, f):
                        split_hi(e + ahead, j)

        dve.wait_ge(slots_loaded, 16)
        fetch(0, 0)
        split_hi(0, 0)
        for t in range(TILES):
            statistics(0, 0, t)
        for t in range(TILES):
            normalise(0, 0, t)
        for t in range(TILES):
            rows_lo(0, t)
        split_hi(0, 1)
        hidden_lo(0, 0)
        over_experts(dve, expert)

    @block.gpsimd
    def _(pool):
        def split_lo(e, j):
            pool.wait_ge(w_hi, 2 * (PAIRS * e + j + 1))
            pool.tensor_tensor(wh1[:, LO, :, PW * j:PW * (j + 1)], raw1[:, j % 2, :, :],
                               wh1[:, HI, :, PW * j:PW * (j + 1)].bitcast(F32), ALU.subtract)
            pool.tensor_tensor(wh2[:, LO, 2 * j:2 * j + 2, :], raw2[:, j % 2, :, :],
                               wh2[:, HI, 2 * j:2 * j + 2, :].bitcast(F32), ALU.subtract).then_inc(w_lo, 1)

        def gather(G, half):
            pool.wait_ge(index_ready, 2 * (G + 1))
            alone(pool, pool_waits_met)
            for t in range(TILES):
                pool.indirect_dma_start(out=rows[:, half, t, :], out_offset=None, in_=x1_dram[:, :],
                                        in_offset=bass.IndirectOffsetOnAxis(ap=index[:, half, t:t + 1], axis=0),
                                        bounds_check=T, oob_is_err=False).then_inc(gathered[half][t], 16)

        def scatter(G, half):
            for t in range(TILES):
                pool.wait_ge(y_done, TILES * G + t + 1)
                alone(pool, pool_waits_met)
                pool.indirect_dma_start(out=out_rows[:, :], in_=rows[:, half, t, :], in_offset=None,
                                        out_offset=bass.IndirectOffsetOnAxis(ap=index[:, half, t:t + 1], axis=0),
                                        bounds_check=T - 1, oob_is_err=False).then_inc(scattered[half], 16)

        def root(G):
            pool.wait_ge(s_stats, G + 1)
            pool.tensor_tensor(rstd2[:, :], var_eps2[:, :], half_neg[:, :], ALU.pow).then_inc(s_rstd, 1)

        def expert(e, first, nxt):
            for half in range(HALVES):
                more = half == 0 or nxt
                G = 2 * e + half
                for f in range(FC):
                    if f == 1 and half == 1:
                        scatter(G - 1, 0)
                    if f == 1 and half == 0 and not first:
                        scatter(G - 1, 1)
                    if f == 4 and more:
                        gather(G + 1, 1 - half)
                    if f == 10 and more:
                        root(G + 1)
                    for ahead, j in weight_pairs(first, nxt, half, f):
                        split_lo(e + ahead, j)

        gather(0, 0)
        split_lo(0, 0)
        root(0)
        split_lo(0, 1)
        over_experts(pool, expert)
        scatter(2 * E - 1, 1)
        for s in scattered:
            pool.wait_ge(s, 16 * TILES * E)


_INS = ["x", "ctx_768", "g_xattn", "g_ffn", "L0_xattn_Wq", "L0_xattn_Wk", "L0_xattn_Wv", "L0_xattn_Wo",
        "L0_xattn_bo", "L0_ffn_router_w", "L0_ffn_w1", "L0_ffn_w2"]


def kernel(**inputs):
    import numpy as _np
    import concourse.bacc as _bacc
    from concourse import mybir as _mybir
    from concourse.bass_utils import run_bass_kernel_spmd as _run

    nc = _bacc.Bacc("TRN2", target_bir_lowering=False, num_devices=1)
    arrays, args = {}, []
    for name in _INS:
        a = _np.ascontiguousarray(inputs[name])
        arrays[f"in_{name}_dram"] = a
        args.append(nc.dram_tensor(f"in_{name}_dram", a.shape, _mybir.dt.from_np(a.dtype), kind="ExternalInput").ap())
    args.append(nc.dram_tensor("out_0_dram", inputs["x"].shape, F32, kind="ExternalOutput").ap())
    flamingo_block(nc, *args)
    r = _run(nc, [arrays], core_ids=[0])
    return r.results[0]["out_0_dram"]
```
